# Optimizing a Trainium2 kernel written in Bass

```python
import numpy as np
import jax
import jax.numpy as jnp

def _softmax(x, axis=-1):
    return jax.nn.softmax(x, axis=axis)

def _gelu(x):
    return jax.nn.gelu(x, approximate=True)

def _silu(x):
    return jax.nn.silu(x)

def _sigmoid(x):
    return jax.nn.sigmoid(x)

def _layernorm(x, axis=-1, eps=1e-05):
    m = jnp.mean(x, axis=axis, keepdims=True)
    v = jnp.var(x, axis=axis, keepdims=True)
    return (x - m) / jnp.sqrt(v + eps)

def _scatter_add(tgt, idx, src, axis=0):
    return tgt.at[idx].add(src)

def _segment_sum(src, seg, n):
    return jax.ops.segment_sum(src, seg, n)
kernel_name = 'mk_flamingo_gated_d2_seqx_r8_eca0f9'

def setup_inputs(seed: int=0):
    np.random.seed(seed)
    _w = jnp.asarray

    def _rec_inputs():
        import jax
        import jax.numpy as jnp
        _rk = jax.random.key(seed)
        x = 7.22e-05 + 1 * jax.random.normal(jax.random.fold_in(_rk, 1), (2, 512, 128), jnp.float32)
        _lenS = 512 - jax.random.randint(jax.random.fold_in(_rk, 7), (2,), 0, max(1, 512 // 4) + 1, jnp.int32)
        _lenS2 = 77 - jax.random.randint(jax.random.fold_in(_rk, 8), (2,), 0, max(1, 77 // 4) + 1, jnp.int32)
        _ctx_1024P = jax.random.normal(jax.random.fold_in(_rk, 11), (2, 16, 128), jnp.float32)
        _ctx_1024c = jax.random.dirichlet(jax.random.fold_in(_rk, 511), 0.3 * jnp.ones((16,), jnp.float32), (2, 77))
        _ctx_1024t = jnp.einsum('bsk,bkd->bsd', _ctx_1024c, _ctx_1024P)
        _ctx_1024t = _ctx_1024t * jax.lax.rsqrt(jnp.mean(jnp.square(_ctx_1024t)) + 1e-12) * 0.953939
        ctx_1024 = 4.13588e-05 + 0.999923 * (_ctx_1024t + 0.3 * jax.random.normal(jax.random.fold_in(_rk, 611), (2, 77, 128), jnp.float32))
        _validS = jnp.arange(512)[None, :] < _lenS[:, None]
        _validS2 = jnp.arange(77)[None, :] < _lenS2[:, None]
        _causal = jnp.tril(jnp.ones((512, 512), dtype=bool))
        mask_Bx8xSxS2_bf0 = jnp.logical_not(jnp.ones((2, 8, 512, 77), dtype=bool))
        _g = jax.random.normal(jax.random.fold_in(_rk, 9001), (2, 2), jnp.float32)
        _g = jnp.sign(_g) * jnp.maximum(jnp.abs(_g), 1.0) + (_g == 0) * 1.0
        g_xattn = _g[0]
        g_ffn = _g[1]
        return (x, ctx_1024, mask_Bx8xSxS2_bf0, g_xattn, g_ffn)
    x, ctx_1024, mask_Bx8xSxS2_bf0, g_xattn, g_ffn = _rec_inputs()

    def _L0_xattn_setup():
        import jax, jax.numpy as jnp
        import numpy as np
        B, L, E = (4, 256, 128)
        H, DQ, DV = (8, 128, 128)
        SCALE = 1.0 / np.sqrt(DQ).astype(np.float32)
        key = jax.random.key(seed)
        ks = jax.random.split(key, 6)
        return {'qInputs': jax.random.normal(ks[0], (B, L, E), dtype=jnp.float32), 'kvInputs': jax.random.normal(ks[1], (B, L, E), dtype=jnp.float32), 'mask': jnp.zeros((B, H, L, L), dtype=jnp.bool_), 'W_Q': jax.random.normal(ks[2], (E, H * DQ), dtype=jnp.float32) * 0.02, 'W_K': jax.random.normal(ks[3], (E, H * DQ), dtype=jnp.float32) * 0.02, 'W_V': jax.random.normal(ks[4], (E, H * DV), dtype=jnp.float32) * 0.02, 'W_fc': jax.random.normal(ks[5], (H * DV, E), dtype=jnp.float32) * 0.02}
    _L0_xattn_all = _L0_xattn_setup()
    _L0_xattn_in = {k: v for k, v in _L0_xattn_all.items() if k in ('W_Q', 'W_K', 'W_V', 'W_fc')}
    del _L0_xattn_all

    def _L0_ffn_setup():
        import jax, jax.numpy as jnp
        import numpy as np
        D_MODEL = 128
        H_SHARED = 256
        H_ROUTED = 128
        N_EXPERTS = 8
        TOP_K = 2
        key = jax.random.key(seed)
        ks = jax.random.split(key, 8)
        B, T = (2, 256)
        sc_d = 1.0 / np.sqrt(D_MODEL)
        sc_hs = 1.0 / np.sqrt(H_SHARED)
        sc_hr = 1.0 / np.sqrt(H_ROUTED)
        return {'x': jax.random.normal(ks[0], (B, T, D_MODEL), dtype=jnp.float32), 'router_w': jax.random.normal(ks[1], (N_EXPERTS, D_MODEL), dtype=jnp.float32) * sc_d, 'router_bias': jnp.zeros((N_EXPERTS,), dtype=jnp.float32), 'sw1': jax.random.normal(ks[2], (D_MODEL, H_SHARED), dtype=jnp.float32) * sc_d, 'sw3': jax.random.normal(ks[3], (D_MODEL, H_SHARED), dtype=jnp.float32) * sc_d, 'sw2': jax.random.normal(ks[4], (H_SHARED, D_MODEL), dtype=jnp.float32) * sc_hs, 'ew1': jax.random.normal(ks[5], (N_EXPERTS, D_MODEL, H_ROUTED), dtype=jnp.float32) * sc_d, 'ew2': jax.random.normal(ks[6], (N_EXPERTS, H_ROUTED, D_MODEL), dtype=jnp.float32) * sc_hr}
    _L0_ffn_all = _L0_ffn_setup()
    _L0_ffn_in = {k: v for k, v in _L0_ffn_all.items() if k in ('router_w', 'router_bias', 'sw1', 'sw3', 'sw2', 'ew1', 'ew2')}
    del _L0_ffn_all

    def _L1_xattn_setup():
        import jax, jax.numpy as jnp
        import numpy as np
        N_EMBD = 128
        N_HEAD = 16
        DIM_HEAD = N_EMBD // N_HEAD
        SCALE = DIM_HEAD ** (-0.5)
        key = jax.random.key(seed)
        k1, k2, k3, k4, k5 = jax.random.split(key, 5)
        B, Tq, Tkv = (2, 256, 256)
        x_q = jax.random.normal(k1, (B, Tq, N_EMBD), dtype=jnp.float32)
        x_kv = jax.random.normal(k2, (B, Tkv, N_EMBD), dtype=jnp.float32)
        s = 0.02
        W_q = jax.random.normal(k3, (N_EMBD, N_EMBD), dtype=jnp.float32) * s
        W_kv = jax.random.normal(k4, (N_EMBD, 2 * N_EMBD), dtype=jnp.float32) * s
        W_proj = jax.random.normal(k5, (N_EMBD, N_EMBD), dtype=jnp.float32) * s
        return {'x_q': x_q, 'x_kv': x_kv, 'W_q': W_q, 'W_kv': W_kv, 'W_proj': W_proj}
    _L1_xattn_all = _L1_xattn_setup()
    _L1_xattn_in = {k: v for k, v in _L1_xattn_all.items() if k in ('W_q', 'W_kv', 'W_proj')}
    del _L1_xattn_all

    def _L1_ffn_setup():
        import jax, jax.numpy as jnp
        import numpy as np
        DIM = 128
        DEPTH = 6
        HEADS = 16
        DIM_HEAD = 64
        WINDOW = 32
        INNER = HEADS * DIM_HEAD
        DIM_INNER = int(DIM * 4 * 2 / 3)
        QK_SCALE = 8.0

        def shift_tokens(t):
            a, s = jnp.split(t, 2, -1)
            s = jnp.pad(s, ((0, 0), (1, 0), (0, 0)))[:, :-1]
            return jnp.concatenate([a, s], -1)

        def l2norm(t):
            return t / jnp.maximum(jnp.linalg.norm(t, axis=-1, keepdims=True), 1e-12)

        def rotate_half(x):
            x1, x2 = jnp.split(x, 2, -1)
            return jnp.concatenate([-x2, x1], -1)

        def rotary_tables(n):
            half = jnp.arange(0, DIM_HEAD, 2, dtype=jnp.float32)
            inv_freq = 1.0 / 10000.0 ** (half / DIM_HEAD)
            t = jnp.arange(n, dtype=jnp.float32)
            freqs = t[:, None] * inv_freq[None, :]
            freqs = jnp.concatenate([freqs, freqs], -1)
            base_scale = (half + 0.4 * DIM_HEAD) / (1.4 * DIM_HEAD)
            power = (t - n // 2) / (WINDOW // 2)
            scale = base_scale[None, :] ** power[:, None]
            scale = jnp.concatenate([scale, scale], -1)
            return (freqs, scale)

        def local_attention(q, k, v):
            b, h, n, d = q.shape
            w = WINDOW
            nw = n // w
            bq = q.reshape(b, h, nw, w, d)
            bk = k.reshape(b, h, nw, w, d)
            bv = v.reshape(b, h, nw, w, d)

            def look(t):
                p = jnp.pad(t, ((0, 0), (0, 0), (1, 0), (0, 0), (0, 0)))
                return jnp.concatenate([p[:, :, :nw], p[:, :, 1:]], axis=3)
            bk2, bv2 = (look(bk), look(bv))
            seq = jnp.arange(n).reshape(nw, w)
            seq_p = jnp.pad(seq, ((1, 0), (0, 0)), constant_values=-1)
            jt = jnp.concatenate([seq_p[:nw], seq_p[1:]], axis=1)
            it = seq[:, :, None]
            jb = jt[:, None, :]
            mask = (it < jb) | (it > jb + w) | (jb == -1)
            sim = jnp.einsum('bhwie,bhwje->bhwij', bq, bk2) * QK_SCALE
            sim = jnp.where(mask, -jnp.finfo(sim.dtype).max, sim)
            attn = jax.nn.softmax(sim, -1)
            out = jnp.einsum('bhwij,bhwje->bhwie', attn, bv2)
            return out.reshape(b, h, n, d)

        def attn_layer(x, Wqkv, qs, ksc, Wo):
            b, n, _ = x.shape
            qkv = x @ Wqkv
            q, k, v = jnp.split(qkv, 3, -1)
            sh = lambda t: t.reshape(b, n, HEADS, DIM_HEAD).transpose(0, 2, 1, 3)
            q, k, v = (sh(q), sh(k), sh(v))
            q = l2norm(q) * qs
            k = l2norm(k) * ksc
            freqs, scale = rotary_tables(n)
            cos, sin = (jnp.cos(freqs), jnp.sin(freqs))
            q = q * cos * scale + rotate_half(q) * sin * scale
            inv = 1.0 / scale
            k = k * cos * inv + rotate_half(k) * sin * inv
            out = local_attention(q, k, v)
            out = out.transpose(0, 2, 1, 3).reshape(b, n, INNER)
            return out @ Wo

        def ffn_layer(x, g, bln, W1, b1, W2, b2):
            mu = x.mean(-1, keepdims=True)
            var = ((x - mu) ** 2).mean(-1, keepdims=True)
            xn = (x - mu) / jnp.sqrt(var + 1e-05) * g + bln
            hg = xn @ W1 + b1
            a, gate = jnp.split(hg, 2, -1)
            return a * jax.nn.gelu(gate, approximate=False) @ W2 + b2
        key = jax.random.key(seed)
        ks = jax.random.split(key, 8)
        B, N = (2, 256)
        init = lambda k, shape: jax.random.normal(k, shape, jnp.float32) * 0.02
        return {'x': jax.random.normal(ks[0], (B, N, DIM), jnp.float32), 'Wqkv': init(ks[1], (DEPTH, DIM, 3 * INNER)), 'q_scale': jnp.ones((DEPTH, DIM_HEAD), jnp.float32), 'k_scale': jnp.ones((DEPTH, DIM_HEAD), jnp.float32), 'Wo': init(ks[2], (DEPTH, INNER, DIM)), 'ln_g': jnp.ones((DEPTH, DIM), jnp.float32), 'ln_b': jnp.zeros((DEPTH, DIM), jnp.float32), 'W1': init(ks[3], (DEPTH, DIM, 2 * DIM_INNER)), 'b1': jnp.zeros((DEPTH, 2 * DIM_INNER), jnp.float32), 'W2': init(ks[4], (DEPTH, DIM_INNER, DIM)), 'b2': jnp.zeros((DEPTH, DIM), jnp.float32)}
    _L1_ffn_all = _L1_ffn_setup()
    _L1_ffn_in = {k: v for k, v in _L1_ffn_all.items() if k in ('Wqkv', 'q_scale', 'k_scale', 'Wo', 'ln_g', 'ln_b', 'W1', 'b1', 'W2', 'b2')}
    del _L1_ffn_all
    return {'x': x, 'ctx_1024': ctx_1024, 'mask_Bx8xSxS2_bf0': mask_Bx8xSxS2_bf0, 'g_xattn': g_xattn, 'g_ffn': g_ffn, 'L0_xattn_W_Q': _L0_xattn_in['W_Q'], 'L0_xattn_W_K': _L0_xattn_in['W_K'], 'L0_xattn_W_V': _L0_xattn_in['W_V'], 'L0_xattn_W_fc': _L0_xattn_in['W_fc'], 'L0_ffn_router_w': _L0_ffn_in['router_w'], 'L0_ffn_router_bias': _L0_ffn_in['router_bias'], 'L0_ffn_sw1': _L0_ffn_in['sw1'], 'L0_ffn_sw3': _L0_ffn_in['sw3'], 'L0_ffn_sw2': _L0_ffn_in['sw2'], 'L0_ffn_ew1': _L0_ffn_in['ew1'], 'L0_ffn_ew2': _L0_ffn_in['ew2'], 'L1_xattn_W_q': _L1_xattn_in['W_q'], 'L1_xattn_W_kv': _L1_xattn_in['W_kv'], 'L1_xattn_W_proj': _L1_xattn_in['W_proj'], 'L1_ffn_Wqkv': _L1_ffn_in['Wqkv'], 'L1_ffn_q_scale': _L1_ffn_in['q_scale'], 'L1_ffn_k_scale': _L1_ffn_in['k_scale'], 'L1_ffn_Wo': _L1_ffn_in['Wo'], 'L1_ffn_ln_g': _L1_ffn_in['ln_g'], 'L1_ffn_ln_b': _L1_ffn_in['ln_b'], 'L1_ffn_W1': _L1_ffn_in['W1'], 'L1_ffn_b1': _L1_ffn_in['b1'], 'L1_ffn_W2': _L1_ffn_in['W2'], 'L1_ffn_b2': _L1_ffn_in['b2']}

def reference(x, ctx_1024, mask_Bx8xSxS2_bf0, g_xattn, g_ffn, L0_xattn_W_Q, L0_xattn_W_K, L0_xattn_W_V, L0_xattn_W_fc, L0_ffn_router_w, L0_ffn_router_bias, L0_ffn_sw1, L0_ffn_sw3, L0_ffn_sw2, L0_ffn_ew1, L0_ffn_ew2, L1_xattn_W_q, L1_xattn_W_kv, L1_xattn_W_proj, L1_ffn_Wqkv, L1_ffn_q_scale, L1_ffn_k_scale, L1_ffn_Wo, L1_ffn_ln_g, L1_ffn_ln_b, L1_ffn_W1, L1_ffn_b1, L1_ffn_W2, L1_ffn_b2):
    import jax
    import jax.numpy as jnp

    def _L0_xattn_ref(qInputs, kvInputs, mask, W_Q, W_K, W_V, W_fc):
        import jax, jax.numpy as jnp
        import numpy as np
        B, L, E = (4, 256, 128)
        H, DQ, DV = (8, 128, 128)
        SCALE = 1.0 / np.sqrt(DQ).astype(np.float32)
        b, lq, _ = qInputs.shape
        lk = kvInputs.shape[1]
        Q = (qInputs @ W_Q).reshape(b, lq, H, DQ).transpose(0, 2, 1, 3)
        K = (kvInputs @ W_K).reshape(b, lk, H, DQ).transpose(0, 2, 1, 3)
        V = (kvInputs @ W_V).reshape(b, lk, H, DV).transpose(0, 2, 1, 3)
        scores = jnp.einsum('bhqd,bhkd->bhqk', Q, K) * SCALE
        scores = jnp.where(mask, jnp.float32(-1000000000.0), scores)
        attn = jax.nn.softmax(scores, axis=-1)
        ctx = jnp.einsum('bhqk,bhkd->bhqd', attn, V)
        ctx = ctx.transpose(0, 2, 1, 3).reshape(b, lq, H * DV)
        return ctx @ W_fc

    def _L0_ffn_ref(x, router_w, router_bias, sw1, sw3, sw2, ew1, ew2):
        import jax, jax.numpy as jnp
        import numpy as np
        D_MODEL = 128
        H_SHARED = 256
        H_ROUTED = 128
        N_EXPERTS = 8
        TOP_K = 2
        B, T, C = x.shape
        xf = x.reshape(-1, C)
        shared_out = jax.nn.silu(xf @ sw1) * (xf @ sw3) @ sw2
        s = jax.nn.sigmoid((xf @ router_w.T).astype(jnp.float32))
        sel_scores = s + router_bias.astype(jnp.float32)
        _, topk_idx = jax.lax.top_k(sel_scores, TOP_K)
        s_sel = jnp.take_along_axis(s, topk_idx, axis=1)
        denom = s_sel.sum(axis=1, keepdims=True)
        gates = jnp.where(denom > 1e-09, s_sel / (denom + 1e-09), 1.0 / TOP_K).astype(x.dtype)
        one_hot = jax.nn.one_hot(topk_idx, N_EXPERTS, dtype=x.dtype)
        comb = jnp.einsum('nke,nk->ne', one_hot, gates)
        h = jax.nn.gelu(jnp.einsum('nd,edh->neh', xf, ew1), approximate=False)
        y = jnp.einsum('neh,ehd->ned', h, ew2)
        routed_out = jnp.einsum('ned,ne->nd', y, comb)
        return (shared_out + routed_out).reshape(B, T, C)

    def _L1_xattn_ref(x_q, x_kv, W_q, W_kv, W_proj):
        import jax, jax.numpy as jnp
        import numpy as np
        N_EMBD = 128
        N_HEAD = 16
        DIM_HEAD = N_EMBD // N_HEAD
        SCALE = DIM_HEAD ** (-0.5)
        B, Tq, C = x_q.shape
        Tkv = x_kv.shape[1]
        q = x_q @ W_q
        kv = x_kv @ W_kv
        k, v = jnp.split(kv, 2, axis=2)
        q = q.reshape(B, Tq, N_HEAD, DIM_HEAD).transpose(0, 2, 1, 3)
        k = k.reshape(B, Tkv, N_HEAD, DIM_HEAD).transpose(0, 2, 1, 3)
        v = v.reshape(B, Tkv, N_HEAD, DIM_HEAD).transpose(0, 2, 1, 3)
        attn = jnp.einsum('bhqd,bhkd->bhqk', q, k) / SCALE
        attn = jax.nn.softmax(attn, axis=-1)
        y = jnp.einsum('bhqk,bhkd->bhqd', attn, v)
        y = y.transpose(0, 2, 1, 3).reshape(B, Tq, C)
        return y @ W_proj

    def _L1_ffn_ref(x, Wqkv, q_scale, k_scale, Wo, ln_g, ln_b, W1, b1, W2, b2):
        import jax, jax.numpy as jnp
        import numpy as np
        DIM = 128
        DEPTH = 6
        HEADS = 16
        DIM_HEAD = 64
        WINDOW = 32
        INNER = HEADS * DIM_HEAD
        DIM_INNER = int(DIM * 4 * 2 / 3)
        QK_SCALE = 8.0

        def shift_tokens(t):
            a, s = jnp.split(t, 2, -1)
            s = jnp.pad(s, ((0, 0), (1, 0), (0, 0)))[:, :-1]
            return jnp.concatenate([a, s], -1)

        def l2norm(t):
            return t / jnp.maximum(jnp.linalg.norm(t, axis=-1, keepdims=True), 1e-12)

        def rotate_half(x):
            x1, x2 = jnp.split(x, 2, -1)
            return jnp.concatenate([-x2, x1], -1)

        def rotary_tables(n):
            half = jnp.arange(0, DIM_HEAD, 2, dtype=jnp.float32)
            inv_freq = 1.0 / 10000.0 ** (half / DIM_HEAD)
            t = jnp.arange(n, dtype=jnp.float32)
            freqs = t[:, None] * inv_freq[None, :]
            freqs = jnp.concatenate([freqs, freqs], -1)
            base_scale = (half + 0.4 * DIM_HEAD) / (1.4 * DIM_HEAD)
            power = (t - n // 2) / (WINDOW // 2)
            scale = base_scale[None, :] ** power[:, None]
            scale = jnp.concatenate([scale, scale], -1)
            return (freqs, scale)

        def local_attention(q, k, v):
            b, h, n, d = q.shape
            w = WINDOW
            nw = n // w
            bq = q.reshape(b, h, nw, w, d)
            bk = k.reshape(b, h, nw, w, d)
            bv = v.reshape(b, h, nw, w, d)

            def look(t):
                p = jnp.pad(t, ((0, 0), (0, 0), (1, 0), (0, 0), (0, 0)))
                return jnp.concatenate([p[:, :, :nw], p[:, :, 1:]], axis=3)
            bk2, bv2 = (look(bk), look(bv))
            seq = jnp.arange(n).reshape(nw, w)
            seq_p = jnp.pad(seq, ((1, 0), (0, 0)), constant_values=-1)
            jt = jnp.concatenate([seq_p[:nw], seq_p[1:]], axis=1)
            it = seq[:, :, None]
            jb = jt[:, None, :]
            mask = (it < jb) | (it > jb + w) | (jb == -1)
            sim = jnp.einsum('bhwie,bhwje->bhwij', bq, bk2) * QK_SCALE
            sim = jnp.where(mask, -jnp.finfo(sim.dtype).max, sim)
            attn = jax.nn.softmax(sim, -1)
            out = jnp.einsum('bhwij,bhwje->bhwie', attn, bv2)
            return out.reshape(b, h, n, d)

        def attn_layer(x, Wqkv, qs, ksc, Wo):
            b, n, _ = x.shape
            qkv = x @ Wqkv
            q, k, v = jnp.split(qkv, 3, -1)
            sh = lambda t: t.reshape(b, n, HEADS, DIM_HEAD).transpose(0, 2, 1, 3)
            q, k, v = (sh(q), sh(k), sh(v))
            q = l2norm(q) * qs
            k = l2norm(k) * ksc
            freqs, scale = rotary_tables(n)
            cos, sin = (jnp.cos(freqs), jnp.sin(freqs))
            q = q * cos * scale + rotate_half(q) * sin * scale
            inv = 1.0 / scale
            k = k * cos * inv + rotate_half(k) * sin * inv
            out = local_attention(q, k, v)
            out = out.transpose(0, 2, 1, 3).reshape(b, n, INNER)
            return out @ Wo

        def ffn_layer(x, g, bln, W1, b1, W2, b2):
            mu = x.mean(-1, keepdims=True)
            var = ((x - mu) ** 2).mean(-1, keepdims=True)
            xn = (x - mu) / jnp.sqrt(var + 1e-05) * g + bln
            hg = xn @ W1 + b1
            a, gate = jnp.split(hg, 2, -1)
            return a * jax.nn.gelu(gate, approximate=False) @ W2 + b2
        for i in range(DEPTH):
            x = attn_layer(shift_tokens(x), Wqkv[i], q_scale[i], k_scale[i], Wo[i]) + x
            x = ffn_layer(shift_tokens(x), ln_g[i], ln_b[i], W1[i], b1[i], W2[i], b2[i]) + x
        return x
    x = x + jnp.tanh(g_xattn[0]) * _L0_xattn_ref(_layernorm(x, axis=-1), ctx_1024, mask_Bx8xSxS2_bf0, L0_xattn_W_Q, L0_xattn_W_K, L0_xattn_W_V, L0_xattn_W_fc)
    x = x + jnp.tanh(g_ffn[0]) * _L0_ffn_ref(_layernorm(x, axis=-1), L0_ffn_router_w, L0_ffn_router_bias, L0_ffn_sw1, L0_ffn_sw3, L0_ffn_sw2, L0_ffn_ew1, L0_ffn_ew2)
    x = x + jnp.tanh(g_xattn[1]) * _L1_xattn_ref(_layernorm(x, axis=-1), ctx_1024, L1_xattn_W_q, L1_xattn_W_kv, L1_xattn_W_proj)
    x = x + jnp.tanh(g_ffn[1]) * _L1_ffn_ref(_layernorm(x, axis=-1), L1_ffn_Wqkv, L1_ffn_q_scale, L1_ffn_k_scale, L1_ffn_Wo, L1_ffn_ln_g, L1_ffn_ln_b, L1_ffn_W1, L1_ffn_b1, L1_ffn_W2, L1_ffn_b2)
    return x

_drawn_inputs = setup_inputs


def setup_inputs(seed=0):
    import zlib

    import numpy as np

    out = dict(_drawn_inputs(seed))
    spreads = {'g_ffn': (-1.0, 0.2),
     'L0_ffn_router_bias': (0.0, 0.1),
     'L1_ffn_q_scale': (1.0, 0.56),
     'L1_ffn_k_scale': (1.0, 0.571),
     'L1_ffn_ln_g': (1.0, 0.6),
     'L1_ffn_ln_b': (0.0, 0.8),
     'L1_ffn_b1': (0.0, 0.1),
     'L1_ffn_b2': (0.0, 0.1)}
    factors = {'L0_xattn_W_Q': 7.2, 'L0_xattn_W_K': 6.294, 'L1_xattn_W_q': 8.0}
    for name, (base, spread) in spreads.items():
        noise = np.random.default_rng([zlib.crc32(name.encode()), seed]).standard_normal(out[name].shape)
        drawn = base * np.exp(spread * noise) if base else spread * noise
        out[name] = jnp.asarray(drawn.astype(out[name].dtype))
    for name, factor in factors.items():
        out[name] = (out[name] * factor).astype(out[name].dtype)
    return out
```

```python
from contextlib import ExitStack, contextmanager

import concourse.bass as bass
import numpy as np
from concourse import mybir

F32 = mybir.dt.float32
BF16 = mybir.dt.bfloat16
I32 = mybir.dt.int32
ALU = mybir.AluOpType
ACT = mybir.ActivationFunctionType
AX = mybir.AxisListType.X

P = 128
D = 128
B, S = 2, 512
CTX = 77
TILES = B * S // P
TB = S // P

LAYERS, HEADS, HD, WIN = 6, 16, 64, 32
PAIRS = HEADS // 2
INNER = HEADS * HD
FF = 341
FC = 3
ROWS = [128, 128, FF - 256]
N = LAYERS * TILES
KEYS = 96
GROUPS = 4
G = 4 * KEYS


class Memory:

    def __init__(self, nc, ctx):
        self.nc, self.ctx, self.buffers = nc, ctx, ctx

    @contextmanager
    def stage(self):
        with ExitStack() as self.buffers:
            yield
        self.buffers = self.ctx

    def sbuf(self, name, shape, dtype=F32):
        return self.buffers.enter_context(self.nc.sbuf_tensor(name, shape, dtype))

    def psum(self, name):
        return self.ctx.enter_context(self.nc.psum_tensor(name, [P, 512], F32))

    def sem(self, name):
        return self.ctx.enter_context(self.nc.semaphore(name))

    def block(self):
        self.open_block = self.nc.Block()
        return self.open_block.__enter__()

    def end_block(self):
        self.open_block.__exit__(None, None, None)


def rsqrt_op(dve, k, a, y, t, chain, before):
    dve.wait_ge(chain, before + k)
    if k == 0:
        ins = dve.tensor_scalar(y.bitcast(I32), a.bitcast(I32), -0.5, float(0x5F3759DF), ALU.mult, ALU.add)
    elif k % 3 == 1:
        ins = dve.tensor_tensor(t, y, y, ALU.mult)
    elif k % 3 == 2:
        ins = dve.scalar_tensor_tensor(t, t, -0.5, a, ALU.mult, ALU.mult)
    else:
        ins = dve.scalar_tensor_tensor(y, t, 1.5, y, ALU.add, ALU.mult)
    ins.then_inc(chain, 1)


RS = 10


def at(buf, index):
    return buf[:, bass.ds(index, 1)]


def need(eng, s, value):
    if not (isinstance(value, int) and value <= 0):
        eng.wait_ge(s, value)


def layer_norm(mem, name, x_all, xn, bank, ident, turn):
    stats = mem.sbuf(name + "_stats", [P, TILES, 6])
    mv = mem.sbuf(name + "_mv", [P, TILES, 2])
    var, rstd, tmp = (mem.sbuf(name + s, [P, TILES]) for s in ("_var", "_rstd", "_tmp"))
    stats_done, aggr_done, chain, rows_done = (mem.sem(name + s) for s in ("_stats", "_aggr", "_chain", "_rows"))
    turned, copied = mem.sem(name + "_turned"), mem.sem(name + "_copied")
    block = mem.block()

    @block.vector
    def _(dve):
        with dve.Fori(0, TILES) as t:
            dve.bn_stats(at(stats, t).rearrange("p t s -> p (t s)"), at(x_all, t).rearrange("p t d -> p (t d)"))\
                .then_inc(stats_done, 1)
        for t in range(TILES):
            dve.wait_ge(stats_done, t + 1)
            dve.bn_aggr(mv[:, t, :], stats[:, t, :]).then_inc(aggr_done, 1)
        dve.wait_ge(aggr_done, TILES)
        dve.tensor_scalar(var[:], mv[:, :, 1], 1e-5, None, ALU.add).then_inc(chain, 1)
        for k in range(RS):
            rsqrt_op(dve, k, var[:], rstd[:], tmp[:], chain, 1)
        dve.wait_ge(chain, 1 + RS)
        with dve.Fori(0, TILES) as t:
            dve.tensor_scalar(at(xn, t), at(x_all, t), mv[:, bass.ds(t, 1), 0], at(rstd, t), ALU.subtract, ALU.mult)\
                .then_inc(rows_done, 1)

    if turn is not None:
        @block.tensor
        def _(pe):
            for t in range(TILES):
                pe.wait_ge(rows_done, t + 1)
                ins = pe.transpose(bank[t // 4][:, P * (t % 4):P * (t % 4) + P], xn[:, t, :], ident[:])
                if t % 4 == 3:
                    ins.then_inc(turned, 1)

        @block.scalar
        def _(act):
            for h in range(2):
                act.wait_ge(turned, h + 1)
                act.copy(turn[:, 4 * h:4 * h + 4, :], bank[h][:].rearrange("p (t n) -> p t n", t=4)).then_inc(copied, 1)

    mem.end_block()


def cross_attention_wide(mem, w, x_all, xnT, bank, ident, gate):
    HEADS, HD, T = 8, 128, CTX
    G = 4 * T
    SCALE = float(1.0 / np.sqrt(np.float32(HD)))
    wq, wk, wv = (mem.sbuf(n, [P, HEADS * HD]) for n in ("s1_wq", "s1_wk", "s1_wv"))
    wfc = mem.sbuf("s1_wfc", [P, HEADS, D])
    kT = mem.sbuf("s1_kT", [P, B, HEADS, T])
    v = mem.sbuf("s1_v", [T, B, HEADS * HD])
    mask = mem.sbuf("s1_mask", [P, TILES, HEADS * T], mybir.dt.uint8)
    mask_cur = mem.sbuf("s1_mask_cur", [P, HEADS * T], mybir.dt.uint8)
    floor = mem.sbuf("s1_floor", [P, G])
    spare = mem.sbuf("s1_spare", [P, 3])
    qT = mem.sbuf("s1_qT", [P, HEADS, P])
    probs = mem.sbuf("s1_probs", [P, 2, G])
    stat = mem.sbuf("s1_stat", [P, 3, HEADS])
    pT = mem.sbuf("s1_pT", [T, HEADS, P])
    oT = mem.sbuf("s1_oT", [P, HEADS, P])
    Q, SC, TR, OUT = bank[0:2], bank[2:4], bank[4:6], bank[6:8]

    loads = mem.loads1
    floor_set, kv_out, kv_copied = mem.sem("s1_floor_set"), mem.sem("s1_kv_out"), mem.sem("s1_kv_copied")
    q_out, score_out, prob_T, attn_out, y_out = (mem.sem("s1_" + n) for n in
                                                 ("q_out", "score_out", "prob_T", "attn_out", "y_out"))
    q_copied, exp_done, prob_copied, attn_copied = (mem.sem("s1_" + n) for n in
                                                    ("q_copied", "exp_done", "prob_copied", "attn_copied"))
    masked, max_done, shifted, summed, inverted, x_done = (mem.sem("s1_" + n) for n in
                                                           ("masked", "max_done", "shifted", "summed", "inverted", "x_done"))
    probs_done, mask_copied = mem.sem("s1_probs_done"), mem.sem("s1_mask_copied")
    block = mem.block()

    @block.sync
    def _(sp):
        sp.dma_start(wk[:], w["L0_xattn_W_K"]).then_inc(loads["wk"], 16)
        sp.dma_start(wv[:], w["L0_xattn_W_V"]).then_inc(loads["wv"], 16)
        sp.dma_start(wq[:], w["L0_xattn_W_Q"]).then_inc(loads["wq"], 16)
        for b in range(B):
            for t in range(TB):
                sp.dma_start(mask[:, TB * b + t, :].rearrange("p (h k) -> p h k", k=T),
                             w["mask"][b, :, P * t:P * t + P, :].rearrange("h q k -> q h k")).then_inc(loads["mask"], 16)
        sp.dma_start(wfc[:], w["L0_xattn_W_fc"].rearrange("(h p) n -> p h n", p=HD)).then_inc(loads["wfc"], 16)
        mem.prefetch(sp)

    @block.tensor
    def _(pe):
        ctxT = mem.ctxT

        def project_q(j):
            for c in range(2):
                need(pe, q_copied, 2 * j + c - 1)
                for h in range(4):
                    head = 4 * c + h
                    ins = pe.matmul(Q[c][:, P * h:P * h + P], wq[:, HD * head:HD * head + HD], at(xnT, j),
                                    start=True, stop=True)
                ins.then_inc(q_out, 1)

        def scores(j):
            for c in range(2):
                pe.wait_ge(q_copied, 2 * j + c + 1)
                need(pe, shifted, 2 * j + c - 1)
                for h in range(4):
                    head = 4 * c + h
                    ins = pe.matmul(SC[c][:, T * h:T * h + T], qT[:, head, :], kT[:, bass.ds(j // TB, 1), head, :],
                                    start=True, stop=True)
                ins.then_inc(score_out, 1)

        def transpose_probs(j):
            for c in range(2):
                pe.wait_ge(probs_done, 2 * j + c + 1)
                need(pe, prob_copied, 2 * j)
                for h in range(4):
                    ins = pe.transpose(TR[c][0:T, P * h:P * h + P], probs[:, c, T * h:T * h + T], ident[:])
                ins.then_inc(prob_T, 1)

        def attend(j, b):
            for c in range(2):
                pe.wait_ge(prob_copied, 2 * j + c + 1)
                if c == 0:
                    need(pe, x_done, j)
                else:
                    need(pe, attn_copied, 2 * j)
                for h in range(4):
                    head = 4 * c + h
                    ins = pe.matmul(OUT[c][:, P * h:P * h + P], v[:, b, HD * head:HD * head + HD], pT[:, head, :],
                                    start=True, stop=True)
                ins.then_inc(attn_out, 1)

        def project_out(j):
            pe.wait_ge(attn_copied, 2 * j + 2)
            for head in range(HEADS):
                ins = pe.matmul(OUT[0][:, 0:D], oT[:, head, :], wfc[:, head, :], start=(head == 0),
                                stop=(head == HEADS - 1))
            ins.then_inc(y_out, 1)

        pe.wait_ge(loads["wk"], 16)
        for c in range(4):
            for h in range(2):
                head = 2 * c + h
                ins = pe.matmul(bank[c][:, 256 * h:256 * h + B * T], wk[:, HD * head:HD * head + HD],
                                ctxT[:, :, :].rearrange("p b t -> p (b t)"), start=True, stop=True)
            ins.then_inc(kv_out, 1)
        pe.wait_ge(loads["wv"], 16)
        for b in range(B):
            for c in range(2):
                pe.matmul(bank[4 + 2 * b + c][0:T, :], ctxT[:, b, :], wv[:, 512 * c:512 * c + 512],
                          start=True, stop=True).then_inc(kv_out, 1)
        pe.wait_ge(loads["wq"], 16)
        pe.wait_ge(kv_copied, 8)
        pe.wait_ge(loads["wfc"], 16)
        project_q(0)
        scores(0)

        def step(j, b):
            project_q(j + 1)
            transpose_probs(j)
            attend(j, b)
            scores(j + 1)
            project_out(j)

        step(0, 0)
        for b in range(B):
            with pe.Fori(max(TB * b, 1), TB * (b + 1) - (b == B - 1)) as j:
                step(j, b)
        transpose_probs(TILES - 1)
        attend(TILES - 1, B - 1)
        project_out(TILES - 1)

    @block.scalar
    def _(act):
        def copy_q(j):
            for c in range(2):
                act.wait_ge(q_out, 2 * j + c + 1)
                need(act, score_out, 2 * j + c - 1)
                act.activation(qT[:, 4 * c:4 * c + 4, :], Q[c][:].rearrange("p (h t) -> p h t", h=4), ACT.Copy,
                               scale=SCALE).then_inc(q_copied, 1)

        def exp(j):
            for c in range(2):
                act.wait_ge(shifted, 2 * j + c + 1)
                act.activation(probs[:, c, :], probs[:, c, :], ACT.Exp).then_inc(exp_done, 1)

        def copy_probs(j):
            for c in range(2):
                act.wait_ge(prob_T, 2 * j + c + 1)
                need(act, attn_out, 2 * j)
                act.copy(pT[:, 4 * c:4 * c + 4, :], TR[c][0:T, :].rearrange("p (h t) -> p h t", h=4))\
                    .then_inc(prob_copied, 1)

        def copy_attn(j):
            for c in range(2):
                act.wait_ge(attn_out, 2 * j + c + 1)
                need(act, y_out, j)
                act.copy(oT[:, 4 * c:4 * c + 4, :], OUT[c][:].rearrange("p (h t) -> p h t", h=4))\
                    .then_inc(attn_copied, 1)

        for c in range(4):
            act.wait_ge(kv_out, c + 1)
            src = bank[c][:, :].rearrange("p (h n) -> p h n", h=2)[:, :, 0:B * T]
            act.copy(kT[:, :, 2 * c:2 * c + 2, :].rearrange("p b h t -> p h b t"),
                     src.rearrange("p h (b t) -> p h b t", b=B)).then_inc(kv_copied, 1)
        for b in range(B):
            for c in range(2):
                act.wait_ge(kv_out, 4 + 2 * b + c + 1)
                act.copy(v[:, b, 512 * c:512 * c + 512], bank[4 + 2 * b + c][0:T, :]).then_inc(kv_copied, 1)
        def step(j):
            copy_q(j + 1)
            copy_probs(j)
            copy_attn(j)
            exp(j + 1)

        copy_q(0)
        exp(0)
        step(0)
        with act.Fori(1, TILES - 1) as j:
            step(j)
        copy_probs(TILES - 1)
        copy_attn(TILES - 1)

    @block.vector
    def _(dve):
        rows = lambda ap: ap.rearrange("p (h k) -> p h k", k=T)

        def softmax_front(j):
            for c in range(2):
                if c == 0:
                    dve.wait_ge(mask_copied, j + 1)
                    dve.memset(spare[:, 2:3], 0.0)
                dve.wait_ge(score_out, 2 * j + c + 1)
                dve.memset(spare[:, c:c + 1], 0.0)
                dve.wait_ge(floor_set, 1)
                dve.copy_predicated(SC[c][:, 0:G], mask_cur[:, G * c:G * c + G], floor[:]).then_inc(masked, 1)
            for c in range(2):
                dve.wait_ge(masked, 2 * j + c + 1)
                dve.tensor_reduce(stat[:, 0, 4 * c:4 * c + 4], rows(SC[c][:, 0:G]), AX, ALU.max).then_inc(max_done, 1)
            for c in range(2):
                dve.wait_ge(max_done, 2 * j + c + 1)
                need(dve, prob_T, 2 * j + c - 1)
                m = stat[:, 0, 4 * c:4 * c + 4].unsqueeze(2).broadcast_to([P, 4, T])
                dve.tensor_tensor(rows(probs[:, c, :]), rows(SC[c][:, 0:G]), m, ALU.subtract).then_inc(shifted, 1)

        def softmax_back(j):
            for c in range(2):
                dve.wait_ge(exp_done, 2 * j + c + 1)
                dve.tensor_reduce(stat[:, 1, 4 * c:4 * c + 4], rows(probs[:, c, :]), AX, ALU.add).then_inc(summed, 1)
            dve.wait_ge(summed, 2 * j + 2)
            need(dve, probs_done, 2 * j)
            dve.reciprocal(stat[:, 2, :], stat[:, 1, :]).then_inc(inverted, 1)

        def add(j):
            dve.wait_ge(y_out, j + 1)
            dve.scalar_tensor_tensor(x_all[:, bass.ds(j, 1), :].rearrange("p a d -> p (a d)"), OUT[0][:, 0:D], gate,
                                     x_all[:, bass.ds(j, 1), :].rearrange("p a d -> p (a d)"),
                                     ALU.mult, ALU.add).then_inc(x_done, 1)

        dve.memset(floor[:], -1e9).then_inc(floor_set, 1)
        def step(j):
            softmax_front(j + 1)
            add(j)
            softmax_back(j + 1)

        softmax_front(0)
        softmax_back(0)
        step(0)
        with dve.Fori(1, TILES - 1) as j:
            step(j)
        add(TILES - 1)

    @block.gpsimd
    def _(pool):
        def copy_mask(j):
            need(pool, masked, 2 * j)
            pool.tensor_copy(mask_cur[:].bitcast(I32).unsqueeze(1), at(mask[:].bitcast(I32), j)).then_inc(mask_copied, 1)

        def normalise_probs(j):
            pool.wait_ge(inverted, j + 1)
            for c in range(2):
                p = probs[:, c, :].rearrange("p (h k) -> p h k", k=T)
                r = stat[:, 2, 4 * c:4 * c + 4].unsqueeze(2).broadcast_to([P, 4, T])
                pool.tensor_tensor(p, p, r, ALU.mult).then_inc(probs_done, 1)

        pool.wait_ge(loads["mask"], 16 * TILES)
        copy_mask(0)
        copy_mask(1)
        normalise_probs(0)
        with pool.Fori(1, TILES - 1) as j:
            copy_mask(j + 1)
            normalise_probs(j)
        normalise_probs(TILES - 1)

    mem.end_block()


def mixture(mem, w, x_all, xnT, bank, ident, gate):
    E, HS = 8, 2
    N = S
    W = mem.w2s
    hT = mem.sbuf("s2_hT", [P, E, N])
    sT = mem.sbuf("s2_sT", [P, HS, N])
    gT = mem.sbuf("s2_gT", [P, HS, N])
    prob = mem.sbuf("s2_prob", [P, TILES, E])
    sel = mem.sbuf("s2_sel", [P, TILES, E])
    cmp = mem.sbuf("s2_cmp", [P, 2, TILES, E, E])
    rank = mem.sbuf("s2_rank", [P, TILES, E])
    comb = mem.sbuf("s2_comb", [P, TILES, E])
    den = mem.sbuf("s2_den", [P, 3, TILES])
    acc = mem.sbuf("s2_acc", [P, 2, D])
    HB, EO, SO = bank[0:4], bank[4:6], bank[6:8]

    route_out, routed = mem.sem("s2_route_out"), mem.sem("s2_routed")
    chain, comb_done = mem.sem("s2_chain"), mem.sem("s2_comb_done")
    hid_out, read_by_act, silu_done, gated = (mem.sem("s2_" + n) for n in ("hid_out", "read_by_act", "silu_done", "gated"))
    y_out, shared_out, acc_step, x_done = (mem.sem("s2_" + n) for n in ("y_out", "shared_out", "acc_step", "x_done"))
    loads = mem.loads2
    block = mem.block()

    @block.tensor
    def _(pe):
        pe.wait_ge(loads, 16 * 8)
        for t in range(TILES):
            ins = pe.matmul(SO[1][:, E * t:E * t + E], xnT[:, t, :], W["router"][:], start=True, stop=True)
        ins.then_inc(route_out, 1)
        pe.wait_ge(routed, 1)

        def hidden(p):
            x = xnT[:, p * TB:(p + 1) * TB, :]
            for c in range(E):
                if c < 2:
                    need(pe, read_by_act, (E + HS) * p)
                elif c < 4:
                    need(pe, gated, HS * p)
                else:
                    pe.wait_ge(read_by_act, (E + HS) * p + c - 3)
                pe.matmul(HB[c % 4][:], W["ew1"][:, c, :], x, start=True, stop=True).then_inc(hid_out, 1)
            for c in range(HS):
                pe.wait_ge(read_by_act, (E + HS) * p + 5 + c)
                pe.matmul(HB[c][:], W["sw1"][:, P * c:P * c + P], x, start=True, stop=True).then_inc(hid_out, 1)
            for c in range(HS):
                pe.wait_ge(read_by_act, (E + HS) * p + 7 + c)
                pe.matmul(HB[2 + c][:], W["sw3"][:, P * c:P * c + P], x, start=True, stop=True).then_inc(hid_out, 1)

        def outputs(p):
            for t in range(TB):
                pe.wait_ge(read_by_act, (E + HS) * p + E)
                need(pe, x_done, TB * p + t)
                cols = slice(P * t, P * t + P)
                for e in range(E):
                    ins = pe.matmul(EO[e // 4][:, D * (e % 4):D * (e % 4) + D], hT[:, e, cols], W["ew2"][:, e, :],
                                    start=True, stop=True)
                ins.then_inc(y_out, 1)
                pe.wait_ge(gated, HS * (p + 1))
                for c in range(HS):
                    ins = pe.matmul(SO[0][:, 0:D], sT[:, c, cols], W["sw2"][:, c, :], start=(c == 0), stop=(c == HS - 1))
                ins.then_inc(shared_out, 1)

        for p in range(B):
            hidden(p)
            outputs(p)

    @block.scalar
    def _(act):
        act.wait_ge(route_out, 1)
        act.activation(prob[:].rearrange("p t e -> p (t e)"), SO[1][:, 0:TILES * E], ACT.Sigmoid).then_inc(routed, 1)
        for p in range(B):
            for c in range(E):
                act.wait_ge(hid_out, 12 * p + c + 1)
                if c == 0:
                    need(act, y_out, TB * p)
                act.activation(hT[:, c, :], HB[c % 4][:], ACT.Gelu).then_inc(read_by_act, 1)
            for c in range(HS):
                act.wait_ge(hid_out, 12 * p + E + c + 1)
                need(act, gated, HS * p)
                act.activation(gT[:, c, :], HB[c][:], ACT.Silu).then_inc(read_by_act, 1)

    @block.vector
    def _(dve):
        steps = [0]

        def chained(ins):
            ins.then_inc(chain, 1)
            steps[0] += 1
            dve.wait_ge(chain, steps[0])

        wide = [P, TILES, E, E]
        dve.wait_ge(routed, 1)
        dve.wait_ge(loads, 16 * 8)
        bias = W["bias"][:].unsqueeze(1).broadcast_to([P, TILES, E])
        chained(dve.tensor_tensor(sel[:], prob[:], bias, ALU.add))
        other, own = sel[:].unsqueeze(2).broadcast_to(wide), sel[:].unsqueeze(3).broadcast_to(wide)
        for t in range(TILES):
            dve.tensor_tensor(cmp[:, 0, t], other[:, t], own[:, t], ALU.is_gt)
            ins = dve.tensor_tensor(cmp[:, 1, t], other[:, t], own[:, t], ALU.is_equal)
        chained(ins)
        before = W["before"][:].unsqueeze(1).broadcast_to([P, TILES, E * E])
        flat = lambda k: cmp[:, k].rearrange("p t e j -> p t (e j)")
        chained(dve.tensor_tensor(flat(1), flat(1), before, ALU.mult))
        chained(dve.tensor_tensor(flat(0), flat(0), flat(1), ALU.add))
        chained(dve.tensor_reduce(rank[:], cmp[:, 0], AX, ALU.add))
        chained(dve.tensor_scalar(rank[:], rank[:], 2.0, None, ALU.is_lt))
        chained(dve.tensor_tensor(comb[:], prob[:], rank[:], ALU.mult))
        chained(dve.tensor_reduce(den[:, 0, :], comb[:], AX, ALU.add))
        chained(dve.tensor_scalar(den[:, 1, :], den[:, 0, :], 1e-9, None, ALU.add))
        chained(dve.reciprocal(den[:, 1, :], den[:, 1, :]))
        chained(dve.tensor_scalar(den[:, 0, :], den[:, 0, :], 1e-9, None, ALU.is_gt))
        chained(dve.tensor_tensor(den[:, 1, :], den[:, 1, :], den[:, 0, :], ALU.mult))
        chained(dve.tensor_scalar(den[:, 2, :], den[:, 0, :], -0.5, 0.5, ALU.mult, ALU.add))
        spread = lambda k: den[:, k, :].unsqueeze(2).broadcast_to([P, TILES, E])
        chained(dve.tensor_tensor(comb[:], comb[:], spread(1), ALU.mult))
        chained(dve.tensor_tensor(rank[:], rank[:], spread(2), ALU.mult))
        chained(dve.tensor_tensor(comb[:], comb[:], rank[:], ALU.add))

        for p in range(B):
            for c in range(HS):
                dve.wait_ge(hid_out, 12 * p + E + HS + c + 1)
                dve.wait_ge(read_by_act, (E + HS) * p + E + c + 1)
                need(dve, shared_out, TB * p)
                dve.tensor_tensor(sT[:, c, :], HB[2 + c][:], gT[:, c, :], ALU.mult).then_inc(gated, 1)
            for t in range(TB):
                j = p * TB + t
                weight = lambda e: comb[:, bass.ds(j, 1), e:e + 1].rearrange("p a e -> p (a e)")
                dve.wait_ge(y_out, j + 1)
                for e in range(E):
                    a = acc[:, e % 2, :]
                    y = EO[e // 4][:, D * (e % 4):D * (e % 4) + D]
                    if e < 2:
                        ins = dve.tensor_scalar(a, y, weight(e), None, ALU.mult)
                    else:
                        dve.wait_ge(acc_step, 9 * j + e - 1)
                        ins = dve.scalar_tensor_tensor(a, y, weight(e), a, ALU.mult, ALU.add)
                    ins.then_inc(acc_step, 1)
                dve.wait_ge(shared_out, j + 1)
                dve.wait_ge(acc_step, 9 * j + 7)
                dve.tensor_tensor(acc[:, 0, :], SO[0][:, 0:D], acc[:, 0, :], ALU.add).then_inc(acc_step, 1)
                dve.wait_ge(acc_step, 9 * j + 9)
                dve.tensor_tensor(acc[:, 0, :], acc[:, 0, :], acc[:, 1, :], ALU.add).then_inc(silu_done, 1)
                dve.wait_ge(silu_done, j + 1)
                xt = x_all[:, bass.ds(j, 1), :].rearrange("p a d -> p (a d)")
                dve.scalar_tensor_tensor(xt, acc[:, 0, :], gate, xt, ALU.mult, ALU.add).then_inc(x_done, 1)

    mem.end_block()


def cross_attention_narrow(mem, w, x_all, xnT, bank, ident, gate):
    HEADS, HD, T = 16, 8, CTX
    SCALE = float(np.float32(1.0) / np.float32(HD ** -0.5))
    PARTS = [(0, 6), (6, 12), (12, 16)]
    W = mem.w3s
    kd = mem.sbuf("s3_kd", [P, B, HEADS, T])
    kT = mem.sbuf("s3_kT", [P, B, T])
    v = mem.sbuf("s3_v", [T, B, D])
    qT = mem.sbuf("s3_qT", [P, P])
    probs = mem.sbuf("s3_probs", [P, HEADS, T])
    stat = mem.sbuf("s3_stat", [P, 3, HEADS])
    pT = mem.sbuf("s3_pT", [T, HEADS, P])
    o = mem.sbuf("s3_o", [P, D])
    oT = mem.sbuf("s3_oT", [P, P])
    SC, TR, QB, AO, YO = bank[0:3], bank[3:5], bank[5], bank[6], bank[7]
    loads = mem.loads3
    kv_out, k_copied, kv_ready = mem.sem("s3_kv_out"), mem.sem("s3_k_copied"), mem.sem("s3_kv_ready")
    v_copied = mem.sem("s3_v_copied")
    q_out, score_out, prob_T, attn_out, o_T, y_out = (mem.sem("s3_" + n) for n in
                                                      ("q_out", "score_out", "prob_T", "attn_out", "o_T", "y_out"))
    q_copied, exp_done, prob_copied, o_copied = (mem.sem("s3_" + n) for n in
                                                 ("q_copied", "exp_done", "prob_copied", "o_copied"))
    max_done, shifted, summed, inverted, o_done, x_done = (mem.sem("s3_" + n) for n in
                                                           ("max_done", "shifted", "summed", "inverted", "o_done", "x_done"))
    block = mem.block()

    @block.tensor
    def _(pe):
        ctxT = mem.ctxT

        def project_q(j):
            need(pe, q_copied, j)
            pe.matmul(QB[:, 0:P], W["wq"][:], at(xnT, j), start=True, stop=True).then_inc(q_out, 1)

        def scores(j):
            pe.wait_ge(q_copied, j + 1)
            for c, (h0, h1) in enumerate(PARTS):
                need(pe, shifted, 3 * j + c - 2)
                pe.matmul(SC[c][:, 0:T * (h1 - h0)], qT[:],
                          kd[:, bass.ds(j // TB, 1), h0:h1, :].rearrange("p b h t -> p (b h t)"),
                          start=True, stop=True).then_inc(score_out, 1)

        def transpose_probs(j):
            for c in range(4):
                need(pe, exp_done, 3 * j + [1, 2, 2, 3][c])
                need(pe, prob_copied, 4 * j + max(c - 1, 0))
                for h in range(4):
                    ins = pe.transpose(TR[c % 2][0:T, P * h:P * h + P], probs[:, 4 * c + h, :], ident[:])
                ins.then_inc(prob_T, 1)

        def attend(j):
            need(pe, o_done, j)
            for c in range(4):
                pe.wait_ge(prob_copied, 4 * j + c + 1)
                for h in range(4 * c, 4 * c + 4):
                    ins = pe.matmul(AO[:, HD * h:HD * h + HD], pT[:, h, :], v[:, bass.ds(j // TB, 1), HD * h:HD * h + HD]
                                    .rearrange("p b n -> p (b n)"), start=True, stop=True)
            ins.then_inc(attn_out, 1)

        def project_out(j):
            pe.wait_ge(o_done, j + 1)
            need(pe, x_done, j)
            pe.transpose(YO[:, 0:P], o[:], ident[:]).then_inc(o_T, 1)
            pe.wait_ge(o_copied, j + 1)
            pe.matmul(YO[:, P:2 * P], oT[:], W["wproj"][:], start=True, stop=True).then_inc(y_out, 1)

        pe.wait_ge(loads, 16 * 4)
        pe.matmul(QB[:, 0:B * T], W["wkv"][:, 0:D], ctxT[:, :, :].rearrange("p b t -> p (b t)"), start=True, stop=True)\
            .then_inc(kv_out, 1)
        for b in range(B):
            pe.matmul(YO[0:T, D * b:D * b + D], ctxT[:, b, :], W["wkv"][:, D:2 * D], start=True, stop=True)\
                .then_inc(kv_out, 1)
        pe.wait_ge(v_copied, 2)
        def step(j):
            project_q(j + 1)
            transpose_probs(j)
            attend(j)
            scores(j + 1)
            project_out(j)

        project_q(0)
        pe.wait_ge(kv_ready, B)
        scores(0)
        step(0)
        with pe.Fori(1, TILES - 1) as j:
            step(j)
        transpose_probs(TILES - 1)
        attend(TILES - 1)
        project_out(TILES - 1)

    @block.scalar
    def _(act):
        def copy_q(j):
            act.wait_ge(q_out, j + 1)
            need(act, score_out, 3 * j)
            act.activation(qT[:], QB[:, 0:P], ACT.Copy, scale=SCALE).then_inc(q_copied, 1)

        def exp(j):
            for c, (h0, h1) in enumerate(PARTS):
                act.wait_ge(shifted, 3 * j + c + 1)
                act.activation(probs[:, h0:h1, :], probs[:, h0:h1, :], ACT.Exp).then_inc(exp_done, 1)

        def copy_probs(j):
            for c in range(4):
                act.wait_ge(prob_T, 4 * j + c + 1)
                if c == 0:
                    need(act, attn_out, j)
                act.copy(pT[:, 4 * c:4 * c + 4, :], TR[c % 2][0:T, :].rearrange("p (h t) -> p h t", h=4))\
                    .then_inc(prob_copied, 1)

        def copy_o(j):
            act.wait_ge(o_T, j + 1)
            need(act, y_out, j)
            act.copy(oT[:], YO[:, 0:P]).then_inc(o_copied, 1)

        act.wait_ge(kv_out, 1)
        act.copy(kT[:].rearrange("p b t -> p (b t)"), QB[:, 0:B * T]).then_inc(k_copied, 1)
        act.wait_ge(kv_out, 3)
        act.copy(v[:].rearrange("p b n -> p (b n)"), YO[0:T, 0:B * D]).then_inc(v_copied, 2)
        def step(j):
            copy_q(j + 1)
            copy_probs(j)
            exp(j + 1)
            copy_o(j)

        copy_q(0)
        exp(0)
        step(0)
        with act.Fori(1, TILES - 1) as j:
            step(j)
        copy_probs(TILES - 1)
        copy_o(TILES - 1)

    @block.vector
    def _(dve):
        def softmax_front(j):
            for c, (h0, h1) in enumerate(PARTS):
                sc = SC[c][:, 0:T * (h1 - h0)].rearrange("p (h k) -> p h k", k=T)
                dve.wait_ge(score_out, 3 * j + c + 1)
                dve.tensor_reduce(stat[:, 0, h0:h1], sc, AX, ALU.max).then_inc(max_done, 1)
            for c, (h0, h1) in enumerate(PARTS):
                sc = SC[c][:, 0:T * (h1 - h0)].rearrange("p (h k) -> p h k", k=T)
                dve.wait_ge(max_done, 3 * j + c + 1)
                need(dve, prob_T, 4 * j)
                dve.tensor_tensor(probs[:, h0:h1, :], sc, stat[:, 0, h0:h1].unsqueeze(2).broadcast_to([P, h1 - h0, T]),
                                  ALU.subtract).then_inc(shifted, 1)

        def softmax_back(j):
            dve.wait_ge(exp_done, 3 * j + 3)
            dve.tensor_reduce(stat[:, 1, :], probs[:], AX, ALU.add).then_inc(summed, 1)
            dve.wait_ge(summed, j + 1)
            dve.reciprocal(stat[:, 2, :], stat[:, 1, :]).then_inc(inverted, 1)

        def normalise(j):
            dve.wait_ge(attn_out, j + 1)
            dve.wait_ge(inverted, j + 1)
            need(dve, o_T, j)
            dve.tensor_tensor(o[:].rearrange("p (h d) -> p h d", d=HD), AO[:, 0:D].rearrange("p (h d) -> p h d", d=HD),
                              stat[:, 2, :].unsqueeze(2).broadcast_to([P, HEADS, HD]), ALU.mult).then_inc(o_done, 1)

        def add(j):
            dve.wait_ge(y_out, j + 1)
            xt = x_all[:, bass.ds(j, 1), :].rearrange("p a d -> p (a d)")
            dve.scalar_tensor_tensor(xt, YO[:, P:2 * P], gate, xt, ALU.mult, ALU.add).then_inc(x_done, 1)

        dve.wait_ge(k_copied, 1)
        dve.wait_ge(loads, 16 * 4)
        for b in range(B):
            dve.tensor_tensor(kd[:, b], kT[:, b, :].unsqueeze(1).broadcast_to([P, HEADS, T]),
                              W["own"][:].unsqueeze(2).broadcast_to([P, HEADS, T]), ALU.mult).then_inc(kv_ready, 1)
        def step(j):
            normalise(j)
            softmax_front(j + 1)
            add(j)
            softmax_back(j + 1)

        softmax_front(0)
        softmax_back(0)
        step(0)
        with dve.Fori(1, TILES - 1) as j:
            step(j)
        normalise(TILES - 1)
        add(TILES - 1)

    mem.end_block()


class Weights:
    pass


def local_weights(mem):
    lw = Weights()
    lw.wqkv = mem.sbuf("wqkv", [P, 2, 3 * INNER])
    lw.wo = mem.sbuf("wo", [P, LAYERS, PAIRS, D])
    lw.w1 = mem.sbuf("w1", [P, 2 * FF])
    lw.w2 = mem.sbuf("w2", [P, LAYERS, FC, D])
    lw.qk_scale = mem.sbuf("qk_scale", [P, LAYERS, 2, HD])
    lw.qk_swapped = mem.sbuf("qk_swapped", [P, LAYERS, 2, HD])
    lw.ln_scale = mem.sbuf("ln_scale", [P, LAYERS])
    lw.ln_shift = mem.sbuf("ln_shift", [P, LAYERS])
    lw.bias1 = mem.sbuf("bias1", [P, LAYERS, 2, FC])
    lw.bias2 = mem.sbuf("bias2", [P, LAYERS, D])
    lw.cos_t = mem.sbuf("cos_t", [P, TB, 2, HD])
    lw.sin_t = mem.sbuf("sin_t", [P, TB, 2, HD])
    lw.band = mem.sbuf("band", [P, TB, G])
    lw.keep = mem.sbuf("keep", [P, TB])
    lw.small_loaded, lw.wqkv_loaded, lw.w1_loaded, lw.wo_loaded, lw.w2_loaded = (
        mem.sem(n) for n in ("small_loaded", "wqkv_loaded", "w1_loaded", "wo_loaded", "w2_loaded"))
    return lw


N_SMALL = 12


def load_local_weights(sp, w, lw):
    small = [
        (lw.qk_scale[:, :, 0, :], w["L1_ffn_q_scale"].partition_broadcast(P)),
        (lw.qk_scale[:, :, 1, :], w["L1_ffn_k_scale"].partition_broadcast(P)),
        (lw.qk_swapped[:, :, 0, :], w["q_swapped"].partition_broadcast(P)),
        (lw.qk_swapped[:, :, 1, :], w["k_swapped"].partition_broadcast(P)),
        (lw.cos_t[:], w["cos"]), (lw.sin_t[:], w["sin"]), (lw.band[:], w["band"]), (lw.keep[:], w["keep"]),
        (lw.ln_scale[:], w["ln_g"]), (lw.ln_shift[:], w["ln_b"]), (lw.bias1[:], w["b1"]),
        (lw.bias2[:], w["L1_ffn_b2"].partition_broadcast(P)),
    ]
    for dst, src in small:
        sp.dma_start(dst, src).then_inc(lw.small_loaded, 16)
    assert len(small) == N_SMALL
    sp.dma_start(lw.wqkv[:, 0, :], w["L1_ffn_Wqkv"][0]).then_inc(lw.wqkv_loaded, 16)
    sp.dma_start(lw.w1[:], w["L1_ffn_W1"][0]).then_inc(lw.w1_loaded, 16)
    sp.dma_start(lw.wo[:], w["L1_ffn_Wo"].rearrange("l (k p) n -> p l k n", p=P)).then_inc(lw.wo_loaded, 16)
    for c in range(FC):
        sp.dma_start(lw.w2[0:ROWS[c], :, c, :], w["L1_ffn_W2"][:, 128 * c:128 * c + ROWS[c], :]
                     .rearrange("l p n -> p l n")).then_inc(lw.w2_loaded, 16)
    sp.wait_ge(lw.wqkv_loaded, 16)
    sp.dma_start(lw.wqkv[:, 1, :], w["L1_ffn_Wqkv"][1]).then_inc(lw.wqkv_loaded, 16)


def local_stage(mem, w, lw, x_all, x_in, ident, ident16, bank, gate, out):
    sbuf, sem = mem.sbuf, mem.sem
    wqkv, wo, w1, w2 = lw.wqkv, lw.wo, lw.w1, lw.w2
    ln_scale, ln_shift, bias1, bias2 = lw.ln_scale, lw.ln_shift, lw.bias1, lw.bias2
    qk_scale, qk_swapped, cos_t, sin_t, band, keep = lw.qk_scale, lw.qk_swapped, lw.cos_t, lw.sin_t, lw.band, lw.keep
    band16 = sbuf("band16", [P, TB, G], BF16)
    small_loaded, wqkv_loaded, w1_loaded, wo_loaded, w2_loaded = (
        lw.small_loaded, lw.wqkv_loaded, lw.w1_loaded, lw.wo_loaded, lw.w2_loaded)

    x_cur = sbuf("x_cur", [P, D])
    xs = sbuf("xs", [P, P + 1])
    ms = sbuf("ms", [P, P + 1])
    squares = sbuf("squares", [P, 2 * INNER])
    heads = sbuf("heads", [P, 2 * INNER])
    turned = sbuf("turned", [P, 2 * INNER])
    cos_l = sbuf("cos_l", [P, 2, HD])
    sin_l = sbuf("sin_l", [P, 2, HD])
    nf = sbuf("nf", [P, 4, 2 * HEADS])
    qT = sbuf("qT", [P, PAIRS, P])
    kT = sbuf("kT", [P, PAIRS, WIN + P])
    v_raw = sbuf("v_raw", [P, 2, INNER])
    v_win = sbuf("v_win", [KEYS, 2, INNER])
    probs = sbuf("probs", [P, GROUPS, G])
    rowmax = sbuf("rowmax", [P, 4 * GROUPS])
    rowsum = sbuf("rowsum", [P, 4 * GROUPS])
    rowinv = sbuf("rowinv", [P, 4 * GROUPS])
    pT = sbuf("pT", [KEYS, GROUPS, 512])
    aT = sbuf("aT", [P, PAIRS, P])
    mid = sbuf("mid", [P, D])
    midb = sbuf("midb", [P, D])
    st = sbuf("st", [P, 6])
    mv = sbuf("mv", [P, 2])
    spare = sbuf("spare", [P, 1])
    lnr = sbuf("lnr", [P, 3])
    xn = sbuf("xn", [P, D])
    xnT = sbuf("xnT", [P, P])
    gel = sbuf("gel", [P, FC, P])
    hT = sbuf("hT", [P, FC, P])

    QK, SC, TR, MX = bank[0:2], bank[2:4], bank[4:6], bank[6:8]

    setup_done, band_ready, kept_zero = sem("setup_done"), sem("band_ready"), sem("kept_zero")
    x_T, qk_out, v_out = sem("x_T"), sem("qk_out"), sem("v_out")
    head_T, score_out, prob_T, attn_T, attn_out = (sem("head_T"), sem("score_out"), sem("prob_T"),
                                                   sem("attn_T"), sem("attn_out"))
    mid_T, mid_back, xn_T, gate_out, up_out, ffn_out = (sem("mid_T"), sem("mid_back"), sem("xn_T"),
                                                        sem("gate_out"), sem("up_out"), sem("ffn_out"))
    squared, v_copied, head_copied, exp_done, prob_copied, attn_copied = (
        sem("squared"), sem("v_copied"), sem("head_copied"), sem("exp_done"), sem("prob_copied"),
        sem("attn_copied"))
    xn_copied, gelu_done = sem("xn_copied"), sem("gelu_done")
    x_shifted, rotated, squares_summed, normed = (sem("x_shifted"), sem("rotated"), sem("squares_summed"),
                                                  sem("normed"))
    keys_kept, shifted, inverted, mid_done = (sem("keys_kept"), sem("shifted"), sem("inverted"),
                                              sem("mid_done"))
    mid_shifted, xn_done, hidden_done, x_done = (sem("mid_shifted"), sem("xn_done"), sem("hidden_done"),
                                                 sem("x_done"))
    nf_step, ln_step, max_step, sum_step = sem("nf_step"), sem("ln_step"), sem("max_step"), sem("sum_step")
    xs_step, ms_step = sem("xs_step"), sem("ms_step")
    NF, LN = 4 + RS, 3 + RS
    x_loaded, tables_done, joined, probs_done, midb_done = (sem("x_loaded"), sem("tables_done"), sem("joined"),
                                                            sem("probs_done"), sem("midb_done"))
    v_placed, stored = sem("v_placed"), sem("stored")
    final_done = sem("final_done")

    block = mem.block()

    @block.sync
    def _(sp):
        def place_values(n):
            sp.wait_ge(v_copied, 2 * n + 2)
            need(sp, attn_T, 2 * n)
            cur = v_raw[:, bass.ds(n % 2, 1), :] if not isinstance(n, int) else v_raw[:, n % 2:n % 2 + 1, :]
            prev = v_raw[:, bass.ds((n + 1) % 2, 1), :] if not isinstance(n, int) else v_raw[:, (n + 1) % 2:(n + 1) % 2 + 1, :]
            sp.dma_start(v_win[WIN:KEYS, 0:1, :], cur[0:KEYS - WIN]).then_inc(v_placed, 16)
            sp.dma_start(v_win[0:KEYS, 1:2, :], cur[P - KEYS:P]).then_inc(v_placed, 16)
            sp.dma_start(v_win[0:WIN, 0:1, :], prev[P - WIN:P]).then_inc(v_placed, 16)

        sp.wait_ge(kept_zero, 1)
        place_values(0)
        place_values(1)
        with sp.Fori(2, TILES + 1) as n:
            place_values(n)
        with sp.Fori(1, LAYERS - 1) as layer:
            place_values(layer * TILES + 1)
            sp.wait_ge(v_out, 2 * TILES * layer)
            sp.dma_start(wqkv[:, bass.ds((layer + 1) % 2, 1), :],
                         w["L1_ffn_Wqkv"][bass.ds(layer + 1, 1)].rearrange("l p n -> p l n")).then_inc(wqkv_loaded, 16)
            sp.wait_ge(up_out, layer * TILES)
            sp.dma_start(w1[:], w["L1_ffn_W1"][bass.ds(layer, 1)].rearrange("l p n -> (l p) n")).then_inc(w1_loaded, 16)
            with sp.Fori(2, TILES + 1) as t:
                place_values(layer * TILES + t)
        last = (LAYERS - 1) * TILES
        place_values(last + 1)
        sp.wait_ge(up_out, last)
        sp.dma_start(w1[:], w["L1_ffn_W1"][LAYERS - 1]).then_inc(w1_loaded, 16)
        with sp.Fori(2, TILES) as t:
            place_values(last + t)
        sp.wait_ge(final_done, 1)
        sp.dma_start(out, x_in[:]).then_inc(stored, 16)
        sp.wait_ge(stored, 16)

    @block.tensor
    def _(pe):
        def transpose_x(n):
            pe.wait_ge(x_loaded, n + 1)
            need(pe, x_done, n - 2)
            pe.transpose(MX[1][:, 0:P], x_cur[:], ident[:]).then_inc(x_T, 1)

        def project_qk(n, c):
            pe.wait_ge(x_shifted, n + 1)
            need(pe, rotated, 4 * n + c - 1)
            layer = n // TILES
            if c == 0:
                pe.wait_ge(wqkv_loaded, 16 * (layer + 1))
            pe.matmul(QK[c % 2][:], xs[:, 0:P], wqkv[:, bass.ds(layer % 2, 1), 512 * c:512 * c + 512],
                      start=True, stop=True).then_inc(qk_out, 1)

        def project_v(n, c):
            if c == 1:
                need(pe, xn_copied, n - 1)
                need(pe, mid_done, n - 1)
            layer = n // TILES
            pe.matmul(MX[1 - c][:], xs[:, 0:P], wqkv[:, bass.ds(layer % 2, 1), 2 * INNER + 512 * c:2 * INNER + 512 * c + 512],
                      start=True, stop=True).then_inc(v_out, 1)

        def transpose_heads(i, c):
            pe.wait_ge(normed, 4 * i + c + 1)
            if c < 2:
                need(pe, prob_copied, 4 * i - 1 + c)
            else:
                pe.wait_ge(head_copied, 4 * i + c - 1)
            for k in range(4):
                col = 512 * c + 128 * k
                ins = pe.transpose(TR[c % 2][:, 128 * k:128 * k + 128], heads[:, col:col + 128], ident[:])
            ins.then_inc(head_T, 1)

        def scores(i, g):
            if g < 2:
                pe.wait_ge(head_copied, 4 * i + 3)
                need(pe, attn_copied, 2 * i - 1 + g)
            else:
                pe.wait_ge(head_copied, 4 * i + 4)
                pe.wait_ge(shifted, 4 * i + g - 1)
            bank = SC[g % 2]
            pe.matmul(bank[:, 0:G], ident16[:], band16[:, bass.ds(i % TB, 1), :], start=True, stop=False,
                      skip_group_check=True)
            for pp in range(2):
                for half in range(2):
                    col = (2 * pp + half) * KEYS
                    for h in range(2):
                        rows = slice(HD * h, HD * h + HD)
                        ins = pe.matmul(bank[rows, col:col + KEYS], qT[rows, 2 * g + pp, 64 * half:64 * half + 64],
                                        kT[rows, 2 * g + pp, 64 * half:64 * half + KEYS],
                                        start=False, stop=True, skip_group_check=True)
            ins.then_inc(score_out, 1)

        def transpose_probs(i, g):
            pe.wait_ge(probs_done, 4 * i + g + 1)
            if g < 2:
                pe.wait_ge(head_copied, 4 * i + 3 + g)
            else:
                pe.wait_ge(prob_copied, 4 * i + g - 1)
            for u in range(4):
                ins = pe.transpose(TR[g % 2][0:KEYS, 128 * u:128 * u + 128],
                                   probs[:, g, KEYS * u:KEYS * u + KEYS], ident[:])
            ins.then_inc(prob_T, 1)

        def attend(i, o):
            pe.wait_ge(prob_copied, 4 * i + 2 * o + 2)
            pe.wait_ge(shifted, 4 * i + 3 + o)
            if o == 0:
                pe.wait_ge(v_placed, 48 * (i + 1))
            for g in (2 * o, 2 * o + 1):
                for pp in range(2):
                    for half in range(2):
                        u = 2 * pp + half
                        col = (2 * (g % 2) + pp) * P + 64 * half
                        for h in range(2):
                            head = 2 * (2 * g + pp) + h
                            ins = pe.matmul(SC[o][HD * h:HD * h + HD, col:col + 64],
                                            v_win[:, half, HD * head:HD * head + HD],
                                            pT[:, g, 128 * u + 64 * h:128 * u + 64 * h + 64],
                                            start=True, stop=True, skip_group_check=True)
            ins.then_inc(attn_T, 1)

        def project_out(i):
            pe.wait_ge(attn_copied, 2 * i + 2)
            layer = i // TILES
            for k in range(PAIRS):
                ins = pe.matmul(MX[0][:, 0:D], aT[:, k, :], wo[:, bass.ds(layer, 1), k, :],
                                start=(k == 0), stop=(k == PAIRS - 1))
            ins.then_inc(attn_out, 1)

        def transpose_mid(m):
            pe.wait_ge(mid_done, m + 1)
            pe.transpose(MX[0][:, 0:P], mid[:], ident[:]).then_inc(mid_T, 1)

        def transpose_back(m):
            pe.wait_ge(mid_shifted, m + 1)
            pe.transpose(MX[0][:, 0:P], ms[:, 0:P], ident[:]).then_inc(mid_back, 1)

        def transpose_normed(m):
            pe.wait_ge(xn_done, m + 1)
            pe.transpose(MX[0][:, 0:P], xn[:], ident[:]).then_inc(xn_T, 1)

        def gate(m, n):
            pe.wait_ge(xn_copied, m + 1)
            pe.wait_ge(w1_loaded, 16 * (m // TILES + 1))
            if n is not None:
                pe.wait_ge(v_copied, 2 * n + 1)
            for c in range(FC):
                ins = pe.matmul(MX[1][0:ROWS[c], 128 * c:128 * c + 128], w1[:, FF + 128 * c:FF + 128 * c + ROWS[c]],
                                xnT[:], start=True, stop=True)
            ins.then_inc(gate_out, 1)

        def up(m, n):
            if n is not None:
                pe.wait_ge(v_copied, 2 * n + 2)
            for c in range(FC):
                ins = pe.matmul(MX[0][0:ROWS[c], 128 * c:128 * c + 128], w1[:, 128 * c:128 * c + ROWS[c]],
                                xnT[:], start=True, stop=True)
            ins.then_inc(up_out, 1)

        def down(m):
            pe.wait_ge(hidden_done, m + 1)
            layer = m // TILES
            for c in range(FC):
                ins = pe.matmul(MX[1][:, 0:D], hT[0:ROWS[c], c, :], w2[0:ROWS[c], bass.ds(layer, 1), c, :],
                                start=(c == 0), stop=(c == FC - 1))
            ins.then_inc(ffn_out, 1)

        def step(i, has_next=True, has_last=True):
            n, m = (i + 1 if has_next else None), i - 1
            transpose_heads(i, 0)
            transpose_heads(i, 1)
            if has_last:
                transpose_mid(m)
            if has_next:
                transpose_x(n)
            transpose_heads(i, 2)
            transpose_heads(i, 3)
            if has_next:
                project_qk(n, 0)
                project_qk(n, 1)
            if has_last:
                transpose_back(m)
            scores(i, 0)
            scores(i, 1)
            if has_next:
                project_qk(n, 2)
            scores(i, 2)
            scores(i, 3)
            if has_next:
                project_qk(n, 3)
                project_v(n, 0)
            if has_last:
                transpose_normed(m)
            transpose_probs(i, 0)
            transpose_probs(i, 1)
            if has_next:
                project_v(n, 1)
            attend(i, 0)
            if has_last:
                gate(m, n)
                up(m, n)
            transpose_probs(i, 2)
            transpose_probs(i, 3)
            attend(i, 1)
            if has_last:
                down(m)
            elif has_next:
                pe.wait_ge(v_copied, 2 * n + 2)
            project_out(i)

        transpose_x(0)
        for c in range(4):
            project_qk(0, c)
        project_v(0, 0)
        project_v(0, 1)
        pe.wait_ge(v_copied, 2)
        pe.wait_ge(wo_loaded, 16)
        pe.wait_ge(w2_loaded, 16 * FC)
        pe.wait_ge(band_ready, 1)
        step(0, has_last=False)
        step(1)
        with pe.Fori(2, N - 1) as i:
            step(i)
        step(N - 1, has_next=False)
        transpose_mid(N - 1)
        transpose_back(N - 1)
        transpose_normed(N - 1)
        gate(N - 1, None)
        up(N - 1, None)
        down(N - 1)

    @block.scalar
    def _(act):
        def copy_head(i, c):
            act.wait_ge(head_T, 4 * i + c + 1)
            if c == 0:
                need(act, score_out, 4 * i)
            if c == 2:
                act.wait_ge(keys_kept, i + 1)
            src = TR[c % 2][:, :].rearrange("p (k t) -> p k t", k=4)
            k0 = 4 * (c % 2)
            dst = qT[:, k0:k0 + 4, :] if c < 2 else kT[:, k0:k0 + 4, WIN:WIN + P]
            act.copy(dst, src).then_inc(head_copied, 1)

        def square(n, c):
            act.wait_ge(qk_out, 4 * n + c + 1)
            if c == 0:
                need(act, squares_summed, n)
            act.activation(squares[:, 512 * c:512 * c + 512], QK[c % 2][:], ACT.Square).then_inc(squared, 1)

        def exp(i, g):
            act.wait_ge(shifted, 4 * i + g + 1)
            act.activation(probs[:, g, :], probs[:, g, :], ACT.Exp).then_inc(exp_done, 1)

        def copy_values(n, c):
            act.wait_ge(v_out, 2 * n + c + 1)
            if c == 0:
                need(act, v_placed, 48 * n)
            par = n % 2
            dst = v_raw[:, bass.ds(par, 1), 512 * c:512 * c + 512]
            act.copy(dst, MX[1 - c][:].unsqueeze(1)).then_inc(v_copied, 1)

        def copy_probs(i, g):
            act.wait_ge(prob_T, 4 * i + g + 1)
            if g == 0:
                need(act, attn_T, 2 * i)
            act.copy(pT[:, g, :], TR[g % 2][0:KEYS, :]).then_inc(prob_copied, 1)

        def copy_attn(i, o):
            act.wait_ge(attn_T, 2 * i + o + 1)
            if o == 0:
                need(act, attn_out, i)
            act.copy(aT[:, 4 * o:4 * o + 4, :], SC[o][:].rearrange("p (k t) -> p k t", k=4)).then_inc(attn_copied, 1)

        def copy_normed(m):
            act.wait_ge(xn_T, m + 1)
            need(act, up_out, m)
            layer = m // TILES
            act.activation(xnT[:], MX[0][:, 0:P], ACT.Identity, scale=at(ln_scale, layer),
                           bias=at(ln_shift, layer)).then_inc(xn_copied, 1)

        def gelu(m):
            act.wait_ge(gate_out, m + 1)
            need(act, hidden_done, m)
            layer = m // TILES
            for c in range(FC):
                ins = act.activation(gel[0:ROWS[c], c, :], MX[1][0:ROWS[c], 128 * c:128 * c + 128], ACT.Gelu,
                                     bias=bias1[0:ROWS[c], bass.ds(layer, 1), 1, c:c + 1].rearrange("p l c -> p (l c)"))
            ins.then_inc(gelu_done, 1)

        def step(i, has_next=True, has_last=True):
            n, m = i + 1, i - 1
            for c in range(4):
                copy_head(i, c)
            if has_next:
                square(n, 0)
                square(n, 1)
            exp(i, 0)
            exp(i, 1)
            if has_next:
                square(n, 2)
            exp(i, 2)
            exp(i, 3)
            if has_next:
                square(n, 3)
                copy_values(n, 0)
            if has_last:
                copy_normed(m)
            copy_probs(i, 0)
            copy_probs(i, 1)
            if has_next:
                copy_values(n, 1)
            copy_attn(i, 0)
            if has_last:
                gelu(m)
            copy_probs(i, 2)
            copy_probs(i, 3)
            copy_attn(i, 1)

        act.wait_ge(small_loaded, 16 * N_SMALL)
        act.wait_ge(kept_zero, 1)
        for c in range(4):
            square(0, c)
        copy_values(0, 0)
        copy_values(0, 1)
        step(0, has_last=False)
        step(1)
        with act.Fori(2, N - 1) as i:
            step(i)
        step(N - 1, has_next=False)
        copy_normed(N - 1)
        gelu(N - 1)

    @block.vector
    def _(dve):
        half_rows = slice(P // 2, P)

        def shift_tokens(buf, bank, tile, step_sem, k0, done):
            dve.tensor_scalar(buf[half_rows, 0:1], buf[half_rows, P:P + 1],
                              keep[half_rows, bass.ds(tile % TB, 1)], None, ALU.mult).then_inc(step_sem, 1)
            dve.tensor_copy(buf[0:P // 2, 0:P], bank[0:P // 2, 0:P])
            dve.wait_ge(step_sem, k0 + 1)
            dve.tensor_copy(buf[half_rows, 1:P + 1], bank[half_rows, 0:P]).then_inc(done, 1)

        def shift_x(n):
            dve.wait_ge(x_T, n + 1)
            need(dve, v_out, 2 * n)
            need(dve, x_shifted, n)
            shift_tokens(xs, MX[1], n, xs_step, n, x_shifted)

        def shift_mid(m):
            dve.wait_ge(mid_T, m + 1)
            need(dve, mid_back, m)
            need(dve, mid_shifted, m)
            shift_tokens(ms, MX[0], m, ms_step, m, mid_shifted)

        def by_head(ap):
            return ap.rearrange("p (h d) -> p h d", d=HD)

        def rotate_cos(n, c):
            dve.wait_ge(squared, 4 * n + c + 1)
            dve.wait_ge(tables_done, 2 * n + 2)
            need(dve, head_T, 4 * n + c - 3)
            table = cos_l[:, c // 2, :].unsqueeze(1).broadcast_to([P, 8, HD])
            dve.tensor_tensor(by_head(heads[:, 512 * c:512 * c + 512]), by_head(QK[c % 2][:]), table, ALU.mult)

        def rotate_sin(n, c):
            need(dve, joined, 4 * n + c - 3)
            halves = lambda ap: ap.rearrange("p (h two d) -> p h two d", two=2, d=HD // 2)
            table = sin_l[:, c // 2, :].rearrange("p (two d) -> p two d", two=2).unsqueeze(1).broadcast_to(
                [P, 8, 2, HD // 2])
            dve.tensor_tensor(halves(turned[:, 512 * c:512 * c + 512]), halves(QK[c % 2][:])[:, :, ::-1, :], table,
                              ALU.mult).then_inc(rotated, 1)

        def sum_squares(n, c):
            dve.wait_ge(squared, 4 * n + c + 1)
            ins = dve.tensor_reduce(nf[:, 0, 8 * c:8 * c + 8], by_head(squares[:, 512 * c:512 * c + 512]), AX, ALU.add)
            ins.then_inc(nf_step, 1)
            if c == 3:
                dve.wait_ge(nf_step, NF * n + 4)
                dve.tensor_scalar(nf[:, 1, :], nf[:, 0, :], 1e-24, None, ALU.max).then_inc(squares_summed, 1)

        def norm_factor(n, k):
            if k == 0:
                dve.wait_ge(squares_summed, n + 1)
            rsqrt_op(dve, k, nf[:, 1, :], nf[:, 2, :], nf[:, 3, :], nf_step, NF * n + 4)

        def normalise(n, c):
            dve.wait_ge(joined, 4 * n + c + 1)
            dve.wait_ge(nf_step, NF * (n + 1))
            r = nf[:, 2, 8 * c:8 * c + 8].unsqueeze(2).broadcast_to([P, 8, HD])
            h = by_head(heads[:, 512 * c:512 * c + 512])
            dve.tensor_tensor(h, h, r, ALU.mult).then_inc(normed, 1)

        def keep_keys(i):
            need(dve, head_copied, 4 * i)
            need(dve, score_out, 4 * i)
            dve.tensor_copy(kT[:, :, 0:WIN], kT[:, :, P:P + WIN]).then_inc(keys_kept, 1)

        def units(ap):
            return ap.rearrange("p (u k) -> p u k", k=KEYS)

        def row_max(i, g):
            dve.wait_ge(score_out, 4 * i + g + 1)
            dve.tensor_reduce(rowmax[:, 4 * g:4 * g + 4], units(SC[g % 2][:, 0:G]), AX, ALU.max).then_inc(max_step, 1)

        def subtract_max(i, g):
            dve.wait_ge(max_step, 4 * i + g + 1)
            need(dve, prob_T, 4 * i + g - 3)
            m = rowmax[:, 4 * g:4 * g + 4].unsqueeze(2).broadcast_to([P, 4, KEYS])
            dve.tensor_tensor(units(probs[:, g, :]), units(SC[g % 2][:, 0:G]), m, ALU.subtract).then_inc(shifted, 1)

        def row_sum(i, g):
            dve.wait_ge(exp_done, 4 * i + g + 1)
            dve.tensor_reduce(rowsum[:, 4 * g:4 * g + 4], units(probs[:, g, :]), AX, ALU.add).then_inc(sum_step, 1)

        def invert(i, g2):
            dve.wait_ge(sum_step, 4 * i + 2 * g2 + 2)
            need(dve, probs_done, 4 * i + 2 * g2 - 2)
            dve.reciprocal(rowinv[:, 8 * g2:8 * g2 + 8], rowsum[:, 8 * g2:8 * g2 + 8]).then_inc(inverted, 1)

        def ln(m, k):
            base = LN * m
            if k == 0:
                dve.wait_ge(mid_back, m + 1)
                dve.bn_stats(st[:], MX[0][:, 0:D]).then_inc(ln_step, 1)
            elif k == 1:
                dve.wait_ge(ln_step, base + 1)
                dve.memset(spare[:], 0.0)
                dve.bn_aggr(mv[:], st[:]).then_inc(ln_step, 1)
            elif k == 2:
                dve.wait_ge(ln_step, base + 2)
                dve.tensor_scalar(lnr[:, 0:1], mv[:, 1:2], 1e-5, None, ALU.add).then_inc(ln_step, 1)
            elif k < LN:
                rsqrt_op(dve, k - 3, lnr[:, 0:1], lnr[:, 1:2], lnr[:, 2:3], ln_step, base + 3)
            else:
                dve.wait_ge(ln_step, base + LN)
                need(dve, xn_T, m)
                dve.tensor_scalar(xn[:], MX[0][:, 0:D], mv[:, 0:1], lnr[:, 1:2], ALU.subtract, ALU.mult)\
                    .then_inc(xn_done, 1)

        def hidden(m):
            dve.wait_ge(up_out, m + 1)
            dve.wait_ge(gelu_done, m + 1)
            need(dve, ffn_out, m)
            layer = m // TILES
            for c in range(FC):
                ins = dve.scalar_tensor_tensor(
                    hT[0:ROWS[c], c, :], MX[0][0:ROWS[c], 128 * c:128 * c + 128],
                    bias1[0:ROWS[c], bass.ds(layer, 1), 0, c:c + 1].rearrange("p l c -> p (l c)"),
                    gel[0:ROWS[c], c, :], ALU.add, ALU.mult)
            ins.then_inc(hidden_done, 1)

        def new_x(m):
            dve.wait_ge(ffn_out, m + 1)
            dve.wait_ge(midb_done, m + 1)
            dve.tensor_tensor(x_all[:, bass.ds(m % TILES, 1), :], MX[1][:, 0:D].unsqueeze(1), midb[:].unsqueeze(1),
                              ALU.add).then_inc(x_done, 1)

        def new_mid(i):
            dve.wait_ge(attn_out, i + 1)
            need(dve, mid_T, i)
            need(dve, midb_done, i)
            dve.tensor_tensor(mid[:].unsqueeze(1), MX[0][:, 0:D].unsqueeze(1), x_all[:, bass.ds(i % TILES, 1), :],
                              ALU.add).then_inc(mid_done, 1)

        def step(i, has_next=True, has_last=True):
            n, m = i + 1, i - 1
            norm = (lambda k: ln(m, k)) if has_last else (lambda k: None)
            keep_keys(i)
            if has_last:
                shift_mid(m)
            if has_next:
                shift_x(n)
                rotate_cos(n, 0)
                rotate_sin(n, 0)
                rotate_cos(n, 1)
                rotate_sin(n, 1)
            norm(0)
            row_max(i, 0)
            norm(1)
            row_max(i, 1)
            norm(2)
            subtract_max(i, 0)
            norm(3)
            subtract_max(i, 1)
            norm(4)
            if has_next:
                rotate_cos(n, 2)
            norm(5)
            if has_next:
                rotate_sin(n, 2)
            norm(6)
            row_max(i, 2)
            norm(7)
            row_max(i, 3)
            norm(8)
            subtract_max(i, 2)
            norm(9)
            subtract_max(i, 3)
            norm(10)
            row_sum(i, 0)
            norm(11)
            row_sum(i, 1)
            norm(12)
            invert(i, 0)
            if has_next:
                rotate_cos(n, 3)
            norm(13)
            if has_next:
                rotate_sin(n, 3)
            row_sum(i, 2)
            row_sum(i, 3)
            invert(i, 1)
            if has_next:
                for c in range(4):
                    sum_squares(n, c)
                for k in range(RS // 2):
                    norm_factor(n, k)
            if has_last:
                hidden(m)
            if has_next:
                for k in range(RS // 2, RS):
                    norm_factor(n, k)
                for c in range(4):
                    normalise(n, c)
            if has_last:
                new_x(m)
            new_mid(i)

        dve.wait_ge(setup_done, 3)
        dve.wait_ge(small_loaded, 16 * N_SMALL)
        dve.tensor_copy(band16[:], band[:]).then_inc(band_ready, 1)
        shift_x(0)
        for c in range(4):
            rotate_cos(0, c)
            rotate_sin(0, c)
        for c in range(4):
            sum_squares(0, c)
        for k in range(RS):
            norm_factor(0, k)
        for c in range(4):
            normalise(0, c)
        step(0, has_last=False)
        step(1)
        with dve.Fori(2, N - 1) as i:
            step(i)
        step(N - 1, has_next=False)
        shift_mid(N - 1)
        for k in range(LN + 1):
            ln(N - 1, k)
        hidden(N - 1)
        new_x(N - 1)
        dve.wait_ge(x_done, N)
        dve.scalar_tensor_tensor(x_in[:], x_all[:], gate, x_in[:], ALU.mult, ALU.add).then_inc(final_done, 1)

    @block.gpsimd
    def _(pool):
        def load_x(n):
            need(pool, x_T, n)
            need(pool, x_done, n - 2)
            pool.tensor_copy(x_cur[:].unsqueeze(1), x_all[:, bass.ds(n % TILES, 1), :]).then_inc(x_loaded, 1)

        def tables(n):
            need(pool, rotated, 4 * n)
            layer = n // TILES
            sc = qk_scale[:, bass.ds(layer, 1), :, :]
            pool.tensor_tensor(cos_l[:].unsqueeze(1), cos_t[:, bass.ds(n % TB, 1), :, :], sc, ALU.mult)\
                .then_inc(tables_done, 1)
            pool.tensor_tensor(sin_l[:].unsqueeze(1), sin_t[:, bass.ds(n % TB, 1), :, :],
                               qk_swapped[:, bass.ds(layer, 1), :, :], ALU.mult).then_inc(tables_done, 1)

        def join(n, c):
            pool.wait_ge(rotated, 4 * n + c + 1)
            cols = slice(512 * c, 512 * c + 512)
            pool.tensor_tensor(heads[:, cols], heads[:, cols], turned[:, cols], ALU.add).then_inc(joined, 1)

        def normalise_probs(i, g):
            pool.wait_ge(inverted, 2 * i + g // 2 + 1)
            r = rowinv[:, 4 * g:4 * g + 4].unsqueeze(2).broadcast_to([P, 4, KEYS])
            p = probs[:, g, :].rearrange("p (u k) -> p u k", k=KEYS)
            pool.tensor_tensor(p, p, r, ALU.mult).then_inc(probs_done, 1)

        def add_bias(i):
            pool.wait_ge(mid_done, i + 1)
            need(pool, x_done, i)
            pool.tensor_tensor(midb[:].unsqueeze(1), mid[:].unsqueeze(1), bias2[:, bass.ds(i // TILES, 1), :],
                               ALU.add).then_inc(midb_done, 1)

        def step(i, has_next=True):
            n = i + 1
            if has_next:
                load_x(n)
                tables(n)
                join(n, 0)
                join(n, 1)
                join(n, 2)
            normalise_probs(i, 0)
            normalise_probs(i, 1)
            if has_next:
                join(n, 3)
            normalise_probs(i, 2)
            normalise_probs(i, 3)
            add_bias(i)

        load_x(0)
        pool.memzero(xs[:]).then_inc(setup_done, 1)
        pool.memzero(ms[:]).then_inc(setup_done, 1)
        pool.memzero(kT[:]).then_inc(setup_done, 1)
        pool.memzero(v_raw[:, 1, :]).then_inc(kept_zero, 1)
        pool.wait_ge(small_loaded, 16 * N_SMALL)
        tables(0)
        for c in range(4):
            join(0, c)
        step(0)
        step(1)
        with pool.Fori(2, N - 1) as i:
            step(i)
        step(N - 1, has_next=False)

    mem.end_block()


def program(nc, w, out):
    with ExitStack() as ctx:
        mem = Memory(nc, ctx)
        bank = [mem.psum(f"bank{k}") for k in range(8)]
        x_all = mem.sbuf("x_all", [P, TILES, D])
        xn = mem.sbuf("xn_all", [P, TILES, D])
        xnT = mem.sbuf("xnT_all", [P, TILES, P])
        ident = mem.sbuf("ident", [P, P])
        ident16 = mem.sbuf("ident16", [P, P], BF16)
        gates = mem.sbuf("gates", [P, 4])
        gates_t = mem.sbuf("gates_t", [P, 4])
        ctx_rows = mem.sbuf("ctx_rows", [CTX, B, D])
        mem.ctxT = mem.sbuf("ctxT", [P, B, CTX])
        mem.w2s = {n: mem.sbuf("w2_" + n, s) for n, s in (
            ("ew1", [P, 8, P]), ("ew2", [P, 8, D]), ("sw1", [P, 2 * P]), ("sw3", [P, 2 * P]), ("sw2", [P, 2, D]),
            ("router", [P, 8]), ("bias", [P, 8]), ("before", [P, 64]))}
        mem.w3s = {n: mem.sbuf("w3_" + n, s) for n, s in (
            ("wq", [P, D]), ("wkv", [P, 2 * D]), ("wproj", [P, D]), ("own", [P, 16]))}
        lw = local_weights(mem)
        loaded, x_loaded0, turned, ready = mem.sem("loaded"), mem.sem("x_loaded0"), mem.sem("turned"), mem.sem("ready")
        mem.loads1 = {n: mem.sem("s1_load_" + n) for n in ("wk", "wv", "wq", "mask", "wfc")}
        mem.loads2, mem.loads3 = mem.sem("s2_loads"), mem.sem("s3_loads")

        def prefetch(sp):
            for name, src in (("ew1", w["L0_ffn_ew1"].rearrange("e p n -> p e n")),
                              ("ew2", w["L0_ffn_ew2"].rearrange("e p n -> p e n")),
                              ("sw1", w["L0_ffn_sw1"]), ("sw3", w["L0_ffn_sw3"]),
                              ("sw2", w["L0_ffn_sw2"].rearrange("(c p) n -> p c n", p=P)),
                              ("router", w["router_T"]), ("bias", w["L0_ffn_router_bias"].partition_broadcast(P)),
                              ("before", w["before"])):
                sp.dma_start(mem.w2s[name][:], src).then_inc(mem.loads2, 16)
            for name, src in (("wq", w["L1_xattn_W_q"]), ("wkv", w["L1_xattn_W_kv"]), ("wproj", w["L1_xattn_W_proj"]),
                              ("own", w["own"])):
                sp.dma_start(mem.w3s[name][:], src).then_inc(mem.loads3, 16)
            load_local_weights(sp, w, lw)

        mem.prefetch = prefetch
        block = mem.block()

        @block.sync
        def _(sp):
            sp.dma_start(ident[:], w["ident"]).then_inc(loaded, 16)
            sp.dma_start(ctx_rows[:], w["ctx_1024"].rearrange("b t d -> t b d")).then_inc(loaded, 16)
            sp.dma_start(gates[:, 0:2], w["g_xattn"].partition_broadcast(P)).then_inc(loaded, 16)
            sp.dma_start(gates[:, 2:4], w["g_ffn"].partition_broadcast(P)).then_inc(loaded, 16)
            sp.dma_start(x_all[:], w["x"].rearrange("b (t p) d -> p (b t) d", p=P)).then_inc(x_loaded0, 16)
            sp.wait_ge(x_loaded0, 16)

        @block.tensor
        def _(pe):
            pe.wait_ge(loaded, 64)
            for b in range(B):
                ins = pe.transpose(bank[0][:, CTX * b:CTX * b + CTX], ctx_rows[:, b, :], ident[0:CTX, 0:CTX])
            ins.then_inc(turned, 1)

        @block.vector
        def _(dve):
            dve.wait_ge(loaded, 64)
            dve.tensor_copy(ident16[:], ident[:]).then_inc(ready, 1)

        @block.scalar
        def _(act):
            act.wait_ge(loaded, 64)
            act.activation(gates_t[:], gates[:], ACT.Tanh).then_inc(ready, 1)
            act.wait_ge(turned, 1)
            act.copy(mem.ctxT[:].rearrange("p b t -> p (b t)"), bank[0][:, 0:B * CTX]).then_inc(ready, 1)

        mem.end_block()
        with mem.stage():
            layer_norm(mem, "ln1", x_all, xn, bank, ident, xnT)
        with mem.stage():
            cross_attention_wide(mem, w, x_all, xnT, bank, ident, gates_t[:, 0:1])
        with mem.stage():
            layer_norm(mem, "ln2", x_all, xn, bank, ident, xnT)
        with mem.stage():
            mixture(mem, w, x_all, xnT, bank, ident, gates_t[:, 2:3])
        with mem.stage():
            layer_norm(mem, "ln3", x_all, xn, bank, ident, xnT)
        with mem.stage():
            cross_attention_narrow(mem, w, x_all, xnT, bank, ident, gates_t[:, 1:2])
        with mem.stage():
            layer_norm(mem, "ln4", x_all, xn, bank, ident, None)
        with mem.stage():
            local_stage(mem, w, lw, xn, x_all, ident, ident16, bank, gates_t[:, 3:4], out)


_DIRECT = ["x", "ctx_1024", "g_xattn", "g_ffn", "L0_xattn_W_Q", "L0_xattn_W_K", "L0_xattn_W_V", "L0_xattn_W_fc",
           "L0_ffn_router_bias", "L0_ffn_sw1", "L0_ffn_sw3", "L0_ffn_sw2", "L0_ffn_ew1", "L0_ffn_ew2", "L1_xattn_W_q",
           "L1_xattn_W_kv", "L1_xattn_W_proj", "L1_ffn_Wqkv", "L1_ffn_q_scale", "L1_ffn_k_scale", "L1_ffn_Wo",
           "L1_ffn_W1", "L1_ffn_W2", "L1_ffn_b2"]


def _constants():
    half = np.arange(0, HD, 2, dtype=np.float64)
    position = np.arange(S, dtype=np.float64)
    angle = np.tile(position[:, None] * 10000.0 ** (-half / HD)[None, :], (1, 2))
    base = (half + 0.4 * HD) / (1.4 * HD)
    scale = np.tile(base[None, :] ** ((position - S // 2) / (WIN // 2))[:, None], (1, 2))
    sign = np.repeat([-1.0, 1.0], HD // 2)
    cos, sin = np.cos(angle), np.sin(angle) * sign
    by_tile = lambda q, k: np.stack([q, k], 1).reshape(TB, P, 2, HD).transpose(1, 0, 2, 3).astype(np.float32)
    query, key = np.arange(P)[:, None] % (P // 2), np.arange(KEYS)[None, :]
    seen = (key >= query) & (key <= query + WIN)
    band = np.zeros((P, TB, 4, KEYS), np.float32)
    for t in range(TB):
        for unit in range(4):
            first = (t == 0) and (unit % 2 == 0)
            band[:, t, unit][~(seen & (key >= WIN)) if first else ~seen] = -1e30
    keep = np.ones((P, TB), np.float32)
    keep[:, 0] = 0.0
    before = np.tile(np.tril(np.ones((8, 8), np.float32), -1).reshape(1, 64), (P, 1))
    own = (np.arange(P)[:, None] // 8 == np.arange(16)[None, :]).astype(np.float32)
    q_factor = 8.0
    return {"ident": np.eye(P, dtype=np.float32), "cos": by_tile(q_factor * cos * scale, cos / scale),
            "sin": by_tile(q_factor * sin * scale, sin / scale), "band": band.reshape(P, TB, G), "keep": keep,
            "before": before, "own": own}


def kernel(**inputs):
    import concourse.bacc as _bacc
    from concourse.bass_utils import run_bass_kernel_spmd as _run

    arrays = {n: np.asarray(inputs[n]) for n in _DIRECT}
    arrays["mask"] = np.asarray(inputs["mask_Bx8xSxS2_bf0"])
    arrays["router_T"] = np.asarray(inputs["L0_ffn_router_w"]).T
    for name in "qk":
        arrays[f"{name}_swapped"] = np.roll(np.asarray(inputs[f"L1_ffn_{name}_scale"]), HD // 2, axis=1)
    arrays["ln_g"] = np.asarray(inputs["L1_ffn_ln_g"]).T
    arrays["ln_b"] = np.asarray(inputs["L1_ffn_ln_b"]).T
    b1 = np.zeros((LAYERS, 2, FC * P), np.float32)
    b1[:, :, 0:FF] = np.asarray(inputs["L1_ffn_b1"]).reshape(LAYERS, 2, FF)
    arrays["b1"] = b1.reshape(LAYERS, 2, FC, P).transpose(3, 0, 1, 2)
    arrays.update(_constants())
    arrays = {n: np.ascontiguousarray(a) for n, a in arrays.items()}

    nc = _bacc.Bacc("TRN2", target_bir_lowering=False, num_devices=1)
    w = {n: nc.dram_tensor(f"in_{n}", a.shape, mybir.dt.from_np(a.dtype), kind="ExternalInput").ap()
         for n, a in arrays.items()}
    out = nc.dram_tensor("out_x", (B, S, D), F32, kind="ExternalOutput").ap()
    program(nc, w, out.rearrange("b (t p) d -> p (b t) d", p=P))
    r = _run(nc, [{f"in_{n}": a for n, a in arrays.items()}], core_ids=[0])
    return r.results[0]["out_x"]
```

```python
from contextlib import ExitStack, contextmanager

import concourse.bass as bass
import numpy as np
from concourse import mybir

F32 = mybir.dt.float32
BF16 = mybir.dt.bfloat16
I32 = mybir.dt.int32
ALU = mybir.AluOpType
ACT = mybir.ActivationFunctionType
AX = mybir.AxisListType.X

P = 128
D = 128
B, S = 2, 512
CTX = 77
TILES = B * S // P
TB = S // P

LAYERS, HEADS, HD, WIN = 6, 16, 64, 32
PAIRS = HEADS // 2
INNER = HEADS * HD
FF = 341
FC = 3
ROWS = [128, 128, FF - 256]
N = LAYERS * TILES
KEYS = 96
ORDER = (0, 2, 1, 3)
GROUPS = 4
G = 4 * KEYS


class Memory:

    def __init__(self, nc, ctx):
        self.nc, self.ctx, self.buffers = nc, ctx, ctx

    @contextmanager
    def stage(self):
        with ExitStack() as self.buffers:
            yield
        self.buffers = self.ctx

    def sbuf(self, name, shape, dtype=F32):
        return self.buffers.enter_context(self.nc.sbuf_tensor(name, shape, dtype))

    def psum(self, name):
        return self.ctx.enter_context(self.nc.psum_tensor(name, [P, 512], F32))

    def sem(self, name):
        return self.ctx.enter_context(self.nc.semaphore(name))

    def block(self):
        self.open_block = self.nc.Block()
        return self.open_block.__enter__()

    def end_block(self):
        self.open_block.__exit__(None, None, None)


def rsqrt_op(dve, k, a, y, t, chain, before):
    dve.wait_ge(chain, before + k)
    if k == 0:
        ins = dve.tensor_scalar(y.bitcast(I32), a.bitcast(I32), -0.5, float(0x5F3759DF), ALU.mult, ALU.add)
    elif k % 3 == 1:
        ins = dve.tensor_tensor(t, y, y, ALU.mult)
    elif k % 3 == 2:
        ins = dve.scalar_tensor_tensor(t, t, -0.5, a, ALU.mult, ALU.mult)
    else:
        ins = dve.scalar_tensor_tensor(y, t, 1.5, y, ALU.add, ALU.mult)
    ins.then_inc(chain, 1)


RS = 10


def at(buf, index):
    return buf[:, bass.ds(index, 1)]


def need(eng, s, value):
    if not (isinstance(value, int) and value <= 0):
        eng.wait_ge(s, value)


def layer_norm(mem, name, x_all, xn, bank, ident, turn):
    stats = mem.sbuf(name + "_stats", [P, TILES, 6])
    mv = mem.sbuf(name + "_mv", [P, TILES, 2])
    var, rstd, tmp = (mem.sbuf(name + s, [P, TILES]) for s in ("_var", "_rstd", "_tmp"))
    stats_done, aggr_done, chain, rows_done = (mem.sem(name + s) for s in ("_stats", "_aggr", "_chain", "_rows"))
    turned, copied = mem.sem(name + "_turned"), mem.sem(name + "_copied")
    block = mem.block()

    @block.vector
    def _(dve):
        for t in range(TILES):
            dve.bn_stats(stats[:, t, :], x_all[:, t, :]).then_inc(stats_done, 1)
        for t in range(TILES):
            dve.wait_ge(stats_done, t + 1)
            dve.bn_aggr(mv[:, t, :], stats[:, t, :]).then_inc(aggr_done, 1)
        dve.wait_ge(aggr_done, TILES)
        dve.tensor_scalar(var[:], mv[:, :, 1], 1e-5, None, ALU.add).then_inc(chain, 1)
        for k in range(RS):
            rsqrt_op(dve, k, var[:], rstd[:], tmp[:], chain, 1)
        dve.wait_ge(chain, 1 + RS)
        for t in range(TILES):
            dve.tensor_scalar(xn[:, t, :], x_all[:, t, :], mv[:, t, 0:1], rstd[:, t:t + 1], ALU.subtract, ALU.mult)\
                .then_inc(rows_done, 1)

    if turn is not None:
        @block.tensor
        def _(pe):
            for t in range(TILES):
                pe.wait_ge(rows_done, t + 1)
                ins = pe.transpose(bank[t // 4][:, P * (t % 4):P * (t % 4) + P], xn[:, t, :], ident[:])
                if t % 4 == 3:
                    ins.then_inc(turned, 1)

        @block.scalar
        def _(act):
            for h in range(2):
                act.wait_ge(turned, h + 1)
                act.copy(turn[:, 4 * h:4 * h + 4, :], bank[h][:].rearrange("p (t n) -> p t n", t=4)).then_inc(copied, 1)

    mem.end_block()


def cross_attention_wide(mem, w, x_all, xnT, bank, ident, gate):
    HEADS, HD, T = 8, 128, CTX
    G = 4 * T
    SCALE = float(1.0 / np.sqrt(np.float32(HD)))
    wq, wk, wv = (mem.sbuf(n, [P, HEADS * HD]) for n in ("s1_wq", "s1_wk", "s1_wv"))
    wfc = mem.sbuf("s1_wfc", [P, HEADS, D])
    kT = mem.sbuf("s1_kT", [P, HEADS, B, T])
    vT = mem.sbuf("s1_vT", [P, HEADS, B, T])
    wqT = mem.sbuf("s1_wqT", [P, HEADS, D])
    to_scores = mem.sbuf("s1_to_scores", [P, B, HEADS, T])
    to_out = mem.sbuf("s1_to_out", [T, B, HEADS, D])
    mask = mem.sbuf("s1_mask", [P, TILES, HEADS * T], mybir.dt.uint8)
    mask_cur = mem.sbuf("s1_mask_cur", [P, HEADS * T], mybir.dt.uint8)
    floor = mem.sbuf("s1_floor", [P, G])
    spare = mem.sbuf("s1_spare", [P, 3])
    x_cur = mem.sbuf("s1_x_cur", [P, 2, P])
    probs = mem.sbuf("s1_probs", [P, 2, 2, G])
    stat = mem.sbuf("s1_stat", [P, 2, 3, HEADS])
    pT = mem.sbuf("s1_pT", [T, HEADS, P])
    SC, TR, OUT = bank[2:4], bank[4:6], bank[6:8]

    loads = mem.loads1
    k_out, v_out, wq_T, m_out, o_out = (mem.sem("s1_" + n) for n in ("k_out", "v_out", "wq_T", "m_out", "o_out"))
    k_copied, v_copied, wq_copied, m_copied, o_copied = (
        mem.sem("s1_" + n) for n in ("k_copied", "v_copied", "wq_copied", "m_copied", "o_copied"))
    floor_set, x_copied, mask_copied = (mem.sem("s1_" + n) for n in ("floor_set", "x_copied", "mask_copied"))
    score_out, prob_T, y_out = mem.sem("s1_score_out"), mem.sem("s1_prob_T"), mem.sem("s1_y_out")
    exp_done, prob_copied, probs_done = mem.sem("s1_exp_done"), mem.sem("s1_prob_copied"), mem.sem("s1_probs_done")
    masked, max_done, shifted, summed, inverted, x_done = (
        mem.sem("s1_" + n) for n in ("masked", "max_done", "shifted", "summed", "inverted", "x_done"))

    def run_steps(engine, step):
        step(0, None, 0)
        step(1, 0, 1)
        step(2, 1, 0)
        with engine.Fori(1, TILES // 2 - 1) as turn:
            step(2 * turn + 1, 2 * turn, 1)
            step(2 * turn + 2, 2 * turn + 1, 0)
        step(TILES - 1, TILES - 2, 1)
        step(None, TILES - 1, 0)

    block = mem.block()

    @block.sync
    def _(sp):
        sp.dma_start(wk[:], w["L0_xattn_W_K"]).then_inc(loads["wk"], 16)
        sp.dma_start(wv[:], w["L0_xattn_W_V"]).then_inc(loads["wv"], 16)
        sp.dma_start(wq[:], w["L0_xattn_W_Q"]).then_inc(loads["wq"], 16)
        sp.dma_start(wfc[:], w["L0_xattn_W_fc"].rearrange("(h p) n -> p h n", p=HD)).then_inc(loads["wfc"], 16)
        for b in range(B):
            for t in range(TB):
                sp.dma_start(mask[:, TB * b + t, :].rearrange("p (h k) -> p h k", k=T),
                             w["mask"][b, :, P * t:P * t + P, :].rearrange("h q k -> q h k")).then_inc(loads["mask"], 16)
        mem.prefetch(sp)

    @block.tensor
    def _(pe):
        ctx_cols = mem.ctxT[:, :, :].rearrange("p b t -> p (b t)")
        half = lambda b, h: b[:, 256 * h:256 * h + B * T]

        def scores(i, par):
            pe.wait_ge(x_copied, i + 1)
            for c in range(2):
                need(pe, shifted, 2 * i + c - 1)
                pe.matmul(SC[c][:, 0:G], x_cur[:, par, :],
                          to_scores[:, bass.ds(i // TB, 1), 4 * c:4 * c + 4, :].rearrange("p b h t -> p (b h t)"),
                          start=True, stop=True).then_inc(score_out, 1)

        def transpose_probs(j, par):
            for c in range(2):
                pe.wait_ge(probs_done, 2 * j + c + 1)
                need(pe, prob_copied, 2 * j + c - 1)
                for h in range(4):
                    ins = pe.transpose(TR[c][0:T, P * h:P * h + P], probs[:, par, c, T * h:T * h + T], ident[:])
                ins.then_inc(prob_T, 1)

        def output(j, par):
            need(pe, x_done, j - 1)
            for h in range(HEADS):
                if h % 4 == 0:
                    pe.wait_ge(prob_copied, 2 * j + h // 4 + 1)
                ins = pe.matmul(OUT[par][:, 0:D], pT[:, h, :], to_out[:, bass.ds(j // TB, 1), h, :],
                                start=(h == 0), stop=(h == HEADS - 1))
            ins.then_inc(y_out, 1)

        pe.wait_ge(loads["wk"], 16)
        for c in range(4):
            for h in range(2):
                head = 2 * c + h
                ins = pe.matmul(half(bank[c], h), wk[:, HD * head:HD * head + HD], ctx_cols, start=True, stop=True)
            ins.then_inc(k_out, 1)
        pe.wait_ge(loads["wv"], 16)
        for c in range(4):
            for h in range(2):
                head = 2 * c + h
                ins = pe.matmul(half(bank[4 + c], h), wv[:, HD * head:HD * head + HD], ctx_cols, start=True, stop=True)
            ins.then_inc(v_out, 1)
        pe.wait_ge(loads["wq"], 16)
        for c in range(2):
            pe.wait_ge(k_copied, c + 1)
            for h in range(4):
                head = 4 * c + h
                ins = pe.transpose(bank[c][:, P * h:P * h + P], wq[:, HD * head:HD * head + HD], ident[:])
            ins.then_inc(wq_T, 1)
        for c in range(4):
            if c < 2:
                pe.wait_ge(k_copied, c + 3)
            else:
                pe.wait_ge(v_copied, c - 1)
            pe.wait_ge(wq_copied, c // 2 + 1)
            pe.wait_ge(k_copied, c + 1)
            for h in range(2):
                head = 2 * c + h
                ins = pe.matmul(half(bank[2 + c], h), wqT[:, head, :], kT[:, head, :, :].rearrange("p b t -> p (b t)"),
                                start=True, stop=True)
            ins.then_inc(m_out, 1)
        pe.wait_ge(loads["wfc"], 16)
        pe.wait_ge(v_copied, 4)
        for k in range(4):
            b, c = k // 2, k % 2
            for h in range(4):
                head = 4 * c + h
                ins = pe.matmul(bank[(6 + k) % 8][0:T, D * h:D * h + D], vT[:, head, b, :], wfc[:, head, :],
                                start=True, stop=True)
            ins.then_inc(o_out, 1)

        def step(i, j, par):
            if i is not None:
                scores(i, par)
            if j is not None:
                transpose_probs(j, 1 - par)
                if isinstance(j, int) and j == 0:
                    pe.wait_ge(o_copied, 4)
                output(j, 1 - par)

        pe.wait_ge(m_copied, 4)
        run_steps(pe, step)

    @block.scalar
    def _(act):
        def exp(i, par):
            for c in range(2):
                act.wait_ge(shifted, 2 * i + c + 1)
                act.activation(probs[:, par, c, :], probs[:, par, c, :], ACT.Exp).then_inc(exp_done, 1)

        def copy_probs(j):
            for c in range(2):
                act.wait_ge(prob_T, 2 * j + c + 1)
                need(act, y_out, j)
                act.copy(pT[:, 4 * c:4 * c + 4, :], TR[c][0:T, :].rearrange("p (h t) -> p h t", h=4))\
                    .then_inc(prob_copied, 1)

        for c in range(4):
            act.wait_ge(k_out, c + 1)
            act.copy(kT[:, 2 * c:2 * c + 2, :, :].rearrange("p h b t -> p h (b t)"),
                     bank[c][:, :].rearrange("p (h n) -> p h n", h=2)[:, :, 0:B * T]).then_inc(k_copied, 1)
        for c in range(2):
            act.wait_ge(wq_T, c + 1)
            act.copy(wqT[:, 4 * c:4 * c + 4, :], bank[c][:].rearrange("p (h n) -> p h n", h=4)).then_inc(wq_copied, 1)
        for k in range(4):
            act.wait_ge(o_out, k + 1)
            act.copy(to_out[:, k // 2, 4 * (k % 2):4 * (k % 2) + 4, :],
                     bank[(6 + k) % 8][0:T, :].rearrange("p (h n) -> p h n", h=4)).then_inc(o_copied, 1)

        def step(i, j, par):
            if j is not None:
                copy_probs(j)
            if i is not None:
                exp(i, par)

        run_steps(act, step)

    @block.vector
    def _(dve):
        rows = lambda ap: ap.rearrange("p (h k) -> p h k", k=T)

        def softmax_front(i, par):
            for c in range(2):
                if c == 0:
                    dve.wait_ge(mask_copied, i + 1)
                    dve.memset(spare[:, 2:3], 0.0)
                dve.wait_ge(score_out, 2 * i + c + 1)
                dve.memset(spare[:, c:c + 1], 0.0)
                dve.wait_ge(floor_set, 1)
                dve.copy_predicated(SC[c][:, 0:G], mask_cur[:, G * c:G * c + G], floor[:]).then_inc(masked, 1)
            for c in range(2):
                dve.wait_ge(masked, 2 * i + c + 1)
                dve.tensor_reduce(stat[:, par, 0, 4 * c:4 * c + 4], rows(SC[c][:, 0:G]), AX, ALU.max)\
                    .then_inc(max_done, 1)
            for c in range(2):
                dve.wait_ge(max_done, 2 * i + c + 1)
                need(dve, prob_T, 2 * i + c - 3)
                m = stat[:, par, 0, 4 * c:4 * c + 4].unsqueeze(2).broadcast_to([P, 4, T])
                dve.tensor_tensor(rows(probs[:, par, c, :]), rows(SC[c][:, 0:G]), m, ALU.subtract).then_inc(shifted, 1)

        def softmax_back(i, par):
            for c in range(2):
                dve.wait_ge(exp_done, 2 * i + c + 1)
                dve.tensor_reduce(stat[:, par, 1, 4 * c:4 * c + 4], rows(probs[:, par, c, :]), AX, ALU.add)\
                    .then_inc(summed, 1)
            dve.wait_ge(summed, 2 * i + 2)
            need(dve, probs_done, 2 * i - 2)
            dve.reciprocal(stat[:, par, 2, :], stat[:, par, 1, :]).then_inc(inverted, 1)

        def add(j, par):
            dve.wait_ge(y_out, j + 1)
            xt = x_all[:, bass.ds(j, 1), :].rearrange("p a d -> p (a d)")
            dve.scalar_tensor_tensor(xt, OUT[par][:, 0:D], gate, xt, ALU.mult, ALU.add).then_inc(x_done, 1)

        dve.memset(floor[:], -1e9).then_inc(floor_set, 1)
        for c in range(4):
            dve.wait_ge(v_out, c + 1)
            dve.tensor_copy(vT[:, 2 * c:2 * c + 2, :, :].rearrange("p h b t -> p h (b t)"),
                            bank[4 + c][:, :].rearrange("p (h n) -> p h n", h=2)[:, :, 0:B * T]).then_inc(v_copied, 1)
        for c in range(4):
            dve.wait_ge(m_out, c + 1)
            for h in range(2):
                ins = dve.tensor_scalar(to_scores[:, :, 2 * c + h, :], bank[2 + c][:, 256 * h:256 * h + B * T]
                                        .rearrange("p (b t) -> p b t", b=B), SCALE, None, ALU.mult)
            ins.then_inc(m_copied, 1)

        def step(i, j, par):
            if i is not None:
                softmax_front(i, par)
                softmax_back(i, par)
            if j is not None:
                add(j, 1 - par)

        run_steps(dve, step)

    @block.gpsimd
    def _(pool):
        def copy_mask(i):
            need(pool, masked, 2 * i)
            pool.tensor_copy(mask_cur[:].bitcast(I32).unsqueeze(1), at(mask[:].bitcast(I32), i)).then_inc(mask_copied, 1)

        def copy_x(i, par):
            need(pool, score_out, 2 * i - 2)
            pool.tensor_copy(x_cur[:, par:par + 1, :], at(xnT, i)).then_inc(x_copied, 1)

        def normalise_probs(i, par):
            pool.wait_ge(inverted, i + 1)
            for c in range(2):
                p = probs[:, par, c, :].rearrange("p (h k) -> p h k", k=T)
                r = stat[:, par, 2, 4 * c:4 * c + 4].unsqueeze(2).broadcast_to([P, 4, T])
                pool.tensor_tensor(p, p, r, ALU.mult).then_inc(probs_done, 1)

        def step(i, j, par):
            if i is not None:
                copy_x(i, par)
                copy_mask(i)
            if j is not None:
                normalise_probs(j, 1 - par)

        pool.wait_ge(loads["mask"], 16 * TILES)
        run_steps(pool, step)

    mem.end_block()


def mixture(mem, w, x_all, xnT, bank, ident, gate):
    E, HS = 8, 2
    N = S
    W = mem.w2s
    hT = mem.sbuf("s2_hT", [P, E, N])
    sT = mem.sbuf("s2_sT", [P, HS, N])
    gT = mem.sbuf("s2_gT", [P, HS, N])
    prob = mem.sbuf("s2_prob", [P, TILES, E])
    sel = mem.sbuf("s2_sel", [P, TILES, E])
    cmp = mem.sbuf("s2_cmp", [P, 2, TILES, E, E])
    rank = mem.sbuf("s2_rank", [P, TILES, E])
    comb = mem.sbuf("s2_comb", [P, TILES, E])
    den = mem.sbuf("s2_den", [P, 3, TILES])
    acc = mem.sbuf("s2_acc", [P, 2, D])
    HB, EO, SO = bank[0:4], bank[4:6], bank[6:8]

    route_out, routed = mem.sem("s2_route_out"), mem.sem("s2_routed")
    chain, comb_done = mem.sem("s2_chain"), mem.sem("s2_comb_done")
    hid_out, read_by_act, silu_done, gated = (mem.sem("s2_" + n) for n in ("hid_out", "read_by_act", "silu_done", "gated"))
    y_out, shared_out, acc_step, x_done = (mem.sem("s2_" + n) for n in ("y_out", "shared_out", "acc_step", "x_done"))
    loads = mem.loads2
    block = mem.block()

    @block.tensor
    def _(pe):
        pe.wait_ge(loads, 16 * 8)
        for t in range(TILES):
            ins = pe.matmul(SO[1][:, E * t:E * t + E], xnT[:, t, :], W["router"][:], start=True, stop=True)
        ins.then_inc(route_out, 1)
        pe.wait_ge(routed, 1)

        def hidden(p):
            x = xnT[:, p * TB:(p + 1) * TB, :]
            for c in range(E):
                if c < 2:
                    need(pe, read_by_act, (E + HS) * p)
                elif c < 4:
                    need(pe, gated, HS * p)
                else:
                    pe.wait_ge(read_by_act, (E + HS) * p + c - 3)
                pe.matmul(HB[c % 4][:], W["ew1"][:, c, :], x, start=True, stop=True).then_inc(hid_out, 1)
            for c in range(HS):
                pe.wait_ge(read_by_act, (E + HS) * p + 5 + c)
                pe.matmul(HB[c][:], W["sw1"][:, P * c:P * c + P], x, start=True, stop=True).then_inc(hid_out, 1)
            for c in range(HS):
                pe.wait_ge(read_by_act, (E + HS) * p + 7 + c)
                pe.matmul(HB[2 + c][:], W["sw3"][:, P * c:P * c + P], x, start=True, stop=True).then_inc(hid_out, 1)

        def outputs(p):
            for t in range(TB):
                pe.wait_ge(read_by_act, (E + HS) * p + E)
                need(pe, x_done, TB * p + t)
                cols = slice(P * t, P * t + P)
                for e in range(E):
                    ins = pe.matmul(EO[e // 4][:, D * (e % 4):D * (e % 4) + D], hT[:, e, cols], W["ew2"][:, e, :],
                                    start=True, stop=True)
                ins.then_inc(y_out, 1)
                pe.wait_ge(gated, HS * (p + 1))
                for c in range(HS):
                    ins = pe.matmul(SO[0][:, 0:D], sT[:, c, cols], W["sw2"][:, c, :], start=(c == 0), stop=(c == HS - 1))
                ins.then_inc(shared_out, 1)

        for p in range(B):
            hidden(p)
            outputs(p)

    @block.scalar
    def _(act):
        act.wait_ge(route_out, 1)
        act.activation(prob[:].rearrange("p t e -> p (t e)"), SO[1][:, 0:TILES * E], ACT.Sigmoid).then_inc(routed, 1)
        for p in range(B):
            for c in range(E):
                act.wait_ge(hid_out, 12 * p + c + 1)
                if c == 0:
                    need(act, y_out, TB * p)
                act.activation(hT[:, c, :], HB[c % 4][:], ACT.Gelu).then_inc(read_by_act, 1)
            for c in range(HS):
                act.wait_ge(hid_out, 12 * p + E + c + 1)
                need(act, gated, HS * p)
                act.activation(gT[:, c, :], HB[c][:], ACT.Silu).then_inc(read_by_act, 1)

    @block.vector
    def _(dve):
        steps = [0]

        def chained(ins):
            ins.then_inc(chain, 1)
            steps[0] += 1
            dve.wait_ge(chain, steps[0])

        wide = [P, TILES, E, E]
        dve.wait_ge(routed, 1)
        dve.wait_ge(loads, 16 * 8)
        bias = W["bias"][:].unsqueeze(1).broadcast_to([P, TILES, E])
        chained(dve.tensor_tensor(sel[:], prob[:], bias, ALU.add))
        other, own = sel[:].unsqueeze(2).broadcast_to(wide), sel[:].unsqueeze(3).broadcast_to(wide)
        for t in range(TILES):
            dve.tensor_tensor(cmp[:, 0, t], other[:, t], own[:, t], ALU.is_gt)
            ins = dve.tensor_tensor(cmp[:, 1, t], other[:, t], own[:, t], ALU.is_equal)
        chained(ins)
        before = W["before"][:].unsqueeze(1).broadcast_to([P, TILES, E * E])
        flat = lambda k: cmp[:, k].rearrange("p t e j -> p t (e j)")
        chained(dve.tensor_tensor(flat(1), flat(1), before, ALU.mult))
        chained(dve.tensor_tensor(flat(0), flat(0), flat(1), ALU.add))
        chained(dve.tensor_reduce(rank[:], cmp[:, 0], AX, ALU.add))
        chained(dve.tensor_scalar(rank[:], rank[:], 2.0, None, ALU.is_lt))
        chained(dve.tensor_tensor(comb[:], prob[:], rank[:], ALU.mult))
        chained(dve.tensor_reduce(den[:, 0, :], comb[:], AX, ALU.add))
        chained(dve.tensor_scalar(den[:, 1, :], den[:, 0, :], 1e-9, None, ALU.add))
        chained(dve.reciprocal(den[:, 1, :], den[:, 1, :]))
        chained(dve.tensor_scalar(den[:, 0, :], den[:, 0, :], 1e-9, None, ALU.is_gt))
        chained(dve.tensor_tensor(den[:, 1, :], den[:, 1, :], den[:, 0, :], ALU.mult))
        chained(dve.tensor_scalar(den[:, 2, :], den[:, 0, :], -0.5, 0.5, ALU.mult, ALU.add))
        spread = lambda k: den[:, k, :].unsqueeze(2).broadcast_to([P, TILES, E])
        chained(dve.tensor_tensor(comb[:], comb[:], spread(1), ALU.mult))
        chained(dve.tensor_tensor(rank[:], rank[:], spread(2), ALU.mult))
        chained(dve.tensor_tensor(comb[:], comb[:], rank[:], ALU.add))

        for p in range(B):
            for c in range(HS):
                dve.wait_ge(hid_out, 12 * p + E + HS + c + 1)
                dve.wait_ge(read_by_act, (E + HS) * p + E + c + 1)
                need(dve, shared_out, TB * p)
                dve.tensor_tensor(sT[:, c, :], HB[2 + c][:], gT[:, c, :], ALU.mult).then_inc(gated, 1)
            for t in range(TB):
                j = p * TB + t
                weight = lambda e: comb[:, bass.ds(j, 1), e:e + 1].rearrange("p a e -> p (a e)")
                dve.wait_ge(y_out, j + 1)
                for e in range(E):
                    a = acc[:, e % 2, :]
                    y = EO[e // 4][:, D * (e % 4):D * (e % 4) + D]
                    if e < 2:
                        ins = dve.tensor_scalar(a, y, weight(e), None, ALU.mult)
                    else:
                        dve.wait_ge(acc_step, 9 * j + e - 1)
                        ins = dve.scalar_tensor_tensor(a, y, weight(e), a, ALU.mult, ALU.add)
                    ins.then_inc(acc_step, 1)
                dve.wait_ge(shared_out, j + 1)
                dve.wait_ge(acc_step, 9 * j + 7)
                dve.tensor_tensor(acc[:, 0, :], SO[0][:, 0:D], acc[:, 0, :], ALU.add).then_inc(acc_step, 1)
                dve.wait_ge(acc_step, 9 * j + 9)
                dve.tensor_tensor(acc[:, 0, :], acc[:, 0, :], acc[:, 1, :], ALU.add).then_inc(silu_done, 1)
                dve.wait_ge(silu_done, j + 1)
                xt = x_all[:, bass.ds(j, 1), :].rearrange("p a d -> p (a d)")
                dve.scalar_tensor_tensor(xt, acc[:, 0, :], gate, xt, ALU.mult, ALU.add).then_inc(x_done, 1)

    mem.end_block()


def cross_attention_narrow(mem, w, x_all, xnT, bank, ident, gate):
    HEADS, HD, T = 16, 8, CTX
    SCALE = float(np.float32(1.0) / np.float32(HD ** -0.5))
    PARTS = [(0, 6), (6, 12), (12, 16)]
    W = mem.w3s
    kd = mem.sbuf("s3_kd", [P, B, HEADS, T])
    kT = mem.sbuf("s3_kT", [P, B, T])
    v = mem.sbuf("s3_v", [T, B, D])
    qT = mem.sbuf("s3_qT", [P, P])
    probs = mem.sbuf("s3_probs", [P, HEADS, T])
    stat = mem.sbuf("s3_stat", [P, 3, HEADS])
    pT = mem.sbuf("s3_pT", [T, HEADS, P])
    o = mem.sbuf("s3_o", [P, D])
    oT = mem.sbuf("s3_oT", [P, P])
    SC, TR, QB, AO, YO = bank[0:3], bank[3:5], bank[5], bank[6], bank[7]
    loads = mem.loads3
    kv_out, k_copied, kv_ready = mem.sem("s3_kv_out"), mem.sem("s3_k_copied"), mem.sem("s3_kv_ready")
    v_copied = mem.sem("s3_v_copied")
    q_out, score_out, prob_T, attn_out, o_T, y_out = (mem.sem("s3_" + n) for n in
                                                      ("q_out", "score_out", "prob_T", "attn_out", "o_T", "y_out"))
    q_copied, exp_done, prob_copied, o_copied = (mem.sem("s3_" + n) for n in
                                                 ("q_copied", "exp_done", "prob_copied", "o_copied"))
    max_done, shifted, summed, inverted, o_done, x_done = (mem.sem("s3_" + n) for n in
                                                           ("max_done", "shifted", "summed", "inverted", "o_done", "x_done"))
    block = mem.block()

    @block.tensor
    def _(pe):
        ctxT = mem.ctxT

        def project_q(j):
            need(pe, q_copied, j)
            pe.matmul(QB[:, 0:P], W["wq"][:], at(xnT, j), start=True, stop=True).then_inc(q_out, 1)

        def scores(j):
            pe.wait_ge(q_copied, j + 1)
            for c, (h0, h1) in enumerate(PARTS):
                need(pe, shifted, 3 * j + c - 2)
                pe.matmul(SC[c][:, 0:T * (h1 - h0)], qT[:],
                          kd[:, bass.ds(j // TB, 1), h0:h1, :].rearrange("p b h t -> p (b h t)"),
                          start=True, stop=True).then_inc(score_out, 1)

        def transpose_probs(j):
            for c in range(4):
                need(pe, exp_done, 3 * j + [1, 2, 2, 3][c])
                need(pe, prob_copied, 4 * j + max(c - 1, 0))
                for h in range(4):
                    ins = pe.transpose(TR[c % 2][0:T, P * h:P * h + P], probs[:, 4 * c + h, :], ident[:])
                ins.then_inc(prob_T, 1)

        def attend(j):
            need(pe, o_done, j)
            for c in range(4):
                pe.wait_ge(prob_copied, 4 * j + c + 1)
                for h in range(4 * c, 4 * c + 4):
                    ins = pe.matmul(AO[:, HD * h:HD * h + HD], pT[:, h, :], v[:, bass.ds(j // TB, 1), HD * h:HD * h + HD]
                                    .rearrange("p b n -> p (b n)"), start=True, stop=True)
            ins.then_inc(attn_out, 1)

        def project_out(j):
            pe.wait_ge(o_done, j + 1)
            need(pe, x_done, j)
            pe.transpose(YO[:, 0:P], o[:], ident[:]).then_inc(o_T, 1)
            pe.wait_ge(o_copied, j + 1)
            pe.matmul(YO[:, P:2 * P], oT[:], W["wproj"][:], start=True, stop=True).then_inc(y_out, 1)

        pe.wait_ge(loads, 16 * 4)
        pe.matmul(QB[:, 0:B * T], W["wkv"][:, 0:D], ctxT[:, :, :].rearrange("p b t -> p (b t)"), start=True, stop=True)\
            .then_inc(kv_out, 1)
        for b in range(B):
            pe.matmul(YO[0:T, D * b:D * b + D], ctxT[:, b, :], W["wkv"][:, D:2 * D], start=True, stop=True)\
                .then_inc(kv_out, 1)
        pe.wait_ge(v_copied, 2)
        def step(j, more=True):
            transpose_probs(j)
            scores(j + 1)
            attend(j)
            if more:
                project_q(j + 2)
            project_out(j)

        project_q(0)
        pe.wait_ge(kv_ready, B)
        scores(0)
        project_q(1)
        step(0)
        with pe.Fori(1, TILES - 2) as j:
            step(j)
        step(TILES - 2, more=False)
        transpose_probs(TILES - 1)
        attend(TILES - 1)
        project_out(TILES - 1)

    @block.scalar
    def _(act):
        def copy_q(j):
            act.wait_ge(q_out, j + 1)
            need(act, score_out, 3 * j)
            act.activation(qT[:], QB[:, 0:P], ACT.Copy, scale=SCALE).then_inc(q_copied, 1)

        def exp(j):
            for c, (h0, h1) in enumerate(PARTS):
                act.wait_ge(shifted, 3 * j + c + 1)
                act.activation(probs[:, h0:h1, :], probs[:, h0:h1, :], ACT.Exp).then_inc(exp_done, 1)

        def copy_probs(j):
            for c in range(4):
                act.wait_ge(prob_T, 4 * j + c + 1)
                if c == 0:
                    need(act, attn_out, j)
                act.copy(pT[:, 4 * c:4 * c + 4, :], TR[c % 2][0:T, :].rearrange("p (h t) -> p h t", h=4))\
                    .then_inc(prob_copied, 1)

        def copy_o(j):
            act.wait_ge(o_T, j + 1)
            need(act, y_out, j)
            act.copy(oT[:], YO[:, 0:P]).then_inc(o_copied, 1)

        act.wait_ge(kv_out, 1)
        act.copy(kT[:].rearrange("p b t -> p (b t)"), QB[:, 0:B * T]).then_inc(k_copied, 1)
        act.wait_ge(kv_out, 3)
        act.copy(v[:].rearrange("p b n -> p (b n)"), YO[0:T, 0:B * D]).then_inc(v_copied, 2)
        def step(j, more=True):
            copy_probs(j)
            exp(j + 1)
            if more:
                copy_q(j + 2)
            copy_o(j)

        copy_q(0)
        exp(0)
        copy_q(1)
        step(0)
        with act.Fori(1, TILES - 2) as j:
            step(j)
        step(TILES - 2, more=False)
        copy_probs(TILES - 1)
        copy_o(TILES - 1)

    @block.vector
    def _(dve):
        def softmax_front(j):
            for c, (h0, h1) in enumerate(PARTS):
                sc = SC[c][:, 0:T * (h1 - h0)].rearrange("p (h k) -> p h k", k=T)
                dve.wait_ge(score_out, 3 * j + c + 1)
                dve.tensor_reduce(stat[:, 0, h0:h1], sc, AX, ALU.max).then_inc(max_done, 1)
            for c, (h0, h1) in enumerate(PARTS):
                sc = SC[c][:, 0:T * (h1 - h0)].rearrange("p (h k) -> p h k", k=T)
                dve.wait_ge(max_done, 3 * j + c + 1)
                need(dve, prob_T, 4 * j)
                dve.tensor_tensor(probs[:, h0:h1, :], sc, stat[:, 0, h0:h1].unsqueeze(2).broadcast_to([P, h1 - h0, T]),
                                  ALU.subtract).then_inc(shifted, 1)

        def softmax_back(j):
            dve.wait_ge(exp_done, 3 * j + 3)
            dve.tensor_reduce(stat[:, 1, :], probs[:], AX, ALU.add).then_inc(summed, 1)
            dve.wait_ge(summed, j + 1)
            dve.reciprocal(stat[:, 2, :], stat[:, 1, :]).then_inc(inverted, 1)

        def normalise(j):
            dve.wait_ge(attn_out, j + 1)
            dve.wait_ge(inverted, j + 1)
            need(dve, o_T, j)
            dve.tensor_tensor(o[:].rearrange("p (h d) -> p h d", d=HD), AO[:, 0:D].rearrange("p (h d) -> p h d", d=HD),
                              stat[:, 2, :].unsqueeze(2).broadcast_to([P, HEADS, HD]), ALU.mult).then_inc(o_done, 1)

        def add(j):
            dve.wait_ge(y_out, j + 1)
            xt = x_all[:, bass.ds(j, 1), :].rearrange("p a d -> p (a d)")
            dve.scalar_tensor_tensor(xt, YO[:, P:2 * P], gate, xt, ALU.mult, ALU.add).then_inc(x_done, 1)

        dve.wait_ge(k_copied, 1)
        dve.wait_ge(loads, 16 * 4)
        for b in range(B):
            dve.tensor_tensor(kd[:, b], kT[:, b, :].unsqueeze(1).broadcast_to([P, HEADS, T]),
                              W["own"][:].unsqueeze(2).broadcast_to([P, HEADS, T]), ALU.mult).then_inc(kv_ready, 1)
        def step(j):
            softmax_front(j + 1)
            normalise(j)
            softmax_back(j + 1)
            add(j)

        softmax_front(0)
        softmax_back(0)
        step(0)
        with dve.Fori(1, TILES - 1) as j:
            step(j)
        normalise(TILES - 1)
        add(TILES - 1)

    mem.end_block()


class Weights:
    pass


def local_weights(mem):
    lw = Weights()
    lw.wqkv = mem.sbuf("wqkv", [P, 2, 3 * INNER])
    lw.wo = mem.sbuf("wo", [P, LAYERS, PAIRS, D])
    lw.w1 = mem.sbuf("w1", [P, 2 * FF])
    lw.w2 = mem.sbuf("w2", [P, LAYERS, FC, D])
    lw.qk_scale = mem.sbuf("qk_scale", [P, LAYERS, 2, HD])
    lw.qk_swapped = mem.sbuf("qk_swapped", [P, LAYERS, 2, HD])
    lw.ln_scale = mem.sbuf("ln_scale", [P, LAYERS])
    lw.ln_shift = mem.sbuf("ln_shift", [P, LAYERS])
    lw.bias1 = mem.sbuf("bias1", [P, LAYERS, 2, FC])
    lw.bias2 = mem.sbuf("bias2", [P, LAYERS, D])
    lw.cos_t = mem.sbuf("cos_t", [P, TB, 2, HD])
    lw.sin_t = mem.sbuf("sin_t", [P, TB, 2, HD])
    lw.band = mem.sbuf("band", [P, TB, G])
    lw.keep = mem.sbuf("keep", [P, TB])
    lw.small_loaded, lw.wqkv_loaded, lw.w1_loaded, lw.wo_loaded, lw.w2_loaded = (
        mem.sem(n) for n in ("small_loaded", "wqkv_loaded", "w1_loaded", "wo_loaded", "w2_loaded"))
    return lw


N_SMALL = 12


def load_local_weights(sp, w, lw):
    small = [
        (lw.qk_scale[:, :, 0, :], w["L1_ffn_q_scale"].partition_broadcast(P)),
        (lw.qk_scale[:, :, 1, :], w["L1_ffn_k_scale"].partition_broadcast(P)),
        (lw.qk_swapped[:, :, 0, :], w["q_swapped"].partition_broadcast(P)),
        (lw.qk_swapped[:, :, 1, :], w["k_swapped"].partition_broadcast(P)),
        (lw.cos_t[:], w["cos"]), (lw.sin_t[:], w["sin"]), (lw.band[:], w["band"]), (lw.keep[:], w["keep"]),
        (lw.ln_scale[:], w["ln_g"]), (lw.ln_shift[:], w["ln_b"]), (lw.bias1[:], w["b1"]),
        (lw.bias2[:], w["L1_ffn_b2"].partition_broadcast(P)),
    ]
    for dst, src in small:
        sp.dma_start(dst, src).then_inc(lw.small_loaded, 16)
    assert len(small) == N_SMALL
    sp.dma_start(lw.wqkv[:, 0, :], w["L1_ffn_Wqkv"][0]).then_inc(lw.wqkv_loaded, 16)
    sp.dma_start(lw.w1[:], w["L1_ffn_W1"][0]).then_inc(lw.w1_loaded, 16)
    sp.dma_start(lw.wo[:], w["L1_ffn_Wo"].rearrange("l (k p) n -> p l k n", p=P)).then_inc(lw.wo_loaded, 16)
    for c in range(FC):
        sp.dma_start(lw.w2[0:ROWS[c], :, c, :], w["L1_ffn_W2"][:, 128 * c:128 * c + ROWS[c], :]
                     .rearrange("l p n -> p l n")).then_inc(lw.w2_loaded, 16)
    sp.wait_ge(lw.wqkv_loaded, 16)
    sp.dma_start(lw.wqkv[:, 1, :], w["L1_ffn_Wqkv"][1]).then_inc(lw.wqkv_loaded, 16)


def local_stage(mem, w, lw, x_all, x_in, ident, ident16, bank, gate, out):
    sbuf, sem = mem.sbuf, mem.sem
    wqkv, wo, w1, w2 = lw.wqkv, lw.wo, lw.w1, lw.w2
    ln_scale, ln_shift, bias1, bias2 = lw.ln_scale, lw.ln_shift, lw.bias1, lw.bias2
    qk_scale, qk_swapped, cos_t, sin_t, band, keep = lw.qk_scale, lw.qk_swapped, lw.cos_t, lw.sin_t, lw.band, lw.keep
    band16 = sbuf("band16", [P, TB, G], BF16)
    small_loaded, wqkv_loaded, w1_loaded, wo_loaded, w2_loaded = (
        lw.small_loaded, lw.wqkv_loaded, lw.w1_loaded, lw.wo_loaded, lw.w2_loaded)

    half_rows = slice(P // 2, P)

    x_cur = sbuf("x_cur", [P, D])
    xs = sbuf("xs", [P, P + 1])
    ms = sbuf("ms", [P, P + 1])
    squares = sbuf("squares", [P, 2 * INNER])
    kept = sbuf("kept", [P, 2 * INNER])
    turned = sbuf("turned", [P, 2 * INNER])
    heads = sbuf("heads", [P, 2 * INNER])
    cos_l = sbuf("cos_l", [P, 2, HD])
    sin_l = sbuf("sin_l", [P, 2, HD])
    nf = sbuf("nf", [P, 4, 2 * HEADS])
    qT = sbuf("qT", [P, PAIRS, P])
    kT = sbuf("kT", [P, PAIRS, WIN + P])
    v_raw = sbuf("v_raw", [P, 2, INNER])
    v_win = sbuf("v_win", [KEYS, 2, INNER])
    probs = sbuf("probs", [P, GROUPS, G])
    neg_max = sbuf("neg_max", [P, 4 * GROUPS])
    q_factor = sbuf("q_factor", [P, PAIRS, 2])
    exp_bias = sbuf("exp_bias", [P, 4 * GROUPS])
    rowsum = sbuf("rowsum", [P, 4 * GROUPS])
    rowinv = sbuf("rowinv", [P, 4 * GROUPS])
    pT = sbuf("pT", [KEYS, GROUPS, 512])
    aT = sbuf("aT", [P, PAIRS, P])
    mid = sbuf("mid", [P, D])
    midb = sbuf("midb", [P, D])
    st = sbuf("st", [P, 6])
    mv = sbuf("mv", [P, 2])
    spare = sbuf("spare", [P, 1])
    first_use = sbuf("first_use", [P, 2])
    lnr = sbuf("lnr", [P, 3])
    xn = sbuf("xn", [P, D])
    xnT = sbuf("xnT", [P, P])
    gel = sbuf("gel", [P, FC, P])
    hT = sbuf("hT", [P, FC, P])

    QK, SC, TR, MX = bank[0:2], bank[2:4], bank[4:6], bank[6:8]

    setup_done, band_ready, kept_zero = sem("setup_done"), sem("band_ready"), sem("kept_zero")
    x_T, qk_out, v_out = sem("x_T"), sem("qk_out"), sem("v_out")
    head_T, score_out, prob_T, attn_T, attn_out = (sem("head_T"), sem("score_out"), sem("prob_T"),
                                                   sem("attn_T"), sem("attn_out"))
    mid_T, mid_back, xn_T, gate_out, up_out, ffn_out = (sem("mid_T"), sem("mid_back"), sem("xn_T"),
                                                        sem("gate_out"), sem("up_out"), sem("ffn_out"))
    squared, v_copied, head_copied, exp_done, prob_copied, attn_copied = (
        sem("squared"), sem("v_copied"), sem("head_copied"), sem("exp_done"), sem("prob_copied"),
        sem("attn_copied"))
    xn_copied, gelu_done = sem("xn_copied"), sem("gelu_done")
    x_shifted, rotated, squares_summed, normed = (sem("x_shifted"), sem("rotated"), sem("squares_summed"),
                                                  sem("normed"))
    normed_late = sem("normed_late")
    factors_placed = sem("factors_placed")
    keys_kept, biased, inverted, mid_done = (sem("keys_kept"), sem("biased"), sem("inverted"),
                                              sem("mid_done"))
    mid_shifted, xn_done, hidden_done, x_done = (sem("mid_shifted"), sem("xn_done"), sem("hidden_done"),
                                                 sem("x_done"))
    nf_step, ln_step, max_step, sum_step = sem("nf_step"), sem("ln_step"), sem("max_step"), sem("sum_step")
    xs_step, ms_step = sem("xs_step"), sem("ms_step")
    NF, LN = 4 + RS, 3 + RS
    x_loaded, tables_done, joined, probs_done, midb_done = (sem("x_loaded"), sem("tables_done"), sem("joined"),
                                                            sem("probs_done"), sem("midb_done"))
    v_placed, stored = sem("v_placed"), sem("stored")
    final_done = sem("final_done")

    def tiles_of(s, at_edge):
        return [t if not at_edge or 0 <= t < N else None for t in (s, s + 1, s + 2, s - 1, s - 2)]

    block = mem.block()

    @block.sync
    def _(sp):
        def place_values(n):
            sp.wait_ge(v_copied, 2 * n + 2)
            need(sp, attn_T, 2 * n)
            cur = v_raw[:, bass.ds(n % 2, 1), :] if not isinstance(n, int) else v_raw[:, n % 2:n % 2 + 1, :]
            prev = v_raw[:, bass.ds((n + 1) % 2, 1), :] if not isinstance(n, int) else v_raw[:, (n + 1) % 2:(n + 1) % 2 + 1, :]
            sp.dma_start(v_win[WIN:KEYS, 0:1, :], cur[0:KEYS - WIN]).then_inc(v_placed, 16)
            sp.dma_start(v_win[0:KEYS, 1:2, :], cur[P - KEYS:P]).then_inc(v_placed, 16)
            sp.dma_start(v_win[0:WIN, 0:1, :], prev[P - WIN:P]).then_inc(v_placed, 16)

        sp.wait_ge(kept_zero, 1)
        place_values(0)
        place_values(1)
        with sp.Fori(2, TILES + 1) as n:
            place_values(n)
        with sp.Fori(1, LAYERS - 1) as layer:
            place_values(layer * TILES + 1)
            sp.wait_ge(v_out, 2 * TILES * layer)
            sp.dma_start(wqkv[:, bass.ds((layer + 1) % 2, 1), :],
                         w["L1_ffn_Wqkv"][bass.ds(layer + 1, 1)].rearrange("l p n -> p l n")).then_inc(wqkv_loaded, 16)
            sp.wait_ge(up_out, layer * TILES)
            sp.dma_start(w1[:], w["L1_ffn_W1"][bass.ds(layer, 1)].rearrange("l p n -> (l p) n")).then_inc(w1_loaded, 16)
            with sp.Fori(2, TILES + 1) as t:
                place_values(layer * TILES + t)
        last = (LAYERS - 1) * TILES
        place_values(last + 1)
        sp.wait_ge(up_out, last)
        sp.dma_start(w1[:], w["L1_ffn_W1"][LAYERS - 1]).then_inc(w1_loaded, 16)
        with sp.Fori(2, TILES) as t:
            place_values(last + t)
        sp.wait_ge(final_done, 1)
        sp.dma_start(out, x_in[:]).then_inc(stored, 16)
        sp.wait_ge(stored, 16)

    @block.tensor
    def _(pe):
        def transpose_x(n):
            pe.wait_ge(x_loaded, n + 1)
            need(pe, v_copied, 2 * n - 1)
            pe.transpose(QK[0][:, 0:P], x_cur[:], ident[:]).then_inc(x_T, 1)

        def project_qk(n, c):
            pe.wait_ge(x_shifted, n + 1)
            if c == 1:
                need(pe, v_copied, 2 * n)
            elif c > 1:
                pe.wait_ge(rotated, 4 * n + c - 1)
            layer = n // TILES
            if c == 0:
                pe.wait_ge(wqkv_loaded, 16 * (layer + 1))
            pe.matmul(QK[c % 2][:], xs[:, 0:P], wqkv[:, bass.ds(layer % 2, 1), 512 * c:512 * c + 512],
                      start=True, stop=True).then_inc(qk_out, 1)

        def project_v(n, c):
            pe.wait_ge(rotated, 4 * n + c + 3)
            layer = n // TILES
            pe.matmul(QK[c][:], xs[:, 0:P], wqkv[:, bass.ds(layer % 2, 1), 2 * INNER + 512 * c:2 * INNER + 512 * c + 512],
                      start=True, stop=True).then_inc(v_out, 1)

        def transpose_heads(i, k):
            if k % 2 == 0:
                pe.wait_ge(joined, 4 * i + ORDER[k] + 1)
            else:
                pe.wait_ge(normed if k == 1 else normed_late, i + 1)
            if k < 2:
                need(pe, prob_copied, 4 * i - 1 + k)
            else:
                pe.wait_ge(head_copied, 4 * i + k - 1)
            for p in range(4):
                col = 512 * ORDER[k] + 128 * p
                ins = pe.transpose(TR[k % 2][:, 128 * p:128 * p + 128], heads[:, col:col + 128], ident[:])
            ins.then_inc(head_T, 1)

        def scores(i, g):
            if g < 2:
                pe.wait_ge(head_copied, 4 * i + 2)
                need(pe, attn_copied, 2 * i - 1 + g)
            else:
                pe.wait_ge(head_copied, 4 * i + 4)
                pe.wait_ge(exp_done, 4 * i + g - 1)
            bank = SC[g % 2]
            pe.matmul(bank[:, 0:G], ident16[:], band16[:, bass.ds(i % TB, 1), :], start=True, stop=False,
                      skip_group_check=True)
            for pp in range(2):
                for half in range(2):
                    col = (2 * pp + half) * KEYS
                    for h in range(2):
                        rows = slice(HD * h, HD * h + HD)
                        ins = pe.matmul(bank[rows, col:col + KEYS], qT[rows, 2 * g + pp, 64 * half:64 * half + 64],
                                        kT[rows, 2 * g + pp, 64 * half:64 * half + KEYS],
                                        start=False, stop=True, skip_group_check=True)
            ins.then_inc(score_out, 1)

        def transpose_probs(i, g):
            pe.wait_ge(probs_done, 4 * i + g + 1)
            if g < 2:
                pe.wait_ge(head_copied, 4 * i + 3 + g)
            else:
                pe.wait_ge(prob_copied, 4 * i + g - 1)
            for u in range(4):
                ins = pe.transpose(TR[g % 2][0:KEYS, 128 * u:128 * u + 128],
                                   probs[:, g, KEYS * u:KEYS * u + KEYS], ident[:])
            ins.then_inc(prob_T, 1)

        def attend(i, o):
            pe.wait_ge(prob_copied, 4 * i + 2 * o + 2)
            pe.wait_ge(exp_done, 4 * i + 3 + o)
            if o == 0:
                pe.wait_ge(v_placed, 48 * (i + 1))
            for g in (2 * o, 2 * o + 1):
                for pp in range(2):
                    for half in range(2):
                        u = 2 * pp + half
                        col = (2 * (g % 2) + pp) * P + 64 * half
                        for h in range(2):
                            head = 2 * (2 * g + pp) + h
                            ins = pe.matmul(SC[o][HD * h:HD * h + HD, col:col + 64],
                                            v_win[:, half, HD * head:HD * head + HD],
                                            pT[:, g, 128 * u + 64 * h:128 * u + 64 * h + 64],
                                            start=True, stop=True, skip_group_check=True)
            ins.then_inc(attn_T, 1)

        def project_out(j):
            pe.wait_ge(attn_copied, 2 * j + 2)
            need(pe, gelu_done, j)
            layer = j // TILES
            for k in range(PAIRS):
                ins = pe.matmul(MX[1][:, 0:D], aT[:, k, :], wo[:, bass.ds(layer, 1), k, :],
                                start=(k == 0), stop=(k == PAIRS - 1))
            ins.then_inc(attn_out, 1)

        def transpose_mid(m):
            pe.wait_ge(mid_done, m + 1)
            need(pe, hidden_done, m)
            pe.transpose(MX[0][:, 0:P], mid[:], ident[:]).then_inc(mid_T, 1)

        def transpose_back(m):
            pe.wait_ge(mid_shifted, m + 1)
            pe.transpose(MX[0][:, 0:P], ms[:, 0:P], ident[:]).then_inc(mid_back, 1)

        def transpose_normed(m):
            pe.wait_ge(xn_done, m + 1)
            pe.transpose(MX[0][:, 0:P], xn[:], ident[:]).then_inc(xn_T, 1)

        def gate(m):
            pe.wait_ge(xn_copied, m + 1)
            pe.wait_ge(w1_loaded, 16 * (m // TILES + 1))
            pe.wait_ge(mid_done, m + 1)
            need(pe, x_done, m)
            for c in range(FC):
                ins = pe.matmul(MX[1][0:ROWS[c], 128 * c:128 * c + 128], w1[:, FF + 128 * c:FF + 128 * c + ROWS[c]],
                                xnT[:], start=True, stop=True)
            ins.then_inc(gate_out, 1)

        def up(m):
            for c in range(FC):
                ins = pe.matmul(MX[0][0:ROWS[c], 128 * c:128 * c + 128], w1[:, 128 * c:128 * c + ROWS[c]],
                                xnT[:], start=True, stop=True)
            ins.then_inc(up_out, 1)

        def down(m, j):
            pe.wait_ge(hidden_done, m + 1)
            if j is not None:
                pe.wait_ge(mid_done, j + 1)
            layer = m // TILES
            for c in range(FC):
                ins = pe.matmul(MX[1][:, 0:D], hT[0:ROWS[c], c, :], w2[0:ROWS[c], bass.ds(layer, 1), c, :],
                                start=(c == 0), stop=(c == FC - 1))
            ins.then_inc(ffn_out, 1)

        def step(s, at_edge=False):
            i, n, x2, j, m = tiles_of(s, at_edge)
            if j is not None:
                transpose_probs(j, 0)
                transpose_probs(j, 1)
            if n is not None:
                project_qk(n, 0)
                project_qk(n, 1)
            if j is not None:
                transpose_probs(j, 2)
                transpose_probs(j, 3)
                attend(j, 0)
            if i is not None:
                transpose_heads(i, 0)
                transpose_heads(i, 1)
            if j is not None:
                attend(j, 1)
            if i is not None:
                transpose_heads(i, 2)
                transpose_heads(i, 3)
            if m is not None:
                transpose_normed(m)
            if n is not None:
                project_qk(n, 2)
            if m is not None:
                gate(m)
                up(m)
            if n is not None:
                project_qk(n, 3)
            if i is not None:
                scores(i, 0)
                scores(i, 1)
            if j is not None:
                project_out(j)
            if i is not None:
                scores(i, 2)
                scores(i, 3)
            if n is not None:
                project_v(n, 0)
            if j is not None:
                transpose_mid(j)
            if n is not None:
                project_v(n, 1)
            if x2 is not None:
                transpose_x(x2)
            if m is not None:
                down(m, j)
            if j is not None:
                transpose_back(j)

        transpose_x(0)
        for c in range(4):
            project_qk(0, c)
        project_v(0, 0)
        project_v(0, 1)
        transpose_x(1)
        pe.wait_ge(wo_loaded, 16)
        pe.wait_ge(w2_loaded, 16 * FC)
        pe.wait_ge(band_ready, 1)
        for s in range(3):
            step(s, at_edge=True)
        with pe.Fori(3, N - 2) as s:
            step(s)
        for s in range(N - 2, N + 2):
            step(s, at_edge=True)

    @block.scalar
    def _(act):
        def copy_head(i, k):
            act.wait_ge(head_T, 4 * i + k + 1)
            if k == 0:
                need(act, score_out, 4 * i)
            if k == 1:
                act.wait_ge(keys_kept, i + 1)
            c = ORDER[k]
            src = TR[k % 2][:, :].rearrange("p (k t) -> p k t", k=4)
            k0 = 4 * (c % 2)
            dst = qT[:, k0:k0 + 4, :] if c < 2 else kT[:, k0:k0 + 4, WIN:WIN + P]
            act.copy(dst, src).then_inc(head_copied, 1)

        def shift_x(n):
            act.wait_ge(x_T, n + 1)
            need(act, v_out, 2 * n)
            need(act, x_shifted, n)
            act.activation(xs[half_rows, 0:1], xs[half_rows, P:P + 1], ACT.Copy,
                           scale=keep[half_rows, bass.ds(n % TB, 1)]).then_inc(xs_step, 1)
            act.copy(xs[0:P // 2, 0:P], QK[0][0:P // 2, 0:P])
            act.wait_ge(xs_step, n + 1)
            act.copy(xs[half_rows, 1:P + 1], QK[0][half_rows, 0:P]).then_inc(x_shifted, 1)

        def square(n, c):
            act.wait_ge(qk_out, 4 * n + c + 1)
            if c == 0:
                need(act, squares_summed, n)
            act.activation(squares[:, 512 * c:512 * c + 512], QK[c % 2][:], ACT.Square).then_inc(squared, 1)

        def exp(i, g):
            act.wait_ge(biased, 4 * i + g + 1)
            need(act, prob_T, 4 * i + g - 3)
            for u in range(4):
                pair, half = 2 * g + u // 2, u % 2
                ins = act.activation(probs[:, g, KEYS * u:KEYS * u + KEYS], SC[g % 2][:, KEYS * u:KEYS * u + KEYS],
                                     ACT.Exp, scale=q_factor[:, pair, half:half + 1],
                                     bias=exp_bias[:, 4 * g + u:4 * g + u + 1])
            ins.then_inc(exp_done, 1)

        def copy_values(n, c):
            act.wait_ge(v_out, 2 * n + c + 1)
            if c == 0:
                need(act, v_placed, 48 * n)
            par = n % 2
            dst = v_raw[:, bass.ds(par, 1), 512 * c:512 * c + 512]
            act.copy(dst, QK[c][:].unsqueeze(1)).then_inc(v_copied, 1)

        def copy_probs(i, g):
            act.wait_ge(prob_T, 4 * i + g + 1)
            if g == 0:
                need(act, attn_T, 2 * i)
            act.copy(pT[:, g, :], TR[g % 2][0:KEYS, :]).then_inc(prob_copied, 1)

        def copy_attn(i, o):
            act.wait_ge(attn_T, 2 * i + o + 1)
            if o == 0:
                need(act, attn_out, i)
            act.copy(aT[:, 4 * o:4 * o + 4, :], SC[o][:].rearrange("p (k t) -> p k t", k=4)).then_inc(attn_copied, 1)

        def copy_normed(m):
            act.wait_ge(xn_T, m + 1)
            need(act, up_out, m)
            layer = m // TILES
            act.activation(xnT[:], MX[0][:, 0:P], ACT.Identity, scale=at(ln_scale, layer),
                           bias=at(ln_shift, layer)).then_inc(xn_copied, 1)

        def load_table(func, k):
            act.activation(first_use[:, k:k + 1], keep[:, 0:1], func)

        def gelu(m):
            act.wait_ge(gate_out, m + 1)
            need(act, hidden_done, m)
            layer = m // TILES
            for c in range(FC):
                ins = act.activation(gel[0:ROWS[c], c, :], MX[1][0:ROWS[c], 128 * c:128 * c + 128], ACT.Gelu,
                                     bias=bias1[0:ROWS[c], bass.ds(layer, 1), 1, c:c + 1].rearrange("p l c -> p (l c)"))
            ins.then_inc(gelu_done, 1)

        def step(s, at_edge=False):
            i, n, x2, j, m = tiles_of(s, at_edge)
            if j is not None:
                copy_probs(j, 0)
                copy_probs(j, 1)
            if n is not None:
                square(n, 0)
                square(n, 1)
            if j is not None:
                copy_probs(j, 2)
                copy_probs(j, 3)
                copy_attn(j, 0)
            if i is not None:
                copy_head(i, 0)
                copy_head(i, 1)
            if j is not None:
                copy_attn(j, 1)
            if i is not None:
                copy_head(i, 2)
            if m is not None:
                copy_normed(m)
            if i is not None:
                copy_head(i, 3)
            if n is not None:
                square(n, 2)
            if m is not None:
                gelu(m)
            if n is not None:
                square(n, 3)
            if i is not None:
                load_table(ACT.Exp, 0)
                exp(i, 0)
                exp(i, 1)
            if i is not None:
                exp(i, 2)
            if n is not None:
                copy_values(n, 0)
            if i is not None:
                exp(i, 3)
            if n is not None:
                copy_values(n, 1)
            if x2 is not None:
                shift_x(x2)
            if j is not None:
                load_table(ACT.Gelu, 1)

        act.wait_ge(small_loaded, 16 * N_SMALL)
        act.wait_ge(kept_zero, 1)
        act.wait_ge(setup_done, 3)
        shift_x(0)
        for c in range(4):
            square(0, c)
        copy_values(0, 0)
        copy_values(0, 1)
        shift_x(1)
        for s in range(3):
            step(s, at_edge=True)
        with act.Fori(3, N - 2) as s:
            step(s)
        for s in range(N - 2, N + 2):
            step(s, at_edge=True)

    @block.vector
    def _(dve):
        def shift_mid(m):
            dve.wait_ge(mid_T, m + 1)
            need(dve, mid_back, m)
            need(dve, mid_shifted, m)
            dve.tensor_scalar(ms[half_rows, 0:1], ms[half_rows, P:P + 1],
                              keep[half_rows, bass.ds(m % TB, 1)], None, ALU.mult).then_inc(ms_step, 1)
            dve.tensor_copy(ms[0:P // 2, 0:P], MX[0][0:P // 2, 0:P])
            dve.wait_ge(ms_step, m + 1)
            dve.tensor_copy(ms[half_rows, 1:P + 1], MX[0][half_rows, 0:P]).then_inc(mid_shifted, 1)

        def by_head(ap):
            return ap.rearrange("p (h d) -> p h d", d=HD)

        def rotate_cos(n, c):
            dve.wait_ge(squared, 4 * n + c + 1)
            dve.wait_ge(tables_done, 2 * n + 2)
            need(dve, joined, 4 * n + c - 3)
            table = cos_l[:, c // 2, :].unsqueeze(1).broadcast_to([P, 8, HD])
            dve.tensor_tensor(by_head(kept[:, 512 * c:512 * c + 512]), by_head(QK[c % 2][:]), table, ALU.mult)

        def rotate_sin(n, c):
            need(dve, joined, 4 * n + c - 3)
            halves = lambda ap: ap.rearrange("p (h two d) -> p h two d", two=2, d=HD // 2)
            table = sin_l[:, c // 2, :].rearrange("p (two d) -> p two d", two=2).unsqueeze(1).broadcast_to(
                [P, 8, 2, HD // 2])
            dve.tensor_tensor(halves(turned[:, 512 * c:512 * c + 512]), halves(QK[c % 2][:])[:, :, ::-1, :], table,
                              ALU.mult).then_inc(rotated, 1)

        def sum_squares(n, c):
            dve.wait_ge(squared, 4 * n + c + 1)
            ins = dve.tensor_reduce(nf[:, 0, 8 * c:8 * c + 8], by_head(squares[:, 512 * c:512 * c + 512]), AX, ALU.add)
            ins.then_inc(nf_step, 1)
            if c == 3:
                dve.wait_ge(nf_step, NF * n + 4)
                dve.tensor_scalar(nf[:, 1, :], nf[:, 0, :], 1e-24, None, ALU.max).then_inc(squares_summed, 1)

        def norm_factor(n, k):
            if k == 0:
                dve.wait_ge(squares_summed, n + 1)
            rsqrt_op(dve, k, nf[:, 1, :], nf[:, 2, :], nf[:, 3, :], nf_step, NF * n + 4)

        def place_factors(i):
            dve.wait_ge(nf_step, NF * (i + 1))
            need(dve, exp_done, 4 * i)
            for h in range(2):
                for half in range(2):
                    src = nf[HD * half:HD * half + HD, 2, 0:HEADS].rearrange("p (a two) -> p a two", two=2)[:, :, h]
                    ins = dve.tensor_copy(q_factor[HD * h:HD * h + HD, :, half], src)
            ins.then_inc(factors_placed, 1)

        def normalise(n):
            dve.wait_ge(joined, 4 * n + 3)
            dve.wait_ge(nf_step, NF * (n + 1))
            r = nf[:, 2, 2 * 8:3 * 8].unsqueeze(2).broadcast_to([P, 8, HD])
            h = by_head(heads[:, 512 * 2:512 * 3])
            dve.tensor_tensor(h, h, r, ALU.mult).then_inc(normed, 1)

        def keep_keys(i):
            need(dve, head_copied, 4 * i)
            need(dve, score_out, 4 * i)
            dve.tensor_copy(kT[:, :, 0:WIN], kT[:, :, P:P + WIN]).then_inc(keys_kept, 1)

        def units(ap):
            return ap.rearrange("p (u k) -> p u k", k=KEYS)

        def row_max(i, g):
            dve.wait_ge(score_out, 4 * i + g + 1)
            dve.tensor_reduce(neg_max[:, 4 * g:4 * g + 4], units(SC[g % 2][:, 0:G]), AX, ALU.max, negate=True)\
                .then_inc(max_step, 1)

        def bias_rows(i, g):
            dve.wait_ge(max_step, 4 * i + g + 1)
            dve.wait_ge(factors_placed, i + 1)
            need(dve, exp_done, 4 * i + g - 3)
            dve.tensor_tensor(exp_bias[:, 4 * g:4 * g + 4], neg_max[:, 4 * g:4 * g + 4],
                              q_factor[:, 2 * g:2 * g + 2, :].rearrange("p a b -> p (a b)"), ALU.mult).then_inc(biased, 1)

        def row_sum(i, g):
            dve.wait_ge(exp_done, 4 * i + g + 1)
            dve.tensor_reduce(rowsum[:, 4 * g:4 * g + 4], units(probs[:, g, :]), AX, ALU.add).then_inc(sum_step, 1)

        def invert(i, g2):
            dve.wait_ge(sum_step, 4 * i + 2 * g2 + 2)
            need(dve, probs_done, 4 * i + 2 * g2 - 2)
            dve.reciprocal(rowinv[:, 8 * g2:8 * g2 + 8], rowsum[:, 8 * g2:8 * g2 + 8]).then_inc(inverted, 1)

        def ln(m, k):
            base = LN * m
            if k == 0:
                dve.wait_ge(mid_back, m + 1)
                dve.bn_stats(st[:], MX[0][:, 0:D]).then_inc(ln_step, 1)
            elif k == 1:
                dve.wait_ge(ln_step, base + 1)
                dve.memset(spare[:], 0.0)
                dve.bn_aggr(mv[:], st[:]).then_inc(ln_step, 1)
            elif k == 2:
                dve.wait_ge(ln_step, base + 2)
                dve.tensor_scalar(lnr[:, 0:1], mv[:, 1:2], 1e-5, None, ALU.add).then_inc(ln_step, 1)
            elif k < LN:
                rsqrt_op(dve, k - 3, lnr[:, 0:1], lnr[:, 1:2], lnr[:, 2:3], ln_step, base + 3)
            else:
                dve.wait_ge(ln_step, base + LN)
                need(dve, xn_T, m)
                dve.tensor_scalar(xn[:], MX[0][:, 0:D], mv[:, 0:1], lnr[:, 1:2], ALU.subtract, ALU.mult)\
                    .then_inc(xn_done, 1)

        def hidden(m):
            dve.wait_ge(up_out, m + 1)
            dve.wait_ge(gelu_done, m + 1)
            need(dve, ffn_out, m)
            layer = m // TILES
            for c in range(FC):
                ins = dve.scalar_tensor_tensor(
                    hT[0:ROWS[c], c, :], MX[0][0:ROWS[c], 128 * c:128 * c + 128],
                    bias1[0:ROWS[c], bass.ds(layer, 1), 0, c:c + 1].rearrange("p l c -> p (l c)"),
                    gel[0:ROWS[c], c, :], ALU.add, ALU.mult)
            ins.then_inc(hidden_done, 1)

        def new_x(m):
            dve.wait_ge(ffn_out, m + 1)
            dve.wait_ge(midb_done, m + 1)
            dve.tensor_tensor(x_all[:, bass.ds(m % TILES, 1), :], MX[1][:, 0:D].unsqueeze(1), midb[:].unsqueeze(1),
                              ALU.add).then_inc(x_done, 1)

        def new_mid(i):
            dve.wait_ge(attn_out, i + 1)
            need(dve, mid_T, i)
            need(dve, midb_done, i)
            dve.tensor_tensor(mid[:].unsqueeze(1), MX[1][:, 0:D].unsqueeze(1), x_all[:, bass.ds(i % TILES, 1), :],
                              ALU.add).then_inc(mid_done, 1)

        def step(s, at_edge=False):
            i, n, x2, j, m = tiles_of(s, at_edge)
            if i is not None:
                keep_keys(i)
            if m is not None:
                ln(m, 6)
            if i is not None:
                normalise(i)
            if m is not None:
                ln(m, 7)
            if i is not None:
                place_factors(i)
            if m is not None:
                ln(m, 8)
            if n is not None:
                rotate_cos(n, 0)
            if m is not None:
                ln(m, 9)
            if n is not None:
                rotate_sin(n, 0)
            if m is not None:
                ln(m, 10)
            if n is not None:
                rotate_cos(n, 1)
            if m is not None:
                ln(m, 11)
            if n is not None:
                rotate_sin(n, 1)
            if m is not None:
                ln(m, 12)
            if n is not None:
                sum_squares(n, 0)
            if m is not None:
                ln(m, 13)
            if n is not None:
                sum_squares(n, 1)
                rotate_cos(n, 2)
                rotate_sin(n, 2)
            if m is not None:
                hidden(m)
            if n is not None:
                sum_squares(n, 2)
            if i is not None:
                row_max(i, 0)
                bias_rows(i, 0)
                row_max(i, 1)
                bias_rows(i, 1)
            if n is not None:
                sum_squares(n, 3)
                rotate_cos(n, 3)
                norm_factor(n, 0)
                rotate_sin(n, 3)
                norm_factor(n, 1)
            if i is not None:
                row_max(i, 2)
            if n is not None:
                norm_factor(n, 2)
            if j is not None:
                new_mid(j)
            if n is not None:
                norm_factor(n, 3)
            if i is not None:
                bias_rows(i, 2)
            if n is not None:
                norm_factor(n, 4)
            if i is not None:
                row_max(i, 3)
            if n is not None:
                norm_factor(n, 5)
            if i is not None:
                row_sum(i, 0)
            if n is not None:
                norm_factor(n, 6)
            if i is not None:
                bias_rows(i, 3)
                row_sum(i, 1)
            if n is not None:
                norm_factor(n, 7)
            if i is not None:
                invert(i, 0)
            if n is not None:
                norm_factor(n, 8)
            if j is not None:
                shift_mid(j)
            if n is not None:
                norm_factor(n, 9)
            if i is not None:
                row_sum(i, 2)
            if j is not None:
                ln(j, 0)
                ln(j, 1)
                ln(j, 2)
            if i is not None:
                row_sum(i, 3)
            if j is not None:
                ln(j, 3)
            if i is not None:
                invert(i, 1)
            if j is not None:
                ln(j, 4)
            if m is not None:
                new_x(m)
            if j is not None:
                ln(j, 5)

        dve.wait_ge(setup_done, 3)
        dve.wait_ge(small_loaded, 16 * N_SMALL)
        dve.tensor_copy(band16[:], band[:]).then_inc(band_ready, 1)
        for c in range(4):
            rotate_cos(0, c)
            rotate_sin(0, c)
        for c in range(4):
            sum_squares(0, c)
        for k in range(RS):
            norm_factor(0, k)
        for s in range(3):
            step(s, at_edge=True)
        with dve.Fori(3, N - 2) as s:
            step(s)
        for s in range(N - 2, N + 2):
            step(s, at_edge=True)
        dve.wait_ge(x_done, N)
        dve.scalar_tensor_tensor(x_in[:], x_all[:], gate, x_in[:], ALU.mult, ALU.add).then_inc(final_done, 1)

    @block.gpsimd
    def _(pool):
        def load_x(n):
            need(pool, x_T, n)
            need(pool, x_done, n - 4)
            pool.tensor_copy(x_cur[:].unsqueeze(1), x_all[:, bass.ds(n % TILES, 1), :]).then_inc(x_loaded, 1)

        def tables(n):
            need(pool, rotated, 4 * n)
            layer = n // TILES
            sc = qk_scale[:, bass.ds(layer, 1), :, :]
            pool.tensor_tensor(cos_l[:].unsqueeze(1), cos_t[:, bass.ds(n % TB, 1), :, :], sc, ALU.mult)\
                .then_inc(tables_done, 1)
            pool.tensor_tensor(sin_l[:].unsqueeze(1), sin_t[:, bass.ds(n % TB, 1), :, :],
                               qk_swapped[:, bass.ds(layer, 1), :, :], ALU.mult).then_inc(tables_done, 1)

        def join(n, c):
            pool.wait_ge(rotated, 4 * n + c + 1)
            need(pool, head_T, 4 * n - 3 + ORDER.index(c))
            cols = slice(512 * c, 512 * c + 512)
            pool.tensor_tensor(heads[:, cols], kept[:, cols], turned[:, cols], ALU.add).then_inc(joined, 1)

        def normalise(n):
            pool.wait_ge(nf_step, NF * (n + 1))
            pool.wait_ge(joined, 4 * n + 4)
            r = nf[:, 2, 3 * 8:4 * 8].unsqueeze(2).broadcast_to([P, 8, HD])
            h = heads[:, 512 * 3:512 * 4].rearrange("p (h d) -> p h d", d=HD)
            pool.tensor_tensor(h, h, r, ALU.mult).then_inc(normed_late, 1)

        def normalise_probs(i, g):
            pool.wait_ge(inverted, 2 * i + g // 2 + 1)
            r = rowinv[:, 4 * g:4 * g + 4].unsqueeze(2).broadcast_to([P, 4, KEYS])
            p = probs[:, g, :].rearrange("p (u k) -> p u k", k=KEYS)
            pool.tensor_tensor(p, p, r, ALU.mult).then_inc(probs_done, 1)

        def add_bias(i):
            pool.wait_ge(mid_done, i + 1)
            need(pool, x_done, i)
            pool.tensor_tensor(midb[:].unsqueeze(1), mid[:].unsqueeze(1), bias2[:, bass.ds(i // TILES, 1), :],
                               ALU.add).then_inc(midb_done, 1)

        def step(s, at_edge=False):
            i, n, x2, j, m = tiles_of(s, at_edge)
            if m is not None:
                add_bias(m)
            if i is not None:
                normalise(i)
            if x2 is not None:
                load_x(x2)
            if n is not None:
                for c in range(4):
                    join(n, c)
            if x2 is not None:
                tables(x2)
            if i is not None:
                for g in range(GROUPS):
                    normalise_probs(i, g)

        load_x(0)
        pool.memzero(xs[:]).then_inc(setup_done, 1)
        pool.memzero(ms[:]).then_inc(setup_done, 1)
        pool.memzero(kT[:]).then_inc(setup_done, 1)
        pool.memzero(v_raw[:, 1, :]).then_inc(kept_zero, 1)
        pool.wait_ge(small_loaded, 16 * N_SMALL)
        tables(0)
        for c in range(4):
            join(0, c)
        tables(1)
        load_x(1)
        for s in range(3):
            step(s, at_edge=True)
        with pool.Fori(3, N - 2) as s:
            step(s)
        for s in range(N - 2, N + 2):
            step(s, at_edge=True)

    mem.end_block()


def program(nc, w, out):
    with ExitStack() as ctx:
        mem = Memory(nc, ctx)
        bank = [mem.psum(f"bank{k}") for k in range(8)]
        x_all = mem.sbuf("x_all", [P, TILES, D])
        xn = mem.sbuf("xn_all", [P, TILES, D])
        xnT = mem.sbuf("xnT_all", [P, TILES, P])
        ident = mem.sbuf("ident", [P, P])
        ident16 = mem.sbuf("ident16", [P, P], BF16)
        gates = mem.sbuf("gates", [P, 4])
        gates_t = mem.sbuf("gates_t", [P, 4])
        ctx_rows = mem.sbuf("ctx_rows", [CTX, B, D])
        mem.ctxT = mem.sbuf("ctxT", [P, B, CTX])
        mem.w2s = {n: mem.sbuf("w2_" + n, s) for n, s in (
            ("ew1", [P, 8, P]), ("ew2", [P, 8, D]), ("sw1", [P, 2 * P]), ("sw3", [P, 2 * P]), ("sw2", [P, 2, D]),
            ("router", [P, 8]), ("bias", [P, 8]), ("before", [P, 64]))}
        mem.w3s = {n: mem.sbuf("w3_" + n, s) for n, s in (
            ("wq", [P, D]), ("wkv", [P, 2 * D]), ("wproj", [P, D]), ("own", [P, 16]))}
        lw = local_weights(mem)
        loaded, x_loaded0, turned, ready = mem.sem("loaded"), mem.sem("x_loaded0"), mem.sem("turned"), mem.sem("ready")
        mem.loads1 = {n: mem.sem("s1_load_" + n) for n in ("wk", "wv", "wq", "mask", "wfc")}
        mem.loads2, mem.loads3 = mem.sem("s2_loads"), mem.sem("s3_loads")

        def prefetch(sp):
            for name, src in (("ew1", w["L0_ffn_ew1"].rearrange("e p n -> p e n")),
                              ("ew2", w["L0_ffn_ew2"].rearrange("e p n -> p e n")),
                              ("sw1", w["L0_ffn_sw1"]), ("sw3", w["L0_ffn_sw3"]),
                              ("sw2", w["L0_ffn_sw2"].rearrange("(c p) n -> p c n", p=P)),
                              ("router", w["router_T"]), ("bias", w["L0_ffn_router_bias"].partition_broadcast(P)),
                              ("before", w["before"])):
                sp.dma_start(mem.w2s[name][:], src).then_inc(mem.loads2, 16)
            for name, src in (("wq", w["L1_xattn_W_q"]), ("wkv", w["L1_xattn_W_kv"]), ("wproj", w["L1_xattn_W_proj"]),
                              ("own", w["own"])):
                sp.dma_start(mem.w3s[name][:], src).then_inc(mem.loads3, 16)
            load_local_weights(sp, w, lw)

        mem.prefetch = prefetch
        block = mem.block()

        @block.sync
        def _(sp):
            sp.dma_start(ident[:], w["ident"]).then_inc(loaded, 16)
            sp.dma_start(ctx_rows[:], w["ctx_1024"].rearrange("b t d -> t b d")).then_inc(loaded, 16)
            sp.dma_start(gates[:, 0:2], w["g_xattn"].partition_broadcast(P)).then_inc(loaded, 16)
            sp.dma_start(gates[:, 2:4], w["g_ffn"].partition_broadcast(P)).then_inc(loaded, 16)
            sp.dma_start(x_all[:], w["x"].rearrange("b (t p) d -> p (b t) d", p=P)).then_inc(x_loaded0, 16)
            sp.wait_ge(x_loaded0, 16)

        @block.tensor
        def _(pe):
            pe.wait_ge(loaded, 64)
            for b in range(B):
                ins = pe.transpose(bank[0][:, CTX * b:CTX * b + CTX], ctx_rows[:, b, :], ident[0:CTX, 0:CTX])
            ins.then_inc(turned, 1)

        @block.vector
        def _(dve):
            dve.wait_ge(loaded, 64)
            dve.tensor_copy(ident16[:], ident[:]).then_inc(ready, 1)

        @block.scalar
        def _(act):
            act.wait_ge(loaded, 64)
            act.activation(gates_t[:], gates[:], ACT.Tanh).then_inc(ready, 1)
            act.wait_ge(turned, 1)
            act.copy(mem.ctxT[:].rearrange("p b t -> p (b t)"), bank[0][:, 0:B * CTX]).then_inc(ready, 1)

        mem.end_block()
        with mem.stage():
            layer_norm(mem, "ln1", x_all, xn, bank, ident, xnT)
        with mem.stage():
            cross_attention_wide(mem, w, x_all, xnT, bank, ident, gates_t[:, 0:1])
        with mem.stage():
            layer_norm(mem, "ln2", x_all, xn, bank, ident, xnT)
        with mem.stage():
            mixture(mem, w, x_all, xnT, bank, ident, gates_t[:, 2:3])
        with mem.stage():
            layer_norm(mem, "ln3", x_all, xn, bank, ident, xnT)
        with mem.stage():
            cross_attention_narrow(mem, w, x_all, xnT, bank, ident, gates_t[:, 1:2])
        with mem.stage():
            layer_norm(mem, "ln4", x_all, xn, bank, ident, None)
        with mem.stage():
            local_stage(mem, w, lw, xn, x_all, ident, ident16, bank, gates_t[:, 3:4], out)


_DIRECT = ["x", "ctx_1024", "g_xattn", "g_ffn", "L0_xattn_W_Q", "L0_xattn_W_K", "L0_xattn_W_V", "L0_xattn_W_fc",
           "L0_ffn_router_bias", "L0_ffn_sw1", "L0_ffn_sw3", "L0_ffn_sw2", "L0_ffn_ew1", "L0_ffn_ew2", "L1_xattn_W_q",
           "L1_xattn_W_kv", "L1_xattn_W_proj", "L1_ffn_Wqkv", "L1_ffn_q_scale", "L1_ffn_k_scale", "L1_ffn_Wo",
           "L1_ffn_W1", "L1_ffn_W2", "L1_ffn_b2"]


def _constants():
    half = np.arange(0, HD, 2, dtype=np.float64)
    position = np.arange(S, dtype=np.float64)
    angle = np.tile(position[:, None] * 10000.0 ** (-half / HD)[None, :], (1, 2))
    base = (half + 0.4 * HD) / (1.4 * HD)
    scale = np.tile(base[None, :] ** ((position - S // 2) / (WIN // 2))[:, None], (1, 2))
    sign = np.repeat([-1.0, 1.0], HD // 2)
    cos, sin = np.cos(angle), np.sin(angle) * sign
    by_tile = lambda q, k: np.stack([q, k], 1).reshape(TB, P, 2, HD).transpose(1, 0, 2, 3).astype(np.float32)
    query, key = np.arange(P)[:, None] % (P // 2), np.arange(KEYS)[None, :]
    seen = (key >= query) & (key <= query + WIN)
    band = np.zeros((P, TB, 4, KEYS), np.float32)
    for t in range(TB):
        for unit in range(4):
            first = (t == 0) and (unit % 2 == 0)
            band[:, t, unit][~(seen & (key >= WIN)) if first else ~seen] = -1e30
    keep = np.ones((P, TB), np.float32)
    keep[:, 0] = 0.0
    before = np.tile(np.tril(np.ones((8, 8), np.float32), -1).reshape(1, 64), (P, 1))
    own = (np.arange(P)[:, None] // 8 == np.arange(16)[None, :]).astype(np.float32)
    q_factor = 8.0
    return {"ident": np.eye(P, dtype=np.float32), "cos": by_tile(q_factor * cos * scale, cos / scale),
            "sin": by_tile(q_factor * sin * scale, sin / scale), "band": band.reshape(P, TB, G), "keep": keep,
            "before": before, "own": own}


def kernel(**inputs):
    import concourse.bacc as _bacc
    from concourse.bass_utils import run_bass_kernel_spmd as _run

    arrays = {n: np.asarray(inputs[n]) for n in _DIRECT}
    arrays["mask"] = np.asarray(inputs["mask_Bx8xSxS2_bf0"])
    arrays["router_T"] = np.asarray(inputs["L0_ffn_router_w"]).T
    for name in "qk":
        arrays[f"{name}_swapped"] = np.roll(np.asarray(inputs[f"L1_ffn_{name}_scale"]), HD // 2, axis=1)
    arrays["ln_g"] = np.asarray(inputs["L1_ffn_ln_g"]).T
    arrays["ln_b"] = np.asarray(inputs["L1_ffn_ln_b"]).T
    b1 = np.zeros((LAYERS, 2, FC * P), np.float32)
    b1[:, :, 0:FF] = np.asarray(inputs["L1_ffn_b1"]).reshape(LAYERS, 2, FF)
    arrays["b1"] = b1.reshape(LAYERS, 2, FC, P).transpose(3, 0, 1, 2)
    arrays.update(_constants())
    arrays = {n: np.ascontiguousarray(a) for n, a in arrays.items()}

    nc = _bacc.Bacc("TRN2", target_bir_lowering=False, num_devices=1)
    w = {n: nc.dram_tensor(f"in_{n}", a.shape, mybir.dt.from_np(a.dtype), kind="ExternalInput").ap()
         for n, a in arrays.items()}
    out = nc.dram_tensor("out_x", (B, S, D), F32, kind="ExternalOutput").ap()
    program(nc, w, out.rearrange("b (t p) d -> p (b t) d", p=P))
    r = _run(nc, [{f"in_{n}": a for n, a in arrays.items()}], core_ids=[0])
    return r.results[0]["out_x"]
```

```python
from contextlib import ExitStack, contextmanager

import concourse.bass as bass
import numpy as np
from concourse import mybir

F32 = mybir.dt.float32
BF16 = mybir.dt.bfloat16
I32 = mybir.dt.int32
ALU = mybir.AluOpType
ACT = mybir.ActivationFunctionType
AX = mybir.AxisListType.X

P = 128
D = 128
B, S = 2, 512
CTX = 77
TILES = B * S // P
TB = S // P

LAYERS, HEADS, HD, WIN = 6, 16, 64, 32
PAIRS = HEADS // 2
INNER = HEADS * HD
FF = 341
FC = 3
ROWS = [128, 128, FF - 256]
N = LAYERS * TILES
KEYS = 96
ORDER = (0, 2, 1, 3)
GROUPS = 4
G = 4 * KEYS


class Memory:

    def __init__(self, nc, ctx):
        self.nc, self.ctx, self.buffers = nc, ctx, ctx

    @contextmanager
    def stage(self):
        outer = self.buffers
        with ExitStack() as self.buffers:
            yield
        self.buffers = outer

    def sbuf(self, name, shape, dtype=F32):
        return self.buffers.enter_context(self.nc.sbuf_tensor(name, shape, dtype))

    def psum(self, name):
        return self.ctx.enter_context(self.nc.psum_tensor(name, [P, 512], F32))

    def sem(self, name):
        return self.ctx.enter_context(self.nc.semaphore(name))

    def block(self):
        self.open_block = self.nc.Block()
        return self.open_block.__enter__()

    def end_block(self):
        self.open_block.__exit__(None, None, None)


class Weights:
    pass


def rsqrt_op(dve, k, a, y, t, chain, before):
    dve.wait_ge(chain, before + k)
    if k == 0:
        ins = dve.tensor_scalar(y.bitcast(I32), a.bitcast(I32), -0.5, float(0x5F3759DF), ALU.mult, ALU.add)
    elif k % 3 == 1:
        ins = dve.tensor_tensor(t, y, y, ALU.mult)
    elif k % 3 == 2:
        ins = dve.scalar_tensor_tensor(t, t, -0.5, a, ALU.mult, ALU.mult)
    else:
        ins = dve.scalar_tensor_tensor(y, t, 1.5, y, ALU.add, ALU.mult)
    ins.then_inc(chain, 1)


RS = 10


def at(buf, index):
    return buf[:, bass.ds(index, 1)]


def need(eng, s, value):
    if not (isinstance(value, int) and value <= 0):
        eng.wait_ge(s, value)


def layer_norm(mem, name, x_all, xn, bank, ident, turn, beside=None):
    stats = mem.sbuf(name + "_stats", [P, TILES, 6])
    mv = mem.sbuf(name + "_mv", [P, TILES, 2])
    var, rstd, tmp = (mem.sbuf(name + s, [P, TILES]) for s in ("_var", "_rstd", "_tmp"))
    stats_done, aggr_done, chain, rows_done = (mem.sem(name + s) for s in ("_stats", "_aggr", "_chain", "_rows"))
    turned, copied = mem.sem(name + "_turned"), mem.sem(name + "_copied")
    block = mem.block()

    @block.vector
    def _(dve):
        for t in range(TILES):
            dve.bn_stats(stats[:, t, :], x_all[:, t, :]).then_inc(stats_done, 1)
        for t in range(TILES):
            dve.wait_ge(stats_done, t + 1)
            dve.bn_aggr(mv[:, t, :], stats[:, t, :]).then_inc(aggr_done, 1)
        dve.wait_ge(aggr_done, TILES)
        dve.tensor_scalar(var[:], mv[:, :, 1], 1e-5, None, ALU.add).then_inc(chain, 1)
        for k in range(RS):
            rsqrt_op(dve, k, var[:], rstd[:], tmp[:], chain, 1)
        dve.wait_ge(chain, 1 + RS)
        for t in range(TILES):
            dve.tensor_scalar(xn[:, t, :], x_all[:, t, :], mv[:, t, 0:1], rstd[:, t:t + 1], ALU.subtract, ALU.mult)\
                .then_inc(rows_done, 1)

    if turn is not None:
        @block.tensor
        def _(pe):
            if beside is not None:
                beside.tensor(pe)
            for t in range(TILES):
                pe.wait_ge(rows_done, t + 1)
                ins = pe.transpose(bank[t // 4][:, P * (t % 4):P * (t % 4) + P], xn[:, t, :], ident[:])
                if t % 4 == 3:
                    ins.then_inc(turned, 1)

        @block.scalar
        def _(act):
            if beside is not None:
                beside.scalar(act)
            for h in range(2):
                act.wait_ge(turned, h + 1)
                act.copy(turn[:, 4 * h:4 * h + 4, :], bank[h][:].rearrange("p (t n) -> p t n", t=4)).then_inc(copied, 1)

    if beside is not None:
        @block.gpsimd
        def _(pool):
            beside.gpsimd(pool)

    mem.end_block()


def run_steps(engine, step):
    step(0, None, 0)
    step(1, 0, 1)
    step(2, 1, 0)
    with engine.Fori(1, TILES // 2 - 1) as turn:
        step(2 * turn + 1, 2 * turn, 1)
        step(2 * turn + 2, 2 * turn + 1, 0)
    step(TILES - 1, TILES - 2, 1)
    step(None, TILES - 1, 0)


def wide_weights(mem):
    ww = Weights()
    ww.wq, ww.wk, ww.wv = (mem.sbuf(n, [P, 8 * 128]) for n in ("s1_wq", "s1_wk", "s1_wv"))
    ww.wfc = mem.sbuf("s1_wfc", [P, 8, D])
    ww.mask = mem.sbuf("s1_mask", [P, TILES, 8 * CTX], mybir.dt.uint8)
    ww.loads = {n: mem.sem("s1_load_" + n) for n in ("wk", "wv", "wq", "mask", "wfc")}
    return ww


def load_wide_weights(sp, w, ww):
    sp.dma_start(ww.wk[:], w["L0_xattn_W_K"]).then_inc(ww.loads["wk"], 16)
    sp.dma_start(ww.wv[:], w["L0_xattn_W_V"]).then_inc(ww.loads["wv"], 16)
    sp.dma_start(ww.wq[:], w["L0_xattn_W_Q"]).then_inc(ww.loads["wq"], 16)
    sp.dma_start(ww.wfc[:], w["L0_xattn_W_fc"].rearrange("(h p) n -> p h n", p=P)).then_inc(ww.loads["wfc"], 16)
    for b in range(B):
        for t in range(TB):
            sp.dma_start(ww.mask[:, TB * b + t, :].rearrange("p (h k) -> p h k", k=CTX),
                         w["mask"][b, :, P * t:P * t + P, :].rearrange("h q k -> q h k")).then_inc(ww.loads["mask"], 16)


def cross_attention_wide(mem, w, ww, x_all, xnT, bank, ident, gate):
    HEADS, HD, T = 8, 128, CTX
    G = 4 * T
    SCALE = float(1.0 / np.sqrt(np.float32(HD)))
    wq, wk, wv, wfc, mask = ww.wq, ww.wk, ww.wv, ww.wfc, ww.mask
    kT = mem.sbuf("s1_kT", [P, HEADS, B, T])
    vT = mem.sbuf("s1_vT", [P, HEADS, B, T])
    wqT = mem.sbuf("s1_wqT", [P, HEADS, D])
    to_scores = mem.sbuf("s1_to_scores", [P, B, HEADS, T])
    to_out = mem.sbuf("s1_to_out", [T, B, HEADS, D])
    mask_cur = mem.sbuf("s1_mask_cur", [P, HEADS * T], mybir.dt.uint8)
    floor = mem.sbuf("s1_floor", [P, G])
    spare = mem.sbuf("s1_spare", [P, 3])
    x_cur = mem.sbuf("s1_x_cur", [P, 2, P])
    probs = mem.sbuf("s1_probs", [P, 2, 2, G])
    stat = mem.sbuf("s1_stat", [P, 2, 3, HEADS])
    pT = mem.sbuf("s1_pT", [T, HEADS, P])
    SC, TR, OUT = bank[2:4], bank[4:6], bank[6:8]

    loads = ww.loads
    k_out, v_out, wq_T, m_out, o_out = (mem.sem("s1_" + n) for n in ("k_out", "v_out", "wq_T", "m_out", "o_out"))
    k_copied, v_copied, wq_copied, m_copied, o_copied = (
        mem.sem("s1_" + n) for n in ("k_copied", "v_copied", "wq_copied", "m_copied", "o_copied"))
    floor_set, x_copied, mask_copied = (mem.sem("s1_" + n) for n in ("floor_set", "x_copied", "mask_copied"))
    score_out, prob_T, y_out = mem.sem("s1_score_out"), mem.sem("s1_prob_T"), mem.sem("s1_y_out")
    exp_done, prob_copied, probs_done = mem.sem("s1_exp_done"), mem.sem("s1_prob_copied"), mem.sem("s1_probs_done")
    masked, max_done, shifted, summed, inverted, x_done = (
        mem.sem("s1_" + n) for n in ("masked", "max_done", "shifted", "summed", "inverted", "x_done"))

    block = mem.block()

    @block.sync
    def _(sp):
        mem.prefetch(sp)

    @block.tensor
    def _(pe):
        ctx_cols = mem.ctxT[:, :, :].rearrange("p b t -> p (b t)")
        half = lambda b, h: b[:, 256 * h:256 * h + B * T]

        def scores(i, par):
            pe.wait_ge(x_copied, i + 1)
            for c in range(2):
                need(pe, shifted, 2 * i + c - 1)
                pe.matmul(SC[c][:, 0:G], x_cur[:, par, :],
                          to_scores[:, bass.ds(i // TB, 1), 4 * c:4 * c + 4, :].rearrange("p b h t -> p (b h t)"),
                          start=True, stop=True).then_inc(score_out, 1)

        def transpose_probs(j, par):
            for c in range(2):
                pe.wait_ge(probs_done, 2 * j + c + 1)
                need(pe, prob_copied, 2 * j + c - 1)
                for h in range(4):
                    ins = pe.transpose(TR[c][0:T, P * h:P * h + P], probs[:, par, c, T * h:T * h + T], ident[:])
                ins.then_inc(prob_T, 1)

        def output(j, par):
            need(pe, x_done, j - 1)
            for h in range(HEADS):
                if h % 4 == 0:
                    pe.wait_ge(prob_copied, 2 * j + h // 4 + 1)
                ins = pe.matmul(OUT[par][:, 0:D], pT[:, h, :], to_out[:, bass.ds(j // TB, 1), h, :],
                                start=(h == 0), stop=(h == HEADS - 1))
            ins.then_inc(y_out, 1)

        pe.wait_ge(loads["wk"], 16)
        for c in range(4):
            for h in range(2):
                head = 2 * c + h
                ins = pe.matmul(half(bank[c], h), wk[:, HD * head:HD * head + HD], ctx_cols, start=True, stop=True)
            ins.then_inc(k_out, 1)
        pe.wait_ge(loads["wv"], 16)
        for c in range(4):
            for h in range(2):
                head = 2 * c + h
                ins = pe.matmul(half(bank[4 + c], h), wv[:, HD * head:HD * head + HD], ctx_cols, start=True, stop=True)
            ins.then_inc(v_out, 1)
        pe.wait_ge(loads["wq"], 16)
        for c in range(2):
            pe.wait_ge(k_copied, c + 1)
            for h in range(4):
                head = 4 * c + h
                ins = pe.transpose(bank[c][:, P * h:P * h + P], wq[:, HD * head:HD * head + HD], ident[:])
            ins.then_inc(wq_T, 1)
        for c in range(4):
            if c < 2:
                pe.wait_ge(k_copied, c + 3)
            else:
                pe.wait_ge(v_copied, c - 1)
            pe.wait_ge(wq_copied, c // 2 + 1)
            pe.wait_ge(k_copied, c + 1)
            for h in range(2):
                head = 2 * c + h
                ins = pe.matmul(half(bank[2 + c], h), wqT[:, head, :], kT[:, head, :, :].rearrange("p b t -> p (b t)"),
                                start=True, stop=True)
            ins.then_inc(m_out, 1)
        pe.wait_ge(loads["wfc"], 16)
        pe.wait_ge(v_copied, 4)
        for k in range(4):
            b, c = k // 2, k % 2
            for h in range(4):
                head = 4 * c + h
                ins = pe.matmul(bank[(6 + k) % 8][0:T, D * h:D * h + D], vT[:, head, b, :], wfc[:, head, :],
                                start=True, stop=True)
            ins.then_inc(o_out, 1)

        def step(i, j, par):
            if i is not None:
                scores(i, par)
            if j is not None:
                transpose_probs(j, 1 - par)
                if isinstance(j, int) and j == 0:
                    pe.wait_ge(o_copied, 4)
                output(j, 1 - par)

        pe.wait_ge(m_copied, 4)
        run_steps(pe, step)

    @block.scalar
    def _(act):
        def exp(i, par):
            for c in range(2):
                act.wait_ge(shifted, 2 * i + c + 1)
                act.activation(probs[:, par, c, :], probs[:, par, c, :], ACT.Exp).then_inc(exp_done, 1)

        def copy_probs(j):
            for c in range(2):
                act.wait_ge(prob_T, 2 * j + c + 1)
                need(act, y_out, j)
                act.copy(pT[:, 4 * c:4 * c + 4, :], TR[c][0:T, :].rearrange("p (h t) -> p h t", h=4))\
                    .then_inc(prob_copied, 1)

        for c in range(4):
            act.wait_ge(k_out, c + 1)
            act.copy(kT[:, 2 * c:2 * c + 2, :, :].rearrange("p h b t -> p h (b t)"),
                     bank[c][:, :].rearrange("p (h n) -> p h n", h=2)[:, :, 0:B * T]).then_inc(k_copied, 1)
        for c in range(2):
            act.wait_ge(wq_T, c + 1)
            act.copy(wqT[:, 4 * c:4 * c + 4, :], bank[c][:].rearrange("p (h n) -> p h n", h=4)).then_inc(wq_copied, 1)
        for k in range(4):
            act.wait_ge(o_out, k + 1)
            act.copy(to_out[:, k // 2, 4 * (k % 2):4 * (k % 2) + 4, :],
                     bank[(6 + k) % 8][0:T, :].rearrange("p (h n) -> p h n", h=4)).then_inc(o_copied, 1)

        def step(i, j, par):
            if j is not None:
                copy_probs(j)
            if i is not None:
                exp(i, par)

        run_steps(act, step)

    @block.vector
    def _(dve):
        rows = lambda ap: ap.rearrange("p (h k) -> p h k", k=T)

        def softmax_front(i, par):
            for c in range(2):
                if c == 0:
                    dve.wait_ge(mask_copied, i + 1)
                    dve.memset(spare[:, 2:3], 0.0)
                dve.wait_ge(score_out, 2 * i + c + 1)
                dve.memset(spare[:, c:c + 1], 0.0)
                dve.wait_ge(floor_set, 1)
                dve.copy_predicated(SC[c][:, 0:G], mask_cur[:, G * c:G * c + G], floor[:]).then_inc(masked, 1)
            for c in range(2):
                dve.wait_ge(masked, 2 * i + c + 1)
                dve.tensor_reduce(stat[:, par, 0, 4 * c:4 * c + 4], rows(SC[c][:, 0:G]), AX, ALU.max)\
                    .then_inc(max_done, 1)
            for c in range(2):
                dve.wait_ge(max_done, 2 * i + c + 1)
                need(dve, prob_T, 2 * i + c - 3)
                m = stat[:, par, 0, 4 * c:4 * c + 4].unsqueeze(2).broadcast_to([P, 4, T])
                dve.tensor_tensor(rows(probs[:, par, c, :]), rows(SC[c][:, 0:G]), m, ALU.subtract).then_inc(shifted, 1)

        def softmax_back(i, par):
            for c in range(2):
                dve.wait_ge(exp_done, 2 * i + c + 1)
                dve.tensor_reduce(stat[:, par, 1, 4 * c:4 * c + 4], rows(probs[:, par, c, :]), AX, ALU.add)\
                    .then_inc(summed, 1)
            dve.wait_ge(summed, 2 * i + 2)
            need(dve, probs_done, 2 * i - 2)
            dve.reciprocal(stat[:, par, 2, :], stat[:, par, 1, :]).then_inc(inverted, 1)

        def add(j, par):
            dve.wait_ge(y_out, j + 1)
            xt = x_all[:, bass.ds(j, 1), :].rearrange("p a d -> p (a d)")
            dve.scalar_tensor_tensor(xt, OUT[par][:, 0:D], gate, xt, ALU.mult, ALU.add).then_inc(x_done, 1)

        dve.memset(floor[:], -1e9).then_inc(floor_set, 1)
        for c in range(4):
            dve.wait_ge(v_out, c + 1)
            dve.tensor_copy(vT[:, 2 * c:2 * c + 2, :, :].rearrange("p h b t -> p h (b t)"),
                            bank[4 + c][:, :].rearrange("p (h n) -> p h n", h=2)[:, :, 0:B * T]).then_inc(v_copied, 1)
        for c in range(4):
            dve.wait_ge(m_out, c + 1)
            for h in range(2):
                ins = dve.tensor_scalar(to_scores[:, :, 2 * c + h, :], bank[2 + c][:, 256 * h:256 * h + B * T]
                                        .rearrange("p (b t) -> p b t", b=B), SCALE, None, ALU.mult)
            ins.then_inc(m_copied, 1)

        def step(i, j, par):
            if i is not None:
                softmax_front(i, par)
                softmax_back(i, par)
            if j is not None:
                add(j, 1 - par)

        run_steps(dve, step)

    @block.gpsimd
    def _(pool):
        def copy_mask(i):
            need(pool, masked, 2 * i)
            pool.tensor_copy(mask_cur[:].bitcast(I32).unsqueeze(1), at(mask[:].bitcast(I32), i)).then_inc(mask_copied, 1)

        def copy_x(i, par):
            need(pool, score_out, 2 * i - 2)
            pool.tensor_copy(x_cur[:, par:par + 1, :], at(xnT, i)).then_inc(x_copied, 1)

        def normalise_probs(i, par):
            pool.wait_ge(inverted, i + 1)
            for c in range(2):
                p = probs[:, par, c, :].rearrange("p (h k) -> p h k", k=T)
                r = stat[:, par, 2, 4 * c:4 * c + 4].unsqueeze(2).broadcast_to([P, 4, T])
                pool.tensor_tensor(p, p, r, ALU.mult).then_inc(probs_done, 1)

        def step(i, j, par):
            if i is not None:
                copy_x(i, par)
                copy_mask(i)
            if j is not None:
                normalise_probs(j, 1 - par)

        pool.wait_ge(loads["mask"], 16 * TILES)
        run_steps(pool, step)

    mem.end_block()


def mixture(mem, w, x_all, xnT, bank, ident, gate):
    E, HS = 8, 2
    N = S
    W = mem.w2s
    hT = mem.sbuf("s2_hT", [P, B, E, N])
    sT = mem.sbuf("s2_sT", [P, B, HS, N])
    gT = mem.sbuf("s2_gT", [P, B, HS, N])
    prob = mem.sbuf("s2_prob", [P, TILES, E])
    sel = mem.sbuf("s2_sel", [P, TILES, E])
    cmp = mem.sbuf("s2_cmp", [P, 2, TILES, E, E])
    rank = mem.sbuf("s2_rank", [P, TILES, E])
    comb = mem.sbuf("s2_comb", [P, TILES, E])
    den = mem.sbuf("s2_den", [P, 3, TILES])
    acc = mem.sbuf("s2_acc", [P, 2, 2, D])
    HB = bank[0:4]
    ROUTER = bank[7]
    SETS = [bank[4:7], [bank[0], bank[1], bank[7]]]
    tile_set = lambda j: SETS[1] if j >= TB and j % 2 == 0 else SETS[0]

    route_out, routed = mem.sem("s2_route_out"), mem.sem("s2_routed")
    chain = mem.sem("s2_chain")
    hid_out, read_by_act, gated = (mem.sem("s2_" + n) for n in ("hid_out", "read_by_act", "gated"))
    y_out, shared_out, acc_step, x_done = (mem.sem("s2_" + n) for n in ("y_out", "shared_out", "acc_step", "x_done"))
    loads = mem.loads2
    block = mem.block()

    @block.tensor
    def _(pe):
        pe.wait_ge(loads, 16 * 8)
        for t in range(TILES):
            ins = pe.matmul(ROUTER[:, E * t:E * t + E], xnT[:, t, :], W["router"][:], start=True, stop=True)
        ins.then_inc(route_out, 1)
        pe.wait_ge(routed, 1)

        def hidden(p, c):
            x = xnT[:, p * TB:(p + 1) * TB, :]
            if c < HS:
                need(pe, read_by_act, (E + HS) * p - HS + 1 + c if p else 0)
            elif c < 4:
                need(pe, gated, HS * p - 3 + c if p else 0)
            else:
                pe.wait_ge(read_by_act, (E + HS) * p + c - 3)
            if c < E:
                weights = W["ew1"][:, c, :]
            elif c < E + HS:
                weights = W["sw1"][:, P * (c - E):P * (c - E) + P]
            else:
                weights = W["sw3"][:, P * (c - E - HS):P * (c - E - HS) + P]
            pe.matmul(HB[c % 4][:], weights, x, start=True, stop=True).then_inc(hid_out, 1)

        def outputs(j):
            p, t = j // TB, j % TB
            EO, SO = tile_set(j)[0:2], tile_set(j)[2]
            pe.wait_ge(read_by_act, (E + HS) * (p + 1))
            need(pe, x_done, j if j < TB else j - 1 if j > TB else 0)
            cols = slice(P * t, P * t + P)
            for e in range(E):
                ins = pe.matmul(EO[e // 4][:, D * (e % 4):D * (e % 4) + D], hT[:, p, e, cols], W["ew2"][:, e, :],
                                start=True, stop=True)
            ins.then_inc(y_out, 1)
            pe.wait_ge(gated, HS * (p + 1))
            for c in range(HS):
                ins = pe.matmul(SO[:, 0:D], sT[:, p, c, cols], W["sw2"][:, c, :], start=(c == 0), stop=(c == HS - 1))
            ins.then_inc(shared_out, 1)

        for c in range(E + 2 * HS):
            hidden(0, c)
        for t in range(TB):
            for c in range(3 * t, 3 * t + 3):
                hidden(1, c)
            outputs(t)
        for t in range(TB):
            outputs(TB + t)

    @block.scalar
    def _(act):
        act.wait_ge(route_out, 1)
        act.activation(prob[:].rearrange("p t e -> p (t e)"), ROUTER[:, 0:TILES * E], ACT.Sigmoid).then_inc(routed, 1)
        for p in range(B):
            for c in range(E):
                act.wait_ge(hid_out, 12 * p + c + 1)
                act.activation(hT[:, p, c, :], HB[c % 4][:], ACT.Gelu).then_inc(read_by_act, 1)
            for c in range(HS):
                act.wait_ge(hid_out, 12 * p + E + c + 1)
                act.activation(gT[:, p, c, :], HB[c][:], ACT.Silu).then_inc(read_by_act, 1)

    @block.vector
    def _(dve):
        steps = [0]

        def chained(ins):
            ins.then_inc(chain, 1)
            steps[0] += 1
            dve.wait_ge(chain, steps[0])

        wide = [P, TILES, E, E]
        dve.wait_ge(routed, 1)
        dve.wait_ge(loads, 16 * 8)
        bias = W["bias"][:].unsqueeze(1).broadcast_to([P, TILES, E])
        chained(dve.tensor_tensor(sel[:], prob[:], bias, ALU.add))
        other, own = sel[:].unsqueeze(2).broadcast_to(wide), sel[:].unsqueeze(3).broadcast_to(wide)
        for t in range(TILES):
            dve.tensor_tensor(cmp[:, 0, t], other[:, t], own[:, t], ALU.is_gt)
            ins = dve.tensor_tensor(cmp[:, 1, t], other[:, t], own[:, t], ALU.is_equal)
        chained(ins)
        before = W["before"][:].unsqueeze(1).broadcast_to([P, TILES, E * E])
        flat = lambda k: cmp[:, k].rearrange("p t e j -> p t (e j)")
        chained(dve.tensor_tensor(flat(1), flat(1), before, ALU.mult))
        chained(dve.tensor_tensor(flat(0), flat(0), flat(1), ALU.add))
        chained(dve.tensor_reduce(rank[:], cmp[:, 0], AX, ALU.add))
        chained(dve.tensor_scalar(rank[:], rank[:], 2.0, None, ALU.is_lt))
        chained(dve.tensor_tensor(comb[:], prob[:], rank[:], ALU.mult))
        chained(dve.tensor_reduce(den[:, 0, :], comb[:], AX, ALU.add))
        chained(dve.tensor_scalar(den[:, 1, :], den[:, 0, :], 1e-9, None, ALU.add))
        chained(dve.reciprocal(den[:, 1, :], den[:, 1, :]))
        chained(dve.tensor_scalar(den[:, 0, :], den[:, 0, :], 1e-9, None, ALU.is_gt))
        chained(dve.tensor_tensor(den[:, 1, :], den[:, 1, :], den[:, 0, :], ALU.mult))
        chained(dve.tensor_scalar(den[:, 2, :], den[:, 0, :], -0.5, 0.5, ALU.mult, ALU.add))
        spread = lambda k: den[:, k, :].unsqueeze(2).broadcast_to([P, TILES, E])
        chained(dve.tensor_tensor(comb[:], comb[:], spread(1), ALU.mult))
        chained(dve.tensor_tensor(rank[:], rank[:], spread(2), ALU.mult))
        chained(dve.tensor_tensor(comb[:], comb[:], rank[:], ALU.add))
        chained(dve.tensor_scalar(comb[:], comb[:], gate, None, ALU.mult))

        def gate_shared(p):
            for c in range(HS):
                dve.wait_ge(hid_out, 12 * p + E + HS + c + 1)
                dve.wait_ge(read_by_act, (E + HS) * p + E + c + 1)
                dve.tensor_tensor(sT[:, p, c, :], HB[2 + c][:], gT[:, p, c, :], ALU.mult).then_inc(gated, 1)

        def combine(j):
            EO, SO = tile_set(j)[0:2], tile_set(j)[2]
            dve.wait_ge(y_out, j + 1)
            for e in range(E):
                a = acc[:, j % 2, e % 2, :]
                y = EO[e // 4][:, D * (e % 4):D * (e % 4) + D]
                weight = comb[:, j, e:e + 1]
                if e == 0:
                    ins = dve.scalar_tensor_tensor(a, y, weight, x_all[:, j, :], ALU.mult, ALU.add)
                elif e == 1:
                    ins = dve.tensor_scalar(a, y, weight, None, ALU.mult)
                else:
                    dve.wait_ge(acc_step, 9 * j + e - 1)
                    ins = dve.scalar_tensor_tensor(a, y, weight, a, ALU.mult, ALU.add)
                ins.then_inc(acc_step, 1)
            dve.wait_ge(shared_out, j + 1)
            dve.wait_ge(acc_step, 9 * j + 7)
            dve.scalar_tensor_tensor(acc[:, j % 2, 0, :], SO[:, 0:D], gate, acc[:, j % 2, 0, :], ALU.mult, ALU.add).then_inc(acc_step, 1)
            dve.wait_ge(acc_step, 9 * j + 9)
            dve.tensor_tensor(x_all[:, j, :], acc[:, j % 2, 0, :], acc[:, j % 2, 1, :], ALU.add).then_inc(x_done, 1)

        gate_shared(0)
        for j in range(TILES):
            if j == TB - 1:
                gate_shared(1)
            combine(j)

    mem.end_block()


N_HEADS, N_HD = 16, 8
PARTS = [(0, 6), (6, 12), (12, 16)]


def narrow_products(mem):
    nar = Weights()
    nar.vT = mem.sbuf("s3_vT", [P, B, CTX])
    nar.to_scores = mem.sbuf("s3_to_scores", [P, B, N_HEADS, CTX])
    nar.to_out = mem.sbuf("s3_to_out", [CTX, B, N_HEADS, D])
    return nar


def own_rows(mem, name):
    return mem.sbuf(name, [P, B, N_HEADS, CTX])


def spread_heads(pool, mem, dst, src, done):
    own = mem.w3s["own"][:].unsqueeze(2).broadcast_to([P, N_HEADS, CTX])
    for b in range(B):
        pool.tensor_tensor(dst[:, b], src[:, b, :].unsqueeze(1).broadcast_to([P, N_HEADS, CTX]), own, ALU.mult)\
            .then_inc(done, 1)


def form_to_scores(mem, nar, bank, ident):
    SCALE = float(np.float32(1.0) / np.float32(N_HD ** -0.5))
    W = mem.w3s
    kT, wqT, k_own = mem.sbuf("s3_kT", [P, B, CTX]), mem.sbuf("s3_wqT", [P, D]), own_rows(mem, "s3_k_own")
    setup_out, setup_copied, k_ready, m_out, m_copied = (
        mem.sem("s3_" + n) for n in ("setup_out", "setup_copied", "k_ready", "m_out", "m_copied"))
    PRODUCT = [bank[2 + (3 + k) % 6] for k in range(2 * len(PARTS))]
    beside = Weights()

    def tensor(pe):
        ctx_cols = mem.ctxT[:, :, :].rearrange("p b t -> p (b t)")
        pe.wait_ge(mem.loads3, 16 * 4)
        pe.matmul(bank[2][:, 0:B * CTX], W["wkv"][:, 0:D], ctx_cols, start=True, stop=True).then_inc(setup_out, 1)
        pe.transpose(bank[3][:, 0:D], W["wq"][:], ident[:]).then_inc(setup_out, 1)
        pe.matmul(bank[4][:, 0:B * CTX], W["wkv"][:, D:2 * D], ctx_cols, start=True, stop=True).then_inc(setup_out, 1)
        pe.wait_ge(setup_copied, 3)
        for b in range(B):
            pe.wait_ge(k_ready, b + 1)
            for c, (h0, h1) in enumerate(PARTS):
                pe.matmul(PRODUCT[3 * b + c][:, 0:CTX * (h1 - h0)], wqT[:],
                          k_own[:, b, h0:h1, :].rearrange("p h t -> p (h t)"), start=True, stop=True).then_inc(m_out, 1)

    def scalar(act):
        for k, (dst, src) in enumerate([(kT[:].rearrange("p b t -> p (b t)"), bank[2][:, 0:B * CTX]),
                                        (wqT[:], bank[3][:, 0:D]),
                                        (nar.vT[:].rearrange("p b t -> p (b t)"), bank[4][:, 0:B * CTX])]):
            act.wait_ge(setup_out, k + 1)
            act.copy(dst, src).then_inc(setup_copied, 1)
        for b in range(B):
            for c, (h0, h1) in enumerate(PARTS):
                act.wait_ge(m_out, 3 * b + c + 1)
                act.activation(nar.to_scores[:, b, h0:h1, :].rearrange("p h t -> p (h t)"),
                               PRODUCT[3 * b + c][:, 0:CTX * (h1 - h0)], ACT.Copy, scale=SCALE).then_inc(m_copied, 1)

    def gpsimd(pool):
        pool.wait_ge(setup_copied, 1)
        pool.wait_ge(mem.loads3, 16 * 4)
        spread_heads(pool, mem, k_own, kT, k_ready)

    beside.tensor, beside.scalar, beside.gpsimd = tensor, scalar, gpsimd
    return beside


def form_to_out(mem, nar, bank):
    v_own = own_rows(mem, "s3_v_own")
    v_ready, o_out, o_copied = mem.sem("s3_v_ready"), mem.sem("s3_o_out"), mem.sem("s3_o_copied")
    beside = Weights()

    def tensor(pe):
        for k in range(8):
            b, c = k // 4, k % 4
            pe.wait_ge(v_ready, b + 1)
            need(pe, o_copied, k - 5)
            for h in range(4):
                ins = pe.matmul(bank[2 + k % 6][0:CTX, D * h:D * h + D], v_own[:, b, 4 * c + h, :],
                                mem.w3s["wproj"][:], start=True, stop=True)
            ins.then_inc(o_out, 1)

    def scalar(act):
        for k in range(8):
            act.wait_ge(o_out, k + 1)
            act.copy(nar.to_out[:, k // 4, 4 * (k % 4):4 * (k % 4) + 4, :],
                     bank[2 + k % 6][0:CTX, :].rearrange("p (h n) -> p h n", h=4)).then_inc(o_copied, 1)

    def gpsimd(pool):
        spread_heads(pool, mem, v_own, nar.vT, v_ready)

    beside.tensor, beside.scalar, beside.gpsimd = tensor, scalar, gpsimd
    return beside


def cross_attention_narrow(mem, nar, x_all, xnT, bank, ident, gate):
    HEADS, T = N_HEADS, CTX
    to_scores, to_out = nar.to_scores, nar.to_out
    x_cur = mem.sbuf("s3_x_cur", [P, 2, P])
    probs = mem.sbuf("s3_probs", [P, 2, HEADS, T])
    stat = mem.sbuf("s3_stat", [P, 2, 3, HEADS])
    pT = mem.sbuf("s3_pT", [T, HEADS, P])
    SC, TR, OUT = bank[0:3], bank[3:5], bank[5:7]
    x_copied, score_out, prob_T, y_out = (mem.sem("s3_" + n) for n in ("x_copied", "score_out", "prob_T", "y_out"))
    exp_done, prob_copied, probs_done = mem.sem("s3_exp_done"), mem.sem("s3_prob_copied"), mem.sem("s3_probs_done")
    max_done, shifted, summed, inverted, x_done = (mem.sem("s3_" + n) for n in
                                                   ("max_done", "shifted", "summed", "inverted", "x_done"))
    block = mem.block()

    @block.tensor
    def _(pe):
        def scores(i, par):
            pe.wait_ge(x_copied, i + 1)
            for c, (h0, h1) in enumerate(PARTS):
                need(pe, shifted, 3 * i + c - 2)
                pe.matmul(SC[c][:, 0:T * (h1 - h0)], x_cur[:, par, :],
                          to_scores[:, bass.ds(i // TB, 1), h0:h1, :].rearrange("p b h t -> p (b h t)"),
                          start=True, stop=True).then_inc(score_out, 1)

        def transpose_probs(j, par):
            for c in range(4):
                pe.wait_ge(probs_done, 2 * j + c // 2 + 1)
                need(pe, prob_copied, 4 * j + c - 1)
                for h in range(4):
                    ins = pe.transpose(TR[c % 2][0:T, P * h:P * h + P], probs[:, par, 4 * c + h, :], ident[:])
                ins.then_inc(prob_T, 1)

        def output(j, par):
            need(pe, x_done, j - 1)
            for h in range(HEADS):
                if h % 4 == 0:
                    pe.wait_ge(prob_copied, 4 * j + h // 4 + 1)
                ins = pe.matmul(OUT[par][:, 0:D], pT[:, h, :], to_out[:, bass.ds(j // TB, 1), h, :],
                                start=(h == 0), stop=(h == HEADS - 1))
            ins.then_inc(y_out, 1)

        def step(i, j, par):
            if i is not None:
                scores(i, par)
            if j is not None:
                transpose_probs(j, 1 - par)
                output(j, 1 - par)

        run_steps(pe, step)

    @block.scalar
    def _(act):
        def exp(i, par):
            for c, (h0, h1) in enumerate(PARTS):
                act.wait_ge(shifted, 3 * i + c + 1)
                act.activation(probs[:, par, h0:h1, :], probs[:, par, h0:h1, :], ACT.Exp).then_inc(exp_done, 1)

        def copy_probs(j):
            for c in range(4):
                act.wait_ge(prob_T, 4 * j + c + 1)
                need(act, y_out, j)
                act.copy(pT[:, 4 * c:4 * c + 4, :], TR[c % 2][0:T, :].rearrange("p (h t) -> p h t", h=4))\
                    .then_inc(prob_copied, 1)

        def step(i, j, par):
            if j is not None:
                copy_probs(j)
            if i is not None:
                exp(i, par)

        run_steps(act, step)

    @block.vector
    def _(dve):
        def softmax_front(i, par):
            for c, (h0, h1) in enumerate(PARTS):
                sc = SC[c][:, 0:T * (h1 - h0)].rearrange("p (h k) -> p h k", k=T)
                dve.wait_ge(score_out, 3 * i + c + 1)
                dve.tensor_reduce(stat[:, par, 0, h0:h1], sc, AX, ALU.max).then_inc(max_done, 1)
            for c, (h0, h1) in enumerate(PARTS):
                sc = SC[c][:, 0:T * (h1 - h0)].rearrange("p (h k) -> p h k", k=T)
                dve.wait_ge(max_done, 3 * i + c + 1)
                need(dve, prob_T, 4 * i - 4)
                dve.tensor_tensor(probs[:, par, h0:h1, :], sc,
                                  stat[:, par, 0, h0:h1].unsqueeze(2).broadcast_to([P, h1 - h0, T]),
                                  ALU.subtract).then_inc(shifted, 1)

        def softmax_back(i, par):
            dve.wait_ge(exp_done, 3 * i + 3)
            dve.tensor_reduce(stat[:, par, 1, :], probs[:, par], AX, ALU.add).then_inc(summed, 1)
            dve.wait_ge(summed, i + 1)
            need(dve, probs_done, 2 * i - 2)
            dve.reciprocal(stat[:, par, 2, :], stat[:, par, 1, :]).then_inc(inverted, 1)

        def add(j, par):
            dve.wait_ge(y_out, j + 1)
            xt = x_all[:, bass.ds(j, 1), :].rearrange("p a d -> p (a d)")
            dve.scalar_tensor_tensor(xt, OUT[par][:, 0:D], gate, xt, ALU.mult, ALU.add).then_inc(x_done, 1)

        def step(i, j, par):
            if i is not None:
                softmax_front(i, par)
                softmax_back(i, par)
            if j is not None:
                add(j, 1 - par)

        run_steps(dve, step)

    @block.gpsimd
    def _(pool):
        def copy_x(i, par):
            need(pool, score_out, 3 * i - 3)
            pool.tensor_copy(x_cur[:, par:par + 1, :], at(xnT, i)).then_inc(x_copied, 1)

        def normalise_probs(i, par):
            pool.wait_ge(inverted, i + 1)
            for c in range(2):
                p = probs[:, par, 8 * c:8 * c + 8, :]
                r = stat[:, par, 2, 8 * c:8 * c + 8].unsqueeze(2).broadcast_to([P, 8, T])
                pool.tensor_tensor(p, p, r, ALU.mult).then_inc(probs_done, 1)

        def step(i, j, par):
            if i is not None:
                copy_x(i, par)
            if j is not None:
                normalise_probs(j, 1 - par)

        run_steps(pool, step)

    mem.end_block()


def local_weights(mem):
    lw = Weights()
    lw.wqkv = mem.sbuf("wqkv", [P, 2, 3 * INNER])
    lw.wo = mem.sbuf("wo", [P, LAYERS, PAIRS, D])
    lw.w1 = mem.sbuf("w1", [P, 2 * FF])
    lw.w2 = mem.sbuf("w2", [P, LAYERS, FC, D])
    lw.qk_scale = mem.sbuf("qk_scale", [P, LAYERS, 2, HD])
    lw.qk_swapped = mem.sbuf("qk_swapped", [P, LAYERS, 2, HD])
    lw.ln_scale = mem.sbuf("ln_scale", [P, LAYERS])
    lw.ln_shift = mem.sbuf("ln_shift", [P, LAYERS])
    lw.bias1 = mem.sbuf("bias1", [P, LAYERS, 2, FC])
    lw.bias2 = mem.sbuf("bias2", [P, LAYERS, D])
    lw.cos_t = mem.sbuf("cos_t", [P, TB, 2, HD])
    lw.sin_t = mem.sbuf("sin_t", [P, TB, 2, HD])
    lw.band = mem.sbuf("band", [P, TB, G])
    lw.keep = mem.sbuf("keep", [P, TB])
    lw.small_loaded, lw.wqkv_loaded, lw.w1_loaded, lw.wo_loaded, lw.w2_loaded = (
        mem.sem(n) for n in ("small_loaded", "wqkv_loaded", "w1_loaded", "wo_loaded", "w2_loaded"))
    return lw


N_SMALL = 12


def load_local_weights(sp, w, lw):
    small = [
        (lw.qk_scale[:, :, 0, :], w["L1_ffn_q_scale"].partition_broadcast(P)),
        (lw.qk_scale[:, :, 1, :], w["L1_ffn_k_scale"].partition_broadcast(P)),
        (lw.qk_swapped[:, :, 0, :], w["q_swapped"].partition_broadcast(P)),
        (lw.qk_swapped[:, :, 1, :], w["k_swapped"].partition_broadcast(P)),
        (lw.cos_t[:], w["cos"]), (lw.sin_t[:], w["sin"]), (lw.band[:], w["band"]), (lw.keep[:], w["keep"]),
        (lw.ln_scale[:], w["ln_g"]), (lw.ln_shift[:], w["ln_b"]), (lw.bias1[:], w["b1"]),
        (lw.bias2[:], w["L1_ffn_b2"].partition_broadcast(P)),
    ]
    for dst, src in small:
        sp.dma_start(dst, src).then_inc(lw.small_loaded, 16)
    assert len(small) == N_SMALL
    sp.dma_start(lw.wqkv[:, 0, :], w["L1_ffn_Wqkv"][0]).then_inc(lw.wqkv_loaded, 16)
    sp.dma_start(lw.w1[:], w["L1_ffn_W1"][0]).then_inc(lw.w1_loaded, 16)
    sp.dma_start(lw.wo[:], w["L1_ffn_Wo"].rearrange("l (k p) n -> p l k n", p=P)).then_inc(lw.wo_loaded, 16)
    for c in range(FC):
        sp.dma_start(lw.w2[0:ROWS[c], :, c, :], w["L1_ffn_W2"][:, 128 * c:128 * c + ROWS[c], :]
                     .rearrange("l p n -> p l n")).then_inc(lw.w2_loaded, 16)
    sp.wait_ge(lw.wqkv_loaded, 16)
    sp.dma_start(lw.wqkv[:, 1, :], w["L1_ffn_Wqkv"][1]).then_inc(lw.wqkv_loaded, 16)


def local_stage(mem, w, lw, x_all, x_in, ident, ident16, bank, gate, out):
    sbuf, sem = mem.sbuf, mem.sem
    wqkv, wo, w1, w2 = lw.wqkv, lw.wo, lw.w1, lw.w2
    ln_scale, ln_shift, bias1, bias2 = lw.ln_scale, lw.ln_shift, lw.bias1, lw.bias2
    qk_scale, qk_swapped, cos_t, sin_t, band, keep = lw.qk_scale, lw.qk_swapped, lw.cos_t, lw.sin_t, lw.band, lw.keep
    band16 = sbuf("band16", [P, TB, G], BF16)
    small_loaded, wqkv_loaded, w1_loaded, wo_loaded, w2_loaded = (
        lw.small_loaded, lw.wqkv_loaded, lw.w1_loaded, lw.wo_loaded, lw.w2_loaded)

    half_rows = slice(P // 2, P)

    x_cur = sbuf("x_cur", [P, D])
    xs = sbuf("xs", [P, P + 1])
    ms = sbuf("ms", [P, P + 1])
    squares = sbuf("squares", [P, 2 * INNER])
    kept = sbuf("kept", [P, 2 * INNER])
    turned = sbuf("turned", [P, 2 * INNER])
    heads = sbuf("heads", [P, 2 * INNER])
    cos_l = sbuf("cos_l", [P, 2, HD])
    sin_l = sbuf("sin_l", [P, 2, HD])
    nf = sbuf("nf", [P, 4, 2 * HEADS])
    qT = sbuf("qT", [P, PAIRS, P])
    kT = sbuf("kT", [P, PAIRS, WIN + P])
    v_raw = sbuf("v_raw", [P, 2, INNER])
    v_win = sbuf("v_win", [KEYS, 2, INNER])
    probs = sbuf("probs", [P, GROUPS, G])
    neg_max = sbuf("neg_max", [P, 4 * GROUPS])
    q_factor = sbuf("q_factor", [P, PAIRS, 2])
    exp_bias = sbuf("exp_bias", [P, 4 * GROUPS])
    rowsum = sbuf("rowsum", [P, 4 * GROUPS])
    rowinv = sbuf("rowinv", [P, 4 * GROUPS])
    pT = sbuf("pT", [KEYS, GROUPS, 512])
    aT = sbuf("aT", [P, PAIRS, P])
    mid = sbuf("mid", [P, D])
    midb = sbuf("midb", [P, D])
    st = sbuf("st", [P, 6])
    mv = sbuf("mv", [P, 2])
    spare = sbuf("spare", [P, 1])
    first_use = sbuf("first_use", [P, 2])
    lnr = sbuf("lnr", [P, 3])
    xn = sbuf("xn", [P, D])
    xnT = sbuf("xnT", [P, P])
    gel = sbuf("gel", [P, FC, P])
    hT = sbuf("hT", [P, FC, P])

    QK, SC, TR, MX = bank[0:2], bank[2:4], bank[4:6], bank[6:8]

    setup_done, band_ready, kept_zero, final_done, stored = (
        sem(n) for n in ("setup_done", "band_ready", "kept_zero", "final_done", "stored"))
    x_T, mid_T, mid_back, xn_T, attn_out, gate_out, up_out, ffn_out = (
        sem(n) for n in ("x_T", "mid_T", "mid_back", "xn_T", "attn_out", "gate_out", "up_out", "ffn_out"))
    v_out, attn_T = sem("v_out"), sem("attn_T")
    qk_out, head_T, score_out, prob_T = (sem(n) for n in ("qk_out", "head_T", "score_out", "prob_T"))
    x_shifted, xs_step, xn_copied, gelu_done = (
        sem(n) for n in ("x_shifted", "xs_step", "xn_copied", "gelu_done"))
    v_copied, attn_copied = sem("v_copied"), sem("attn_copied")
    squared, head_copied, exp_done, prob_copied = (
        sem(n) for n in ("squared", "head_copied", "exp_done", "prob_copied"))
    squares_summed, normed, factors_placed, keys_kept, mid_done, ms_step, mid_shifted, xn_done, hidden_done, x_done = (
        sem(n) for n in ("squares_summed", "normed", "factors_placed", "keys_kept", "mid_done", "ms_step",
                         "mid_shifted", "xn_done", "hidden_done", "x_done"))
    inverted = sem("inverted")
    rotated, biased, max_step, sum_step = (
        sem(n) for n in ("rotated", "biased", "max_step", "sum_step"))
    nf_step, ln_step = sem("nf_step"), sem("ln_step")
    NF, LN = 4 + RS, 3 + RS
    x_loaded, normed_late, midb_done = sem("x_loaded"), sem("normed_late"), sem("midb_done")
    tables_done = sem("tables_done")
    joined, probs_done = sem("joined"), sem("probs_done")
    v_placed = sem("v_placed")

    def tiles_of(s, at_edge):
        return [t if not at_edge or 0 <= t < N else None for t in (s, s + 1, s + 2, s - 1, s - 2)]

    block = mem.block()

    @block.sync
    def _(sp):
        def place_values(n):
            sp.wait_ge(v_copied, 2 * n + 2)
            need(sp, attn_T, 2 * n)
            cur, prev = at(v_raw, n % 2), at(v_raw, (n + 1) % 2)
            sp.dma_start(v_win[WIN:KEYS, 0:1, :], cur[0:KEYS - WIN]).then_inc(v_placed, 16)
            sp.dma_start(v_win[0:KEYS, 1:2, :], cur[P - KEYS:P]).then_inc(v_placed, 16)
            sp.dma_start(v_win[0:WIN, 0:1, :], prev[P - WIN:P]).then_inc(v_placed, 16)

        sp.wait_ge(kept_zero, 1)
        place_values(0)
        place_values(1)
        with sp.Fori(2, TILES + 1) as n:
            place_values(n)
        with sp.Fori(1, LAYERS - 1) as layer:
            place_values(layer * TILES + 1)
            sp.wait_ge(v_out, 2 * TILES * layer)
            sp.dma_start(wqkv[:, bass.ds((layer + 1) % 2, 1), :],
                         w["L1_ffn_Wqkv"][bass.ds(layer + 1, 1)].rearrange("l p n -> p l n")).then_inc(wqkv_loaded, 16)
            sp.wait_ge(up_out, layer * TILES)
            sp.dma_start(w1[:], w["L1_ffn_W1"][bass.ds(layer, 1)].rearrange("l p n -> (l p) n")).then_inc(w1_loaded, 16)
            with sp.Fori(2, TILES + 1) as t:
                place_values(layer * TILES + t)
        last = (LAYERS - 1) * TILES
        place_values(last + 1)
        sp.wait_ge(up_out, last)
        sp.dma_start(w1[:], w["L1_ffn_W1"][LAYERS - 1]).then_inc(w1_loaded, 16)
        with sp.Fori(2, TILES) as t:
            place_values(last + t)
        sp.wait_ge(final_done, 1)
        sp.dma_start(out, x_in[:]).then_inc(stored, 16)
        sp.wait_ge(stored, 16)

    @block.tensor
    def _(pe):
        def transpose_x(n):
            pe.wait_ge(x_loaded, n + 1)
            need(pe, v_copied, 2 * n - 1)
            pe.transpose(QK[0][:, 0:P], x_cur[:], ident[:]).then_inc(x_T, 1)

        def project_qk(n, c):
            pe.wait_ge(x_shifted, n + 1)
            if c == 1:
                need(pe, v_copied, 2 * n)
            elif c > 1:
                pe.wait_ge(rotated, 4 * n + c - 1)
            layer = n // TILES
            if c == 0:
                pe.wait_ge(wqkv_loaded, 16 * (layer + 1))
            pe.matmul(QK[c % 2][:], xs[:, 0:P], wqkv[:, bass.ds(layer % 2, 1), 512 * c:512 * c + 512],
                      start=True, stop=True).then_inc(qk_out, 1)

        def project_v(n, c):
            pe.wait_ge(rotated, 4 * n + c + 3)
            layer = n // TILES
            pe.matmul(QK[c][:], xs[:, 0:P], wqkv[:, bass.ds(layer % 2, 1), 2 * INNER + 512 * c:2 * INNER + 512 * c + 512],
                      start=True, stop=True).then_inc(v_out, 1)

        def transpose_heads(i, k):
            if k % 2 == 0:
                pe.wait_ge(joined, 4 * i + ORDER[k] + 1)
            else:
                pe.wait_ge(normed if k == 1 else normed_late, i + 1)
            if k < 2:
                need(pe, prob_copied, 4 * i - 1 + k)
            else:
                pe.wait_ge(head_copied, 4 * i + k - 1)
            for p in range(4):
                col = 512 * ORDER[k] + 128 * p
                ins = pe.transpose(TR[k % 2][:, 128 * p:128 * p + 128], heads[:, col:col + 128], ident[:])
            ins.then_inc(head_T, 1)

        def scores(i, g):
            if g < 2:
                pe.wait_ge(head_copied, 4 * i + 2)
                need(pe, attn_copied, 2 * i - 1 + g)
            else:
                pe.wait_ge(head_copied, 4 * i + 4)
                pe.wait_ge(exp_done, 4 * i + g - 1)
            bank = SC[g % 2]
            pe.matmul(bank[:, 0:G], ident16[:], band16[:, bass.ds(i % TB, 1), :], start=True, stop=False,
                      skip_group_check=True)
            for pp in range(2):
                for half in range(2):
                    col = (2 * pp + half) * KEYS
                    for h in range(2):
                        rows = slice(HD * h, HD * h + HD)
                        ins = pe.matmul(bank[rows, col:col + KEYS], qT[rows, 2 * g + pp, 64 * half:64 * half + 64],
                                        kT[rows, 2 * g + pp, 64 * half:64 * half + KEYS],
                                        start=False, stop=True, skip_group_check=True)
            ins.then_inc(score_out, 1)

        def transpose_probs(i, g):
            pe.wait_ge(probs_done, 4 * i + g + 1)
            if g < 2:
                pe.wait_ge(head_copied, 4 * i + 3 + g)
            else:
                pe.wait_ge(prob_copied, 4 * i + g - 1)
            for u in range(4):
                ins = pe.transpose(TR[g % 2][0:KEYS, 128 * u:128 * u + 128],
                                   probs[:, g, KEYS * u:KEYS * u + KEYS], ident[:])
            ins.then_inc(prob_T, 1)

        def attend(i, o):
            pe.wait_ge(prob_copied, 4 * i + 2 * o + 2)
            pe.wait_ge(exp_done, 4 * i + 3 + o)
            if o == 0:
                pe.wait_ge(v_placed, 48 * (i + 1))
            for g in (2 * o, 2 * o + 1):
                for pp in range(2):
                    for half in range(2):
                        u = 2 * pp + half
                        col = (2 * (g % 2) + pp) * P + 64 * half
                        for h in range(2):
                            head = 2 * (2 * g + pp) + h
                            ins = pe.matmul(SC[o][HD * h:HD * h + HD, col:col + 64],
                                            v_win[:, half, HD * head:HD * head + HD],
                                            pT[:, g, 128 * u + 64 * h:128 * u + 64 * h + 64],
                                            start=True, stop=True, skip_group_check=True)
            ins.then_inc(attn_T, 1)

        def project_out(j):
            pe.wait_ge(attn_copied, 2 * j + 2)
            need(pe, gelu_done, j)
            layer = j // TILES
            for k in range(PAIRS):
                ins = pe.matmul(MX[1][:, 0:D], aT[:, k, :], wo[:, bass.ds(layer, 1), k, :],
                                start=(k == 0), stop=(k == PAIRS - 1))
            ins.then_inc(attn_out, 1)

        def transpose_mid(m):
            pe.wait_ge(mid_done, m + 1)
            need(pe, hidden_done, m)
            pe.transpose(MX[0][:, 0:P], mid[:], ident[:]).then_inc(mid_T, 1)

        def transpose_back(m):
            pe.wait_ge(mid_shifted, m + 1)
            pe.transpose(MX[0][:, 0:P], ms[:, 0:P], ident[:]).then_inc(mid_back, 1)

        def transpose_normed(m):
            pe.wait_ge(xn_done, m + 1)
            pe.transpose(MX[0][:, 0:P], xn[:], ident[:]).then_inc(xn_T, 1)

        def gate(m):
            pe.wait_ge(xn_copied, m + 1)
            pe.wait_ge(w1_loaded, 16 * (m // TILES + 1))
            pe.wait_ge(mid_done, m + 1)
            need(pe, x_done, m)
            for c in range(FC):
                ins = pe.matmul(MX[1][0:ROWS[c], 128 * c:128 * c + 128], w1[:, FF + 128 * c:FF + 128 * c + ROWS[c]],
                                xnT[:], start=True, stop=True)
            ins.then_inc(gate_out, 1)

        def up(m):
            for c in range(FC):
                ins = pe.matmul(MX[0][0:ROWS[c], 128 * c:128 * c + 128], w1[:, 128 * c:128 * c + ROWS[c]],
                                xnT[:], start=True, stop=True)
            ins.then_inc(up_out, 1)

        def down(m, j):
            pe.wait_ge(hidden_done, m + 1)
            if j is not None:
                pe.wait_ge(mid_done, j + 1)
            layer = m // TILES
            for c in range(FC):
                ins = pe.matmul(MX[1][:, 0:D], hT[0:ROWS[c], c, :], w2[0:ROWS[c], bass.ds(layer, 1), c, :],
                                start=(c == 0), stop=(c == FC - 1))
            ins.then_inc(ffn_out, 1)

        def step(s, at_edge=False):
            i, n, x2, j, m = tiles_of(s, at_edge)
            if j is not None:
                transpose_probs(j, 0)
                transpose_probs(j, 1)
            if n is not None:
                project_qk(n, 0)
                project_qk(n, 1)
            if j is not None:
                transpose_probs(j, 2)
                transpose_probs(j, 3)
                attend(j, 0)
            if i is not None:
                transpose_heads(i, 0)
                transpose_heads(i, 1)
            if j is not None:
                attend(j, 1)
            if i is not None:
                transpose_heads(i, 2)
                transpose_heads(i, 3)
            if m is not None:
                transpose_normed(m)
            if n is not None:
                project_qk(n, 2)
            if m is not None:
                gate(m)
                up(m)
            if n is not None:
                project_qk(n, 3)
            if i is not None:
                scores(i, 0)
                scores(i, 1)
            if j is not None:
                project_out(j)
            if i is not None:
                scores(i, 2)
                scores(i, 3)
            if n is not None:
                project_v(n, 0)
            if j is not None:
                transpose_mid(j)
            if n is not None:
                project_v(n, 1)
            if x2 is not None:
                transpose_x(x2)
            if m is not None:
                down(m, j)
            if j is not None:
                transpose_back(j)

        transpose_x(0)
        for c in range(4):
            project_qk(0, c)
        project_v(0, 0)
        project_v(0, 1)
        transpose_x(1)
        pe.wait_ge(wo_loaded, 16)
        pe.wait_ge(w2_loaded, 16 * FC)
        pe.wait_ge(band_ready, 1)
        for s in range(3):
            step(s, at_edge=True)
        with pe.Fori(3, N - 2) as s:
            step(s)
        for s in range(N - 2, N + 2):
            step(s, at_edge=True)

    @block.scalar
    def _(act):
        def copy_head(i, k):
            act.wait_ge(head_T, 4 * i + k + 1)
            if k == 0:
                need(act, score_out, 4 * i)
            if k == 1:
                act.wait_ge(keys_kept, i + 1)
            c = ORDER[k]
            src = TR[k % 2][:, :].rearrange("p (k t) -> p k t", k=4)
            k0 = 4 * (c % 2)
            dst = qT[:, k0:k0 + 4, :] if c < 2 else kT[:, k0:k0 + 4, WIN:WIN + P]
            act.copy(dst, src).then_inc(head_copied, 1)

        def shift_x(n):
            act.wait_ge(x_T, n + 1)
            need(act, v_out, 2 * n)
            need(act, x_shifted, n)
            act.activation(xs[half_rows, 0:1], xs[half_rows, P:P + 1], ACT.Copy,
                           scale=keep[half_rows, bass.ds(n % TB, 1)]).then_inc(xs_step, 1)
            act.copy(xs[0:P // 2, 0:P], QK[0][0:P // 2, 0:P])
            act.wait_ge(xs_step, n + 1)
            act.copy(xs[half_rows, 1:P + 1], QK[0][half_rows, 0:P]).then_inc(x_shifted, 1)

        def square(n, c):
            act.wait_ge(qk_out, 4 * n + c + 1)
            if c == 0:
                need(act, squares_summed, n)
            act.activation(squares[:, 512 * c:512 * c + 512], QK[c % 2][:], ACT.Square).then_inc(squared, 1)

        def exp(i, g):
            act.wait_ge(biased, 4 * i + g + 1)
            need(act, prob_T, 4 * i + g - 3)
            for u in range(4):
                pair, half = 2 * g + u // 2, u % 2
                ins = act.activation(probs[:, g, KEYS * u:KEYS * u + KEYS], SC[g % 2][:, KEYS * u:KEYS * u + KEYS],
                                     ACT.Exp, scale=q_factor[:, pair, half:half + 1],
                                     bias=exp_bias[:, 4 * g + u:4 * g + u + 1])
            ins.then_inc(exp_done, 1)

        def copy_values(n, c):
            act.wait_ge(v_out, 2 * n + c + 1)
            if c == 0:
                need(act, v_placed, 48 * n)
            par = n % 2
            dst = v_raw[:, bass.ds(par, 1), 512 * c:512 * c + 512]
            act.copy(dst, QK[c][:].unsqueeze(1)).then_inc(v_copied, 1)

        def copy_probs(i, g):
            act.wait_ge(prob_T, 4 * i + g + 1)
            if g == 0:
                need(act, attn_T, 2 * i)
            act.copy(pT[:, g, :], TR[g % 2][0:KEYS, :]).then_inc(prob_copied, 1)

        def copy_attn(i, o):
            act.wait_ge(attn_T, 2 * i + o + 1)
            if o == 0:
                need(act, attn_out, i)
            act.copy(aT[:, 4 * o:4 * o + 4, :], SC[o][:].rearrange("p (k t) -> p k t", k=4)).then_inc(attn_copied, 1)

        def copy_normed(m):
            act.wait_ge(xn_T, m + 1)
            need(act, up_out, m)
            layer = m // TILES
            act.activation(xnT[:], MX[0][:, 0:P], ACT.Identity, scale=at(ln_scale, layer),
                           bias=at(ln_shift, layer)).then_inc(xn_copied, 1)

        def load_table(func, k):
            act.activation(first_use[:, k:k + 1], keep[:, 0:1], func)

        def gelu(m):
            act.wait_ge(gate_out, m + 1)
            need(act, hidden_done, m)
            layer = m // TILES
            for c in range(FC):
                ins = act.activation(gel[0:ROWS[c], c, :], MX[1][0:ROWS[c], 128 * c:128 * c + 128], ACT.Gelu,
                                     bias=bias1[0:ROWS[c], bass.ds(layer, 1), 1, c:c + 1].rearrange("p l c -> p (l c)"))
            ins.then_inc(gelu_done, 1)

        def step(s, at_edge=False):
            i, n, x2, j, m = tiles_of(s, at_edge)
            if j is not None:
                copy_probs(j, 0)
                copy_probs(j, 1)
            if n is not None:
                square(n, 0)
                square(n, 1)
            if j is not None:
                copy_probs(j, 2)
                copy_probs(j, 3)
                copy_attn(j, 0)
            if i is not None:
                copy_head(i, 0)
                copy_head(i, 1)
            if j is not None:
                copy_attn(j, 1)
            if i is not None:
                copy_head(i, 2)
            if m is not None:
                copy_normed(m)
            if i is not None:
                copy_head(i, 3)
            if n is not None:
                square(n, 2)
            if m is not None:
                gelu(m)
            if n is not None:
                square(n, 3)
            if i is not None:
                load_table(ACT.Exp, 0)
                exp(i, 0)
                exp(i, 1)
            if i is not None:
                exp(i, 2)
            if n is not None:
                copy_values(n, 0)
            if i is not None:
                exp(i, 3)
            if n is not None:
                copy_values(n, 1)
            if x2 is not None:
                shift_x(x2)
            if j is not None:
                load_table(ACT.Gelu, 1)

        act.wait_ge(small_loaded, 16 * N_SMALL)
        act.wait_ge(kept_zero, 1)
        act.wait_ge(setup_done, 3)
        shift_x(0)
        for c in range(4):
            square(0, c)
        copy_values(0, 0)
        copy_values(0, 1)
        shift_x(1)
        for s in range(3):
            step(s, at_edge=True)
        with act.Fori(3, N - 2) as s:
            step(s)
        for s in range(N - 2, N + 2):
            step(s, at_edge=True)

    @block.vector
    def _(dve):
        def shift_mid(m):
            dve.wait_ge(mid_T, m + 1)
            need(dve, mid_back, m)
            need(dve, mid_shifted, m)
            dve.tensor_scalar(ms[half_rows, 0:1], ms[half_rows, P:P + 1],
                              keep[half_rows, bass.ds(m % TB, 1)], None, ALU.mult).then_inc(ms_step, 1)
            dve.tensor_copy(ms[0:P // 2, 0:P], MX[0][0:P // 2, 0:P])
            dve.wait_ge(ms_step, m + 1)
            dve.tensor_copy(ms[half_rows, 1:P + 1], MX[0][half_rows, 0:P]).then_inc(mid_shifted, 1)

        def by_head(ap):
            return ap.rearrange("p (h d) -> p h d", d=HD)

        def rotate_cos(n, c):
            dve.wait_ge(squared, 4 * n + c + 1)
            dve.wait_ge(tables_done, 2 * n + 2)
            need(dve, joined, 4 * n + c - 3)
            table = cos_l[:, c // 2, :].unsqueeze(1).broadcast_to([P, 8, HD])
            dve.tensor_tensor(by_head(kept[:, 512 * c:512 * c + 512]), by_head(QK[c % 2][:]), table, ALU.mult)

        def rotate_sin(n, c):
            need(dve, joined, 4 * n + c - 3)
            halves = lambda ap: ap.rearrange("p (h two d) -> p h two d", two=2, d=HD // 2)
            table = sin_l[:, c // 2, :].rearrange("p (two d) -> p two d", two=2).unsqueeze(1).broadcast_to(
                [P, 8, 2, HD // 2])
            dve.tensor_tensor(halves(turned[:, 512 * c:512 * c + 512]), halves(QK[c % 2][:])[:, :, ::-1, :], table,
                              ALU.mult).then_inc(rotated, 1)

        def sum_squares(n, c):
            dve.wait_ge(squared, 4 * n + c + 1)
            ins = dve.tensor_reduce(nf[:, 0, 8 * c:8 * c + 8], by_head(squares[:, 512 * c:512 * c + 512]), AX, ALU.add)
            ins.then_inc(nf_step, 1)
            if c == 3:
                dve.wait_ge(nf_step, NF * n + 4)
                dve.tensor_scalar(nf[:, 1, :], nf[:, 0, :], 1e-24, None, ALU.max).then_inc(squares_summed, 1)

        def norm_factor(n, k):
            if k == 0:
                dve.wait_ge(squares_summed, n + 1)
            rsqrt_op(dve, k, nf[:, 1, :], nf[:, 2, :], nf[:, 3, :], nf_step, NF * n + 4)

        def place_factors(i):
            dve.wait_ge(nf_step, NF * (i + 1))
            need(dve, exp_done, 4 * i)
            for h in range(2):
                for half in range(2):
                    src = nf[HD * half:HD * half + HD, 2, 0:HEADS].rearrange("p (a two) -> p a two", two=2)[:, :, h]
                    ins = dve.tensor_copy(q_factor[HD * h:HD * h + HD, :, half], src)
            ins.then_inc(factors_placed, 1)

        def normalise(n):
            dve.wait_ge(joined, 4 * n + 3)
            dve.wait_ge(nf_step, NF * (n + 1))
            r = nf[:, 2, 2 * 8:3 * 8].unsqueeze(2).broadcast_to([P, 8, HD])
            h = by_head(heads[:, 512 * 2:512 * 3])
            dve.tensor_tensor(h, h, r, ALU.mult).then_inc(normed, 1)

        def keep_keys(i):
            need(dve, head_copied, 4 * i)
            need(dve, score_out, 4 * i)
            dve.tensor_copy(kT[:, :, 0:WIN], kT[:, :, P:P + WIN]).then_inc(keys_kept, 1)

        def units(ap):
            return ap.rearrange("p (u k) -> p u k", k=KEYS)

        def row_max(i, g):
            dve.wait_ge(score_out, 4 * i + g + 1)
            dve.tensor_reduce(neg_max[:, 4 * g:4 * g + 4], units(SC[g % 2][:, 0:G]), AX, ALU.max, negate=True)\
                .then_inc(max_step, 1)

        def bias_rows(i, g):
            dve.wait_ge(max_step, 4 * i + g + 1)
            dve.wait_ge(factors_placed, i + 1)
            need(dve, exp_done, 4 * i + g - 3)
            dve.tensor_tensor(exp_bias[:, 4 * g:4 * g + 4], neg_max[:, 4 * g:4 * g + 4],
                              q_factor[:, 2 * g:2 * g + 2, :].rearrange("p a b -> p (a b)"), ALU.mult).then_inc(biased, 1)

        def row_sum(i, g):
            dve.wait_ge(exp_done, 4 * i + g + 1)
            dve.tensor_reduce(rowsum[:, 4 * g:4 * g + 4], units(probs[:, g, :]), AX, ALU.add).then_inc(sum_step, 1)

        def invert(i, g2):
            dve.wait_ge(sum_step, 4 * i + 2 * g2 + 2)
            need(dve, probs_done, 4 * i + 2 * g2 - 2)
            dve.reciprocal(rowinv[:, 8 * g2:8 * g2 + 8], rowsum[:, 8 * g2:8 * g2 + 8]).then_inc(inverted, 1)

        def ln(m, k):
            base = LN * m
            if k == 0:
                dve.wait_ge(mid_back, m + 1)
                dve.bn_stats(st[:], MX[0][:, 0:D]).then_inc(ln_step, 1)
            elif k == 1:
                dve.wait_ge(ln_step, base + 1)
                dve.memset(spare[:], 0.0)
                dve.bn_aggr(mv[:], st[:]).then_inc(ln_step, 1)
            elif k == 2:
                dve.wait_ge(ln_step, base + 2)
                dve.tensor_scalar(lnr[:, 0:1], mv[:, 1:2], 1e-5, None, ALU.add).then_inc(ln_step, 1)
            elif k < LN:
                rsqrt_op(dve, k - 3, lnr[:, 0:1], lnr[:, 1:2], lnr[:, 2:3], ln_step, base + 3)
            else:
                dve.wait_ge(ln_step, base + LN)
                need(dve, xn_T, m)
                dve.tensor_scalar(xn[:], MX[0][:, 0:D], mv[:, 0:1], lnr[:, 1:2], ALU.subtract, ALU.mult)\
                    .then_inc(xn_done, 1)

        def hidden(m):
            dve.wait_ge(up_out, m + 1)
            dve.wait_ge(gelu_done, m + 1)
            need(dve, ffn_out, m)
            layer = m // TILES
            for c in range(FC):
                ins = dve.scalar_tensor_tensor(
                    hT[0:ROWS[c], c, :], MX[0][0:ROWS[c], 128 * c:128 * c + 128],
                    bias1[0:ROWS[c], bass.ds(layer, 1), 0, c:c + 1].rearrange("p l c -> p (l c)"),
                    gel[0:ROWS[c], c, :], ALU.add, ALU.mult)
            ins.then_inc(hidden_done, 1)

        def new_x(m):
            dve.wait_ge(ffn_out, m + 1)
            dve.wait_ge(midb_done, m + 1)
            dve.tensor_tensor(x_all[:, bass.ds(m % TILES, 1), :], MX[1][:, 0:D].unsqueeze(1), midb[:].unsqueeze(1),
                              ALU.add).then_inc(x_done, 1)

        def new_mid(i):
            dve.wait_ge(attn_out, i + 1)
            need(dve, mid_T, i)
            need(dve, midb_done, i)
            dve.tensor_tensor(mid[:].unsqueeze(1), MX[1][:, 0:D].unsqueeze(1), x_all[:, bass.ds(i % TILES, 1), :],
                              ALU.add).then_inc(mid_done, 1)

        def step(s, at_edge=False):
            i, n, x2, j, m = tiles_of(s, at_edge)
            if i is not None:
                keep_keys(i)
            if m is not None:
                ln(m, 6)
            if i is not None:
                normalise(i)
            if m is not None:
                ln(m, 7)
            if i is not None:
                place_factors(i)
            if m is not None:
                ln(m, 8)
            if n is not None:
                rotate_cos(n, 0)
            if m is not None:
                ln(m, 9)
            if n is not None:
                rotate_sin(n, 0)
            if m is not None:
                ln(m, 10)
            if n is not None:
                rotate_cos(n, 1)
            if m is not None:
                ln(m, 11)
            if n is not None:
                rotate_sin(n, 1)
            if m is not None:
                ln(m, 12)
                ln(m, 13)
            if n is not None:
                sum_squares(n, 0)
                sum_squares(n, 1)
                rotate_cos(n, 2)
                rotate_sin(n, 2)
            if m is not None:
                hidden(m)
            if n is not None:
                sum_squares(n, 2)
            if i is not None:
                row_max(i, 0)
                bias_rows(i, 0)
                row_max(i, 1)
                bias_rows(i, 1)
            if n is not None:
                sum_squares(n, 3)
                rotate_cos(n, 3)
                norm_factor(n, 0)
                rotate_sin(n, 3)
                norm_factor(n, 1)
            if i is not None:
                row_max(i, 2)
            if n is not None:
                norm_factor(n, 2)
            if j is not None:
                new_mid(j)
            if n is not None:
                norm_factor(n, 3)
            if i is not None:
                bias_rows(i, 2)
                row_sum(i, 0)
            if n is not None:
                norm_factor(n, 4)
            if i is not None:
                row_max(i, 3)
            if n is not None:
                norm_factor(n, 5)
            if i is not None:
                row_sum(i, 1)
            if n is not None:
                norm_factor(n, 6)
            if i is not None:
                bias_rows(i, 3)
            if n is not None:
                norm_factor(n, 7)
            if i is not None:
                invert(i, 0)
            if n is not None:
                norm_factor(n, 8)
            if j is not None:
                shift_mid(j)
            if n is not None:
                norm_factor(n, 9)
            if i is not None:
                row_sum(i, 2)
            if j is not None:
                ln(j, 0)
                ln(j, 1)
                ln(j, 2)
            if i is not None:
                row_sum(i, 3)
            if j is not None:
                ln(j, 3)
            if i is not None:
                invert(i, 1)
            if j is not None:
                ln(j, 4)
            if m is not None:
                new_x(m)
            if j is not None:
                ln(j, 5)

        dve.wait_ge(setup_done, 3)
        dve.wait_ge(small_loaded, 16 * N_SMALL)
        dve.tensor_copy(band16[:], band[:]).then_inc(band_ready, 1)
        for c in range(4):
            rotate_cos(0, c)
            rotate_sin(0, c)
        for c in range(4):
            sum_squares(0, c)
        for k in range(RS):
            norm_factor(0, k)
        for s in range(3):
            step(s, at_edge=True)
        with dve.Fori(3, N - 2) as s:
            step(s)
        for s in range(N - 2, N + 2):
            step(s, at_edge=True)
        dve.wait_ge(x_done, N)
        dve.scalar_tensor_tensor(x_in[:], x_all[:], gate, x_in[:], ALU.mult, ALU.add).then_inc(final_done, 1)

    @block.gpsimd
    def _(pool):
        def load_x(n):
            need(pool, x_T, n)
            need(pool, x_done, n - 4)
            pool.tensor_copy(x_cur[:].unsqueeze(1), x_all[:, bass.ds(n % TILES, 1), :]).then_inc(x_loaded, 1)

        def tables(n):
            need(pool, rotated, 4 * n)
            layer = n // TILES
            sc = qk_scale[:, bass.ds(layer, 1), :, :]
            pool.tensor_tensor(cos_l[:].unsqueeze(1), cos_t[:, bass.ds(n % TB, 1), :, :], sc, ALU.mult)\
                .then_inc(tables_done, 1)
            pool.tensor_tensor(sin_l[:].unsqueeze(1), sin_t[:, bass.ds(n % TB, 1), :, :],
                               qk_swapped[:, bass.ds(layer, 1), :, :], ALU.mult).then_inc(tables_done, 1)

        def join(n, c):
            pool.wait_ge(rotated, 4 * n + c + 1)
            need(pool, head_T, 4 * n - 3 + ORDER.index(c))
            cols = slice(512 * c, 512 * c + 512)
            pool.tensor_tensor(heads[:, cols], kept[:, cols], turned[:, cols], ALU.add).then_inc(joined, 1)

        def normalise(n):
            pool.wait_ge(nf_step, NF * (n + 1))
            pool.wait_ge(joined, 4 * n + 4)
            r = nf[:, 2, 3 * 8:4 * 8].unsqueeze(2).broadcast_to([P, 8, HD])
            h = heads[:, 512 * 3:512 * 4].rearrange("p (h d) -> p h d", d=HD)
            pool.tensor_tensor(h, h, r, ALU.mult).then_inc(normed_late, 1)

        def normalise_probs(i, g):
            pool.wait_ge(inverted, 2 * i + g // 2 + 1)
            r = rowinv[:, 4 * g:4 * g + 4].unsqueeze(2).broadcast_to([P, 4, KEYS])
            p = probs[:, g, :].rearrange("p (u k) -> p u k", k=KEYS)
            pool.tensor_tensor(p, p, r, ALU.mult).then_inc(probs_done, 1)

        def add_bias(i):
            pool.wait_ge(mid_done, i + 1)
            need(pool, x_done, i)
            pool.tensor_tensor(midb[:].unsqueeze(1), mid[:].unsqueeze(1), bias2[:, bass.ds(i // TILES, 1), :],
                               ALU.add).then_inc(midb_done, 1)

        def step(s, at_edge=False):
            i, n, x2, j, m = tiles_of(s, at_edge)
            if m is not None:
                add_bias(m)
            if i is not None:
                normalise(i)
            if x2 is not None:
                load_x(x2)
            if n is not None:
                for c in range(4):
                    join(n, c)
            if x2 is not None:
                tables(x2)
            if i is not None:
                for g in range(GROUPS):
                    normalise_probs(i, g)

        load_x(0)
        pool.memzero(xs[:]).then_inc(setup_done, 1)
        pool.memzero(ms[:]).then_inc(setup_done, 1)
        pool.memzero(kT[:]).then_inc(setup_done, 1)
        pool.memzero(v_raw[:, 1, :]).then_inc(kept_zero, 1)
        pool.wait_ge(small_loaded, 16 * N_SMALL)
        tables(0)
        for c in range(4):
            join(0, c)
        tables(1)
        load_x(1)
        for s in range(3):
            step(s, at_edge=True)
        with pool.Fori(3, N - 2) as s:
            step(s)
        for s in range(N - 2, N + 2):
            step(s, at_edge=True)

    mem.end_block()


def program(nc, w, out):
    with ExitStack() as ctx:
        mem = Memory(nc, ctx)
        bank = [mem.psum(f"bank{k}") for k in range(8)]
        x_all = mem.sbuf("x_all", [P, TILES, D])
        xn = mem.sbuf("xn_all", [P, TILES, D])
        xnT = mem.sbuf("xnT_all", [P, TILES, P])
        ident = mem.sbuf("ident", [P, P])
        ident16 = mem.sbuf("ident16", [P, P], BF16)
        gates = mem.sbuf("gates", [P, 4])
        gates_t = mem.sbuf("gates_t", [P, 4])
        ctx_rows = mem.sbuf("ctx_rows", [CTX, B, D])
        mem.ctxT = mem.sbuf("ctxT", [P, B, CTX])
        mem.w2s = {n: mem.sbuf("w2_" + n, s) for n, s in (
            ("ew1", [P, 8, P]), ("ew2", [P, 8, D]), ("sw1", [P, 2 * P]), ("sw3", [P, 2 * P]), ("sw2", [P, 2, D]),
            ("router", [P, 8]), ("bias", [P, 8]), ("before", [P, 64]))}
        mem.w3s = {n: mem.sbuf("w3_" + n, s) for n, s in (
            ("wq", [P, D]), ("wkv", [P, 2 * D]), ("wproj", [P, D]), ("own", [P, 16]))}
        lw = local_weights(mem)
        loaded, x_loaded0, turned, ready = mem.sem("loaded"), mem.sem("x_loaded0"), mem.sem("turned"), mem.sem("ready")
        mem.loads2, mem.loads3 = mem.sem("s2_loads"), mem.sem("s3_loads")

        def prefetch(sp):
            for name, src in (("ew1", w["L0_ffn_ew1"].rearrange("e p n -> p e n")),
                              ("ew2", w["L0_ffn_ew2"].rearrange("e p n -> p e n")),
                              ("sw1", w["L0_ffn_sw1"]), ("sw3", w["L0_ffn_sw3"]),
                              ("sw2", w["L0_ffn_sw2"].rearrange("(c p) n -> p c n", p=P)),
                              ("router", w["router_T"]), ("bias", w["L0_ffn_router_bias"].partition_broadcast(P)),
                              ("before", w["before"])):
                sp.dma_start(mem.w2s[name][:], src).then_inc(mem.loads2, 16)
            for name, src in (("wq", w["L1_xattn_W_q"]), ("wkv", w["L1_xattn_W_kv"]), ("wproj", w["L1_xattn_W_proj"]),
                              ("own", w["own"])):
                sp.dma_start(mem.w3s[name][:], src).then_inc(mem.loads3, 16)
            load_local_weights(sp, w, lw)

        mem.prefetch = prefetch
        with mem.stage():
            ww = wide_weights(mem)
            block = mem.block()

            @block.sync
            def _(sp):
                sp.dma_start(ident[:], w["ident"]).then_inc(loaded, 16)
                sp.dma_start(ctx_rows[:], w["ctx_1024"].rearrange("b t d -> t b d")).then_inc(loaded, 16)
                sp.dma_start(gates[:, 0:2], w["g_xattn"].partition_broadcast(P)).then_inc(loaded, 16)
                sp.dma_start(gates[:, 2:4], w["g_ffn"].partition_broadcast(P)).then_inc(loaded, 16)
                sp.dma_start(x_all[:], w["x"].rearrange("b (t p) d -> p (b t) d", p=P)).then_inc(x_loaded0, 16)
                load_wide_weights(sp, w, ww)
                sp.wait_ge(x_loaded0, 16)

            @block.tensor
            def _(pe):
                pe.wait_ge(loaded, 64)
                for b in range(B):
                    ins = pe.transpose(bank[0][:, CTX * b:CTX * b + CTX], ctx_rows[:, b, :], ident[0:CTX, 0:CTX])
                ins.then_inc(turned, 1)

            @block.vector
            def _(dve):
                dve.wait_ge(loaded, 64)
                dve.tensor_copy(ident16[:], ident[:]).then_inc(ready, 1)

            @block.scalar
            def _(act):
                act.wait_ge(loaded, 64)
                act.activation(gates_t[:], gates[:], ACT.Tanh).then_inc(ready, 1)
                act.wait_ge(turned, 1)
                act.copy(mem.ctxT[:].rearrange("p b t -> p (b t)"), bank[0][:, 0:B * CTX]).then_inc(ready, 1)

            mem.end_block()
            with mem.stage():
                layer_norm(mem, "ln1", x_all, xn, bank, ident, xnT)
            cross_attention_wide(mem, w, ww, x_all, xnT, bank, ident, gates_t[:, 0:1])
        with mem.stage():
            nar = narrow_products(mem)
            with mem.stage():
                layer_norm(mem, "ln2", x_all, xn, bank, ident, xnT, form_to_scores(mem, nar, bank, ident))
            with mem.stage():
                mixture(mem, w, x_all, xnT, bank, ident, gates_t[:, 2:3])
            with mem.stage():
                layer_norm(mem, "ln3", x_all, xn, bank, ident, xnT, form_to_out(mem, nar, bank))
            cross_attention_narrow(mem, nar, x_all, xnT, bank, ident, gates_t[:, 1:2])
        with mem.stage():
            layer_norm(mem, "ln4", x_all, xn, bank, ident, None)
        with mem.stage():
            local_stage(mem, w, lw, xn, x_all, ident, ident16, bank, gates_t[:, 3:4], out)


_DIRECT = ["x", "ctx_1024", "g_xattn", "g_ffn", "L0_xattn_W_Q", "L0_xattn_W_K", "L0_xattn_W_V", "L0_xattn_W_fc",
           "L0_ffn_router_bias", "L0_ffn_sw1", "L0_ffn_sw3", "L0_ffn_sw2", "L0_ffn_ew1", "L0_ffn_ew2", "L1_xattn_W_q",
           "L1_xattn_W_kv", "L1_xattn_W_proj", "L1_ffn_Wqkv", "L1_ffn_q_scale", "L1_ffn_k_scale", "L1_ffn_Wo",
           "L1_ffn_W1", "L1_ffn_W2", "L1_ffn_b2"]


def _constants():
    half = np.arange(0, HD, 2, dtype=np.float64)
    position = np.arange(S, dtype=np.float64)
    angle = np.tile(position[:, None] * 10000.0 ** (-half / HD)[None, :], (1, 2))
    base = (half + 0.4 * HD) / (1.4 * HD)
    scale = np.tile(base[None, :] ** ((position - S // 2) / (WIN // 2))[:, None], (1, 2))
    sign = np.repeat([-1.0, 1.0], HD // 2)
    cos, sin = np.cos(angle), np.sin(angle) * sign
    by_tile = lambda q, k: np.stack([q, k], 1).reshape(TB, P, 2, HD).transpose(1, 0, 2, 3).astype(np.float32)
    query, key = np.arange(P)[:, None] % (P // 2), np.arange(KEYS)[None, :]
    seen = (key >= query) & (key <= query + WIN)
    band = np.zeros((P, TB, 4, KEYS), np.float32)
    for t in range(TB):
        for unit in range(4):
            first = (t == 0) and (unit % 2 == 0)
            band[:, t, unit][~(seen & (key >= WIN)) if first else ~seen] = -1e30
    keep = np.ones((P, TB), np.float32)
    keep[:, 0] = 0.0
    before = np.tile(np.tril(np.ones((8, 8), np.float32), -1).reshape(1, 64), (P, 1))
    own = (np.arange(P)[:, None] // 8 == np.arange(16)[None, :]).astype(np.float32)
    q_factor = 8.0
    return {"ident": np.eye(P, dtype=np.float32), "cos": by_tile(q_factor * cos * scale, cos / scale),
            "sin": by_tile(q_factor * sin * scale, sin / scale), "band": band.reshape(P, TB, G), "keep": keep,
            "before": before, "own": own}


def kernel(**inputs):
    import concourse.bacc as _bacc
    from concourse.bass_utils import run_bass_kernel_spmd as _run

    arrays = {n: np.asarray(inputs[n]) for n in _DIRECT}
    arrays["mask"] = np.asarray(inputs["mask_Bx8xSxS2_bf0"])
    arrays["router_T"] = np.asarray(inputs["L0_ffn_router_w"]).T
    for name in "qk":
        arrays[f"{name}_swapped"] = np.roll(np.asarray(inputs[f"L1_ffn_{name}_scale"]), HD // 2, axis=1)
    arrays["ln_g"] = np.asarray(inputs["L1_ffn_ln_g"]).T
    arrays["ln_b"] = np.asarray(inputs["L1_ffn_ln_b"]).T
    b1 = np.zeros((LAYERS, 2, FC * P), np.float32)
    b1[:, :, 0:FF] = np.asarray(inputs["L1_ffn_b1"]).reshape(LAYERS, 2, FF)
    arrays["b1"] = b1.reshape(LAYERS, 2, FC, P).transpose(3, 0, 1, 2)
    arrays.update(_constants())
    arrays = {n: np.ascontiguousarray(a) for n, a in arrays.items()}

    nc = _bacc.Bacc("TRN2", target_bir_lowering=False, num_devices=1)
    w = {n: nc.dram_tensor(f"in_{n}", a.shape, mybir.dt.from_np(a.dtype), kind="ExternalInput").ap()
         for n, a in arrays.items()}
    out = nc.dram_tensor("out_x", (B, S, D), F32, kind="ExternalOutput").ap()
    program(nc, w, out.rearrange("b (t p) d -> p (b t) d", p=P))
    r = _run(nc, [{f"in_{n}": a for n, a in arrays.items()}], core_ids=[0])
    return r.results[0]["out_x"]
```
